# Optimizing a Trainium2 kernel written in Bass

```python
import numpy as np
import jax
import jax.numpy as jnp

def _softmax(x, axis=-1):
    return jax.nn.softmax(x, axis=axis)

def _gelu(x):
    return jax.nn.gelu(x, approximate=True)

def _silu(x):
    return jax.nn.silu(x)

def _sigmoid(x):
    return jax.nn.sigmoid(x)

def _layernorm(x, axis=-1, eps=1e-05):
    m = jnp.mean(x, axis=axis, keepdims=True)
    v = jnp.var(x, axis=axis, keepdims=True)
    return (x - m) / jnp.sqrt(v + eps)

def _scatter_add(tgt, idx, src, axis=0):
    return tgt.at[idx].add(src)

def _segment_sum(src, seg, n):
    return jax.ops.segment_sum(src, seg, n)
kernel_name = 'mk_perceiver_d1_seqx_r2_d4f21a'

def setup_inputs(seed: int=0):
    np.random.seed(seed)
    _w = jnp.asarray

    def _rec_inputs():
        import jax
        import jax.numpy as jnp
        _rk = jax.random.key(seed)
        x = 7.22e-05 + 1 * jax.random.normal(jax.random.fold_in(_rk, 1), (1, 512, 512), jnp.float32)
        _lenS = 512 - jax.random.randint(jax.random.fold_in(_rk, 7), (1,), 0, max(1, 512 // 4) + 1, jnp.int32)
        _lenS2 = 8192 - jax.random.randint(jax.random.fold_in(_rk, 8), (1,), 0, max(1, 8192 // 4) + 1, jnp.int32)
        _ctx_768P = jax.random.normal(jax.random.fold_in(_rk, 11), (1, 16, 384), jnp.float32)
        _ctx_768c = jax.random.dirichlet(jax.random.fold_in(_rk, 511), 0.3 * jnp.ones((16,), jnp.float32), (1, 8192))
        _ctx_768t = jnp.einsum('bsk,bkd->bsd', _ctx_768c, _ctx_768P)
        _ctx_768t = _ctx_768t * jax.lax.rsqrt(jnp.mean(jnp.square(_ctx_768t)) + 1e-12) * 0.953939
        ctx_768 = -0.000191848 + 0.999787 * (_ctx_768t + 0.3 * jax.random.normal(jax.random.fold_in(_rk, 611), (1, 8192, 384), jnp.float32))
        return (x, ctx_768)
    x, ctx_768 = _rec_inputs()

    def _L0_xattn_setup():
        import jax, jax.numpy as jnp
        import numpy as np
        NUM_HEADS = 16
        CLAMP = 10000.0
        key = jax.random.key(seed)
        ks = jax.random.split(key, 8)
        B, Nq, Nkv, Cq, Ckv = (4, 1024, 1024, 512, 384)
        s_q = 1.0 / np.sqrt(Cq)
        s_kv = 1.0 / np.sqrt(Ckv)
        return {'query': jax.random.normal(ks[0], (B, Nq, Cq), jnp.float32), 'key_value': jax.random.normal(ks[1], (B, Nkv, Ckv), jnp.float32), 'Wq': jax.random.normal(ks[2], (Cq, Cq), jnp.float32) * s_q, 'bq': jnp.zeros((Cq,), jnp.float32), 'Wk': jax.random.normal(ks[3], (Ckv, Cq), jnp.float32) * s_kv, 'bk': jnp.zeros((Cq,), jnp.float32), 'Wv': jax.random.normal(ks[4], (Ckv, Cq), jnp.float32) * s_kv, 'bv': jnp.zeros((Cq,), jnp.float32), 'Wo': jax.random.normal(ks[5], (Cq, Cq), jnp.float32) * s_q, 'bo': jnp.zeros((Cq,), jnp.float32)}
    _L0_xattn_all = _L0_xattn_setup()
    _L0_xattn_in = {k: v for k, v in _L0_xattn_all.items() if k in ('Wq', 'bq', 'Wk', 'bk', 'Wv', 'bv', 'Wo', 'bo')}
    del _L0_xattn_all

    def _L0_attn_setup():
        import jax, jax.numpy as jnp
        import numpy as np
        D_MODEL = 512
        N_HEADS = 16
        HEAD_DIM = D_MODEL // N_HEADS

        def alibi_slopes(n_heads):
            base = 2.0 ** (-8.0 / n_heads)
            return jnp.asarray([base ** i for i in range(1, n_heads + 1)], dtype=jnp.float32)
        key = jax.random.key(seed)
        kx, kq, kk, kv, ko = jax.random.split(key, 5)
        B, T = (2, 1024)
        scale = 0.02
        x = jax.random.normal(kx, (B, T, D_MODEL), dtype=jnp.float32)
        Wq = jax.random.normal(kq, (D_MODEL, D_MODEL), dtype=jnp.float32) * scale
        Wk = jax.random.normal(kk, (D_MODEL, D_MODEL), dtype=jnp.float32) * scale
        Wv = jax.random.normal(kv, (D_MODEL, D_MODEL), dtype=jnp.float32) * scale
        Wo = jax.random.normal(ko, (D_MODEL, D_MODEL), dtype=jnp.float32) * scale
        return {'x': x, 'Wq': Wq, 'Wk': Wk, 'Wv': Wv, 'Wo': Wo}
    _L0_attn_all = _L0_attn_setup()
    _L0_attn_in = {k: v for k, v in _L0_attn_all.items() if k in ('Wq', 'Wk', 'Wv', 'Wo')}
    del _L0_attn_all

    def _L0_ffn_setup():
        import jax, jax.numpy as jnp
        import numpy as np
        B, S, D, E, K = (4, 1024, 512, 8, 2)
        H = 4 * D
        key = jax.random.key(seed)
        ks = jax.random.split(key, 4)
        sc = lambda n: 1.0 / np.sqrt(n)
        return {'x': jax.random.normal(ks[0], (B, S, D), jnp.float32), 'gate_w': jax.random.normal(ks[1], (D, E), jnp.float32) * sc(D), 'gate_b': jnp.zeros((E,), jnp.float32), 'w1': jax.random.normal(ks[2], (E, D, H), jnp.float32) * sc(D), 'b1': jnp.zeros((E, H), jnp.float32), 'w2': jax.random.normal(ks[3], (E, H, D), jnp.float32) * sc(H), 'b2': jnp.zeros((E, D), jnp.float32)}
    _L0_ffn_all = _L0_ffn_setup()
    _L0_ffn_in = {k: v for k, v in _L0_ffn_all.items() if k in ('gate_w', 'gate_b', 'w1', 'b1', 'w2', 'b2')}
    del _L0_ffn_all
    return {'x': x, 'ctx_768': ctx_768, 'L0_xattn_Wq': _L0_xattn_in['Wq'], 'L0_xattn_bq': _L0_xattn_in['bq'], 'L0_xattn_Wk': _L0_xattn_in['Wk'], 'L0_xattn_bk': _L0_xattn_in['bk'], 'L0_xattn_Wv': _L0_xattn_in['Wv'], 'L0_xattn_bv': _L0_xattn_in['bv'], 'L0_xattn_Wo': _L0_xattn_in['Wo'], 'L0_xattn_bo': _L0_xattn_in['bo'], 'L0_attn_Wq': _L0_attn_in['Wq'], 'L0_attn_Wk': _L0_attn_in['Wk'], 'L0_attn_Wv': _L0_attn_in['Wv'], 'L0_attn_Wo': _L0_attn_in['Wo'], 'L0_ffn_gate_w': _L0_ffn_in['gate_w'], 'L0_ffn_gate_b': _L0_ffn_in['gate_b'], 'L0_ffn_w1': _L0_ffn_in['w1'], 'L0_ffn_b1': _L0_ffn_in['b1'], 'L0_ffn_w2': _L0_ffn_in['w2'], 'L0_ffn_b2': _L0_ffn_in['b2']}

def reference(x, ctx_768, L0_xattn_Wq, L0_xattn_bq, L0_xattn_Wk, L0_xattn_bk, L0_xattn_Wv, L0_xattn_bv, L0_xattn_Wo, L0_xattn_bo, L0_attn_Wq, L0_attn_Wk, L0_attn_Wv, L0_attn_Wo, L0_ffn_gate_w, L0_ffn_gate_b, L0_ffn_w1, L0_ffn_b1, L0_ffn_w2, L0_ffn_b2):
    import jax
    import jax.numpy as jnp

    def _L0_xattn_ref(query, key_value, Wq, bq, Wk, bk, Wv, bv, Wo, bo):
        import jax, jax.numpy as jnp
        import numpy as np
        NUM_HEADS = 16
        CLAMP = 10000.0
        B, Nq, Cq = query.shape
        Nkv = key_value.shape[1]
        H = NUM_HEADS
        D = Cq // H
        scale = D ** (-0.5)
        q = (query @ Wq + bq).reshape(B, Nq, H, D).transpose(0, 2, 1, 3)
        k = (key_value @ Wk + bk).reshape(B, Nkv, H, D).transpose(0, 2, 1, 3)
        v = (key_value @ Wv + bv).reshape(B, Nkv, H, D).transpose(0, 2, 1, 3)
        attn = jnp.einsum('bhqd,bhkd->bhqk', q, k) * scale
        attn = jnp.clip(attn, -CLAMP, CLAMP)
        attn = jax.nn.softmax(attn, axis=-1)
        attn = jnp.where(jnp.any(jnp.isnan(attn)), jnp.asarray(1.0 / Nkv, attn.dtype), attn)
        x = jnp.einsum('bhqk,bhkd->bqhd', attn, v).reshape(B, Nq, Cq)
        return x @ Wo + bo

    def _L0_attn_ref(x, Wq, Wk, Wv, Wo):
        import jax, jax.numpy as jnp
        import numpy as np
        D_MODEL = 512
        N_HEADS = 16
        HEAD_DIM = D_MODEL // N_HEADS

        def alibi_slopes(n_heads):
            base = 2.0 ** (-8.0 / n_heads)
            return jnp.asarray([base ** i for i in range(1, n_heads + 1)], dtype=jnp.float32)
        B, T, D = x.shape
        H, hd = (N_HEADS, HEAD_DIM)

        def proj(W):
            return (x @ W.T).reshape(B, T, H, hd).transpose(0, 2, 1, 3)
        q, k, v = (proj(Wq), proj(Wk), proj(Wv))
        scale = hd ** (-0.5)
        scores = jnp.einsum('bhqd,bhkd->bhqk', q, k) * scale
        pos = jnp.arange(T, dtype=jnp.float32)
        dist = jnp.abs(pos[:, None] - pos[None, :])
        causal = pos[:, None] >= pos[None, :]
        slopes = alibi_slopes(H)
        bias = -slopes[:, None, None] * jnp.where(causal, dist, 0.0)
        scores = scores + bias[None]
        scores = jnp.where(causal[None, None], scores, -jnp.inf)
        attn = jax.nn.softmax(scores, axis=-1)
        out = jnp.einsum('bhqk,bhkd->bhqd', attn, v)
        out = out.transpose(0, 2, 1, 3).reshape(B, T, D)
        return out @ Wo.T

    def _L0_ffn_ref(x, gate_w, gate_b, w1, b1, w2, b2):
        import jax, jax.numpy as jnp
        import numpy as np
        B, S, D, E, K = (4, 1024, 512, 8, 2)
        H = 4 * D
        Bx, Sx, Dx = x.shape
        n_exp = w1.shape[0]
        logits = jnp.einsum('bsd,de->bse', x, gate_w) + gate_b
        scores = jax.nn.softmax(logits, axis=-1)
        topk_s, topk_i = jax.lax.top_k(scores, K)
        onehot = jax.nn.one_hot(topk_i, n_exp, dtype=scores.dtype)
        dispatch = jnp.einsum('bske,bsk->bse', onehot, topk_s)
        xf = x.reshape(-1, Dx)
        wf = dispatch.reshape(-1, n_exp)
        out = jnp.zeros_like(xf)
        for i in range(n_exp):
            wi = wf[:, i:i + 1]
            h = jax.nn.relu(xf * wi @ w1[i] + b1[i])
            y = h @ w2[i] + b2[i]
            out = jnp.where(wi > 0, y, out)
        return out.reshape(Bx, Sx, Dx)
    x = x + _L0_xattn_ref(_layernorm(x, axis=-1), ctx_768, L0_xattn_Wq, L0_xattn_bq, L0_xattn_Wk, L0_xattn_bk, L0_xattn_Wv, L0_xattn_bv, L0_xattn_Wo, L0_xattn_bo)
    x = x + _L0_attn_ref(_layernorm(x, axis=-1), L0_attn_Wq, L0_attn_Wk, L0_attn_Wv, L0_attn_Wo)
    x = x + _L0_ffn_ref(_layernorm(x, axis=-1), L0_ffn_gate_w, L0_ffn_gate_b, L0_ffn_w1, L0_ffn_b1, L0_ffn_w2, L0_ffn_b2)
    return x

_drawn_inputs = setup_inputs


def setup_inputs(seed=0):
    import zlib

    import numpy as np

    out = dict(_drawn_inputs(seed))
    spreads = {'L0_xattn_bq': (0.0, 0.1),
     'L0_xattn_bk': (0.0, 0.8),
     'L0_xattn_bv': (0.0, 0.1),
     'L0_xattn_bo': (0.0, 0.1),
     'L0_ffn_gate_b': (0.0, 0.1),
     'L0_ffn_b1': (0.0, 0.1),
     'L0_ffn_b2': (0.0, 0.1)}
    factors = {'L0_attn_Wq': 5.699, 'L0_attn_Wk': 4.174}
    for name, (base, spread) in spreads.items():
        noise = np.random.default_rng([zlib.crc32(name.encode()), seed]).standard_normal(out[name].shape)
        drawn = base * np.exp(spread * noise) if base else spread * noise
        out[name] = jnp.asarray(drawn.astype(out[name].dtype))
    for name, factor in factors.items():
        out[name] = (out[name] * factor).astype(out[name].dtype)
    return out
```

```python
import numpy as np
import concourse.bass as bass
from concourse import mybir
from contextlib import ExitStack

F32 = mybir.dt.float32
F32R = mybir.dt.float32r
I32 = mybir.dt.int32
ALU = mybir.AluOpType
ACT = mybir.ActivationFunctionType
AX = mybir.AxisListType

P = 128
T, C, CK = 512, 512, 384
N = 8192
H, D = 16, 32
NT = T // P
NC = C // P
NK = CK // P
G, HG = NC, P // D
EPS = 1e-5

KB = 512
NB = N // KB
CB = KB // P
U = G * CB


def bank(ps, i, n=512):
    return ps[:, i * 512:i * 512 + n]


class Stage:
    pass


def layer_norm(s, tag, src, dst):
    nc, ctx = s.nc, ExitStack()
    with ctx:
        stats = ctx.enter_context(nc.sbuf_tensor(f"{tag}_stats", [P, NT, 6], F32))
        mv = ctx.enter_context(nc.sbuf_tensor(f"{tag}_mv", [P, NT, 2], F32))
        std = ctx.enter_context(nc.sbuf_tensor(f"{tag}_std", [P, NT], F32))
        rstd = ctx.enter_context(nc.sbuf_tensor(f"{tag}_rstd", [P, NT], F32))
        stats_done = ctx.enter_context(nc.semaphore(f"{tag}_stats_done"))
        mv_done = ctx.enter_context(nc.semaphore(f"{tag}_mv_done"))
        std_done = ctx.enter_context(nc.semaphore(f"{tag}_std_done"))
        rstd_done = ctx.enter_context(nc.semaphore(f"{tag}_rstd_done"))
        with nc.Block() as block:

            @block.vector
            def _(dve):
                for t in range(NT):
                    dve.bn_stats(stats[:, t, :], src[:, t, :]).then_inc(stats_done, 1)
                for t in range(NT):
                    dve.wait_ge(stats_done, t + 1)
                    dve.bn_aggr(mv[:, t, :], stats[:, t, :]).then_inc(mv_done, 1)
                dve.wait_ge(std_done, 1)
                dve.reciprocal(rstd[:, :], std[:, :]).then_inc(rstd_done, 1)
                dve.wait_ge(rstd_done, 1)
                for t in range(NT):
                    dve.tensor_scalar(dst[:, t, :], src[:, t, :], mv[:, t, 0:1], rstd[:, t:t + 1],
                                      ALU.subtract, ALU.mult)

            @block.scalar
            def _(act):
                act.wait_ge(mv_done, NT)
                act.activation(std[:, :], mv[:, :, 1], ACT.Sqrt, bias=s.eps[:, 0:1]).then_inc(std_done, 1)


def transpose_tokens(s, tag, src, dst):
    nc, ps = s.nc, s.ps
    with ExitStack() as ctx:
        turned = ctx.enter_context(nc.semaphore(f"{tag}_turned"))
        with nc.Block() as block:

            @block.tensor
            def _(pe):
                for k in range(NC):
                    for t in range(NT):
                        last = pe.transpose(ps[:, k * 512 + t * P:k * 512 + t * P + P],
                                            src[:, t, k * P:k * P + P], s.ident[:, :])
                    last.then_inc(turned, 1)

            @block.vector
            def _(dve):
                for k in range(0, NC, 2):
                    dve.wait_ge(turned, k + 1)
                    dve.tensor_copy(dst[:, k, :], bank(ps, k))

            @block.scalar
            def _(act):
                for k in range(1, NC, 2):
                    act.wait_ge(turned, k + 1)
                    act.copy(dst[:, k, :], bank(ps, k))


def cross_attention(s, d, oacc, bad):
    nc, ps = s.nc, s.ps
    outer = ExitStack()
    with outer:
        def sb(ctx, name, shape, dt=F32):
            return ctx.enter_context(nc.sbuf_tensor(name, shape, dt))

        def sem(ctx, name):
            return ctx.enter_context(nc.semaphore(name))

        qs = sb(outer, "q_stack", [P, H, T], F32R)
        wk = [sb(outer, f"wk_{x}", [P, NK, C], F32R) for x in "hl"]
        wv = [sb(outer, f"wv_{x}", [P, NK, C], F32R) for x in "hl"]
        craw = sb(outer, "ctx_raw", [P, NK, KB])
        dacc = sb(outer, "den_acc", [P, G, HG, T])
        ctxT = d["ctxT"].rearrange("(k p) n -> p k n", p=P)

        with ExitStack() as ctx:
            x = sb(ctx, "x_in", [P, NT, C])
            xn = sb(ctx, "xn1", [P, NT, C])
            xnT = sb(ctx, "xnT1", [P, NC, T])
            wq = sb(ctx, "wq", [P, NC, C])
            wraw = sb(ctx, "w_raw", [P, 2, NK, C])
            qf = sb(ctx, "qf", [P, G, T])
            qh = sb(ctx, "qh", [P, G, T], F32R)
            ql = sb(ctx, "ql", [P, G, T], F32R)
            loaded = sem(ctx, "q_loaded")
            split_h = sem(ctx, "w_split_h")
            split_l = sem(ctx, "w_split_l")
            with nc.Block() as block:

                @block.sync
                def _(sp):
                    sp.dma_start(x[:, :, :], d["x"].rearrange("(t p) c -> p t c", p=P)).then_inc(loaded, 16)
                    sp.dma_start(s.ident[:, :], d["ident"]).then_inc(loaded, 16)
                    sp.dma_start(s.cols[:, :], d["cols"]).then_inc(loaded, 16)
                    sp.dma_start(wraw[:, 0], d["Wk"].rearrange("(k p) n -> p k n", p=P)).then_inc(loaded, 16)
                    sp.dma_start(wraw[:, 1], d["Wv"].rearrange("(k p) n -> p k n", p=P)).then_inc(loaded, 16)
                    sp.dma_start(wq[:, :, :], d["Wq"].rearrange("(k p) n -> p k n", p=P)).then_inc(loaded, 16)
                    sp.dma_start(craw[:, :, :], ctxT[:, :, 0:KB]).then_inc(loaded, 16)
                    sp.wait_ge(loaded, 112)

                @block.gpsimd
                def _(pool):
                    pool.memset(s.eps[:, :], EPS)
                    pool.memset(s.ones[:, :], 1.0)

            layer_norm(s, "ln1", x, xn)
            transpose_tokens(s, "ln1", xn, xnT)
            q_done = sem(ctx, "q_done")
            q_copied = sem(ctx, "q_copied")
            q_split = sem(ctx, "q_split")
            stacked = sem(ctx, "q_stacked")
            with nc.Block() as block:

                @block.tensor
                def _(pe):
                    for g in range(G):
                        for k in range(NC):
                            last = pe.matmul(bank(ps, g), wq[:, k, g * P:g * P + P], xnT[:, k, :],
                                             start=(k == 0), stop=(k == NC - 1))
                        last.then_inc(q_done, 1)

                @block.vector
                def _(dve):
                    for g in range(G):
                        dve.wait_ge(q_done, g + 1)
                        dve.tensor_scalar(qf[:, g, :], bank(ps, g), s.bq[:, g:g + 1], float(D) ** -0.5,
                                          ALU.add, ALU.mult).then_inc(q_copied, 1)
                        dve.wait_ge(q_copied, 2 * g + 1)
                        dve.tensor_copy(qh[:, g, :], qf[:, g, :]).then_inc(q_copied, 1)
                        dve.wait_ge(q_copied, 2 * g + 2)
                        dve.tensor_tensor(ql[:, g, :], qf[:, g, :], qh[:, g, :].bitcast(F32),
                                          ALU.subtract).then_inc(q_split, 1)

                @block.scalar
                def _(act):
                    for i, w in enumerate((wk, wv)):
                        act.copy(w[0][:, :, :], wraw[:, i]).then_inc(split_h, 1)

                @block.gpsimd
                def _(pool):
                    for i, w in enumerate((wk, wv)):
                        pool.wait_ge(split_h, i + 1)
                        pool.tensor_tensor(w[1][:, :, :], wraw[:, i], w[0][:, :, :].bitcast(F32), ALU.subtract)

                @block.sync
                def _(sp):
                    for g in range(G):
                        sp.wait_ge(q_split, g + 1)
                        for j in range(HG):
                            for half, part in enumerate((qh, ql)):
                                src = part[D * j:D * j + D, g:g + 1, :].bitcast(F32).broadcast_to([D, 2, T])
                                sp.dma_start(qs[64 * half:64 * half + 64, g * HG + j, :].bitcast(F32), src)\
                                  .then_inc(stacked, 16)
                    sp.dma_start(d["qT_d"].rearrange("(g p) n -> p g n", p=P), qf[:, :, :]).then_inc(stacked, 16)
                    sp.wait_ge(stacked, 16 * 2 * H + 16)

        with ExitStack() as ctx:
            ks = sb(ctx, "k_stack", [P, G, HG, KB], F32R)
            khl = [sb(ctx, f"k_split{i}", [P, 2, KB], F32R) for i in range(2)]
            vb = [sb(ctx, f"v{i}", [P, CB, C]) for i in range(2)]
            ch = [sb(ctx, f"ctx_h{i}", [P, NK, KB], F32R) for i in range(2)]
            cl = [sb(ctx, f"ctx_l{i}", [P, NK, KB], F32R) for i in range(2)]
            pr = [sb(ctx, f"probs{i}", [P, HG, T]) for i in range(2)]
            ND = 3

            names = ("ctx_loaded", "ch_done", "cl_done", "v_made", "k_made", "v_kept", "kh_kept", "kl_kept",
                     "sa_ready", "sb_ready", "ea_done", "eb_done", "pv_done", "o_kept", "den_dve", "den_pool", "o_cleared")
            (ctx_loaded, ch_done, cl_done, v_made, k_made, v_kept, kh_kept, kl_kept,
             sa_ready, sb_ready, ea_done, eb_done, pv_done, o_kept, den_dve, den_pool, o_cleared) = \
                [sem(ctx, n) for n in names]
            k_stacked = [sem(ctx, f"k_stacked{g}") for g in range(G)]
            SD = 16 * 2 * HG

            def sbank(j):
                return bank(ps, j)

            with nc.Block() as block:

                def ctx_low(pool, b, par, k):
                    pool.wait_ge(ch_done, b * NK + k + 1)
                    pool.tensor_tensor(cl[par][:, k, :], craw[:, k, :], ch[par][:, k, :].bitcast(F32),
                                       ALU.subtract).then_inc(cl_done, 1)

                @block.sync
                def _(sp):
                    def stack(b, g):
                        sp.wait_ge(kl_kept, b * G + g + 1)
                        for j in range(HG):
                            for half in range(2):
                                sp.dma_start(ks[64 * half:64 * half + 64, g, j, :].bitcast(F32),
                                             khl[g % 2][D * j:D * j + D, :, :].bitcast(F32)).then_inc(k_stacked[g], 16)

                    def load(b):
                        sp.wait_ge(cl_done, b * NK)
                        src = ctxT[:, :, bass.ds(b * KB, KB)]
                        sp.dma_start(craw[:, :, :], src).then_inc(ctx_loaded, 16)

                    load(1)
                    for g in range(G):
                        stack(0, g)

                    def blocks(it, last=False, first=False):
                        for par in range(2):
                            b = it * 2 + par
                            if not (first and par == 0):
                                stack(b, G - 1)
                            if not last:
                                load(b + 2)
                            if not (last and par == 1):
                                for g in range(G - 1):
                                    stack(b + 1, g)

                    blocks(0, first=True)
                    with sp.Fori(1, NB // 2 - 1) as it:
                        blocks(it)
                    blocks(NB // 2 - 1, last=True)

                @block.gpsimd
                def _(pool):
                    pool.memset(dacc[:, :, ND:, :], 0.0).then_inc(den_pool, 1)
                    for b in range(2):
                        for k in range(NK):
                            ctx_low(pool, b, b, k)

                    def blocks(it, last=False):
                        for par in range(2):
                            b = it * 2 + par
                            for i in range(U):
                                g = i // CB
                                n = b * U + i
                                pool.wait_ge(eb_done, n + 1)
                                pool.wait_ge(den_pool, n + 1)
                                pool.tensor_tensor(dacc[:, g, ND:, :], dacc[:, g, ND:, :], pr[i % 2][:, ND:, :],
                                                   ALU.add).then_inc(den_pool, 1)
                                if i in (6, 10, 14) and not last:
                                    ctx_low(pool, b + 2, par, i // 4 - 1)

                    blocks(0)
                    with pool.Fori(1, NB // 2 - 1) as it:
                        blocks(it)
                    blocks(NB // 2 - 1, last=True)

                @block.tensor
                def _(pe):
                    def product(b, par, kind, g, lo, hi):
                        if lo == 0:
                            if g == 0 and kind == "v":
                                pe.wait_ge(cl_done, b * NK + NK)
                            if kind == "v":
                                if isinstance(b, int) and b * CB + g == 0:
                                    pass
                                else:
                                    pe.wait_ge(v_kept, b * CB + g)
                            else:
                                if isinstance(b, int) and b * G + g == 0:
                                    pass
                                else:
                                    pe.wait_ge(kl_kept, b * G + g)
                        for m in range(lo, hi):
                            k, which = m // 3, m % 3
                            c = (ch, ch, cl)[which][par]
                            w = (wv if kind == "v" else wk)[(0, 1, 0)[which]]
                            cols = slice(g * P, g * P + P)
                            if kind == "v":
                                last = pe.matmul(bank(ps, 6), c[:, k, cols], w[:, k, :],
                                                 start=(m == 0), stop=(m == 8))
                            else:
                                last = pe.matmul(bank(ps, 7), w[:, k, cols], c[:, k, :],
                                                 start=(m == 0), stop=(m == 8))
                        if hi == 9:
                            last.then_inc(v_made if kind == "v" else k_made, 1)

                    def scores(b, i, pair, any_before=True):
                        g, c = i // CB, i % CB
                        if any_before:
                            pe.wait_ge((ea_done, eb_done)[pair], b * U + i)
                        if c == 0 and pair == 0:
                            pe.wait_ge(k_stacked[g], b * SD + SD)
                        for j in (2 * pair, 2 * pair + 1):
                            last = pe.matmul(sbank(j), ks[:, g, j, c * P:c * P + P], qs[:, g * HG + j, :],
                                             start=True, stop=True)
                        last.then_inc((sa_ready, sb_ready)[pair], 1)

                    for g in range(G):
                        product(0, 0, "v", g, 0, 9)
                        product(0, 0, "k", g, 0, 9)
                    scores(0, 0, 0, False)
                    scores(0, 0, 1, False)

                    def blocks(it, first=False, last=False):
                        for par in range(2):
                            b = it * 2 + par
                            end = last and par == 1
                            for i in range(U):
                                g, c = i // CB, i % CB
                                nxt = (b, i + 1) if i < U - 1 else (b + 1, 0)
                                if not (end and i == U - 1):
                                    scores(*nxt, 0)
                                if not end:
                                    kind = "v" if c < 2 else "k"
                                    lo, hi = ((0, 5), (5, 9))[c % 2]
                                    product(b + 1, 1 - par, kind, g, lo, hi)
                                if not (end and i == U - 1):
                                    scores(*nxt, 1)
                                else:
                                    pe.wait_ge(eb_done, b * U + i + 1)
                                if i == 0:
                                    pe.wait_ge(v_kept, b * CB + CB)
                                if c == 0 and not (first and par == 0 and g < 2):
                                    pe.wait_ge(o_kept, b * G + g - 1)
                                for j in range(HG):
                                    hd = (g * HG + j) * D
                                    last_mm = pe.matmul(ps[D * j:D * j + D, (4 + g % 2) * 512:(5 + g % 2) * 512],
                                                        vb[par][:, c, hd:hd + D], pr[i % 2][:, j, :],
                                                        start=(c == 0), stop=(c == CB - 1),
                                                        tile_position=(0, D * j))
                                last_mm.then_inc(pv_done, 1)

                    blocks(0, first=True)
                    with pe.Fori(1, NB // 2 - 1) as it:
                        blocks(it)
                    blocks(NB // 2 - 1, last=True)

                @block.scalar
                def _(act):
                    def keep_v(b, par, g, wait_free):
                        act.wait_ge(v_made, b * CB + g + 1)
                        if wait_free and g == 0:
                            act.wait_ge(pv_done, b * U - U)
                        act.copy(vb[par][:, g, :], bank(ps, 6)).then_inc(v_kept, 1)

                    def keep_kh(b, g, prev_stack):
                        act.wait_ge(k_made, b * G + g + 1)
                        if prev_stack is not None:
                            act.wait_ge(k_stacked[(g + 2) % G], prev_stack)
                        act.activation(khl[g % 2][:, 0, :], bank(ps, 7), ACT.Identity,
                                       bias=s.bk[:, g:g + 1]).then_inc(kh_kept, 1)

                    def exps(b, i, pair, wait_free=True):
                        n = b * U + i
                        act.wait_ge((sa_ready, sb_ready)[pair], n + 1)
                        if wait_free:
                            if pair == 0:
                                act.wait_ge(pv_done, n - 1)
                                act.wait_ge(den_dve, n)
                            else:
                                act.wait_ge(den_pool, n)
                        act.activation(pr[i % 2][:, 2 * pair:2 * pair + 2, :], ps[:, pair * 1024:pair * 1024 + 1024],
                                       ACT.Exp).then_inc((ea_done, eb_done)[pair], 1)

                    def ctx_high(b, par, k):
                        act.copy(ch[par][:, k, :], craw[:, k, :]).then_inc(ch_done, 1)

                    for b in range(2):
                        if b:
                            act.wait_ge(ctx_loaded, 16)
                        for k in range(NK):
                            ctx_high(b, b, k)
                    for g in range(G):
                        keep_v(0, 0, g, False)
                        keep_kh(0, g, SD if g >= 2 else None)

                    def blocks(it, first=False, last=False):
                        for par in range(2):
                            b = it * 2 + par
                            end = last and par == 1
                            for i in range(U):
                                g, c = i // CB, i % CB
                                free = not (first and par == 0 and i < 2)
                                exps(b, i, 0, free)
                                if i in (5, 9, 13) and not last:
                                    if i == 5:
                                        act.wait_ge(ctx_loaded, b * 16 + 32)
                                        act.wait_ge(k_made, b * G + G)
                                    ctx_high(b + 2, par, i // 4 - 1)
                                if c == 2 and not end:
                                    keep_v(b + 1, 1 - par, g, not (first and par == 0))
                                if c == 0:
                                    if i == 0:
                                        if not (first and par == 0):
                                            keep_kh(b, G - 1, b * SD + SD)
                                    elif not end:
                                        q = g - 1
                                        keep_kh(b + 1, q, b * SD + (2 * SD if q >= 2 else SD))
                                exps(b, i, 1, free)

                    blocks(0, first=True)
                    with act.Fori(1, NB // 2 - 1) as it:
                        blocks(it)
                    blocks(NB // 2 - 1, last=True)

                @block.vector
                def _(dve):
                    def keep_kl(b, g):
                        dve.wait_ge(kh_kept, b * G + g + 1)
                        dve.scalar_tensor_tensor(khl[g % 2][:, 1, :], bank(ps, 7), s.bk[:, g:g + 1],
                                                 khl[g % 2][:, 0, :].bitcast(F32), ALU.add,
                                                 ALU.subtract).then_inc(kl_kept, 1)

                    def keep_o(b, g, n):
                        dve.wait_ge(pv_done, n)
                        dve.tensor_tensor(oacc[:, g, :], oacc[:, g, :], bank(ps, 4 + g % 2),
                                          ALU.add).then_inc(o_kept, 1)

                    dve.memset(oacc[:, :, :], 0.0).then_inc(o_cleared, 1)
                    dve.memset(dacc[:, :, 0:ND, :], 0.0).then_inc(den_dve, 1)
                    for g in range(G):
                        keep_kl(0, g)
                    dve.wait_ge(o_cleared, 1)

                    def blocks(it, first=False, last=False):
                        for par in range(2):
                            b = it * 2 + par
                            end = last and par == 1
                            for i in range(U):
                                g, c = i // CB, i % CB
                                n = b * U + i
                                if c == 0:
                                    if i == 0:
                                        if not (first and par == 0):
                                            dve.wait_ge(o_kept, b * G - 1)
                                            keep_o(b - 1, G - 1, b * U)
                                            keep_kl(b, G - 1)
                                    else:
                                        if not (first and par == 0 and g == 1):
                                            dve.wait_ge(o_kept, b * G + g - 1)
                                        keep_o(b, g - 1, n)
                                        if not end:
                                            keep_kl(b + 1, g - 1)
                                dve.wait_ge(eb_done, n + 1)
                                dve.wait_ge(den_dve, n + 1)
                                dve.tensor_tensor(dacc[:, g, 0:ND, :], dacc[:, g, 0:ND, :], pr[i % 2][:, 0:ND, :],
                                                  ALU.add).then_inc(den_dve, 1)

                    blocks(0, first=True)
                    with dve.Fori(1, NB // 2 - 1) as it:
                        blocks(it)
                    blocks(NB // 2 - 1, last=True)
                    dve.wait_ge(o_kept, NB * G - 1)
                    keep_o(NB - 1, G - 1, NB * U)

        test_and_divide(s, d, oacc, dacc, bad)


def general_keys_values(s, d, kT_d, v_d, even):
    nc, ps = s.nc, s.ps
    with ExitStack() as ctx:
        def sb(name, shape, dt=F32):
            return ctx.enter_context(nc.sbuf_tensor(name, shape, dt))

        def sem(name):
            return ctx.enter_context(nc.semaphore(name))

        wk, wv = sb("g_wk", [P, NK, C]), sb("g_wv", [P, NK, C])
        cx = sb("g_ctx", [P, NK, KB])
        kb, vb = sb("g_k", [P, G, KB]), sb("g_v", [P, CB, C])
        c_in, k_made, v_made, kv_kept, stored = \
            [sem(n) for n in ("g_c_in", "g_k_made", "g_v_made", "g_kv_kept", "g_stored")]
        ctxT = d["ctxT"].rearrange("(k p) n -> p k n", p=P)
        with nc.Block() as block:

            @block.sync
            def _(sp):
                sp.dma_start(wk[:, :, :], d["Wk"].rearrange("(k p) n -> p k n", p=P)).then_inc(stored, 16)
                sp.dma_start(wv[:, :, :], d["Wv"].rearrange("(k p) n -> p k n", p=P)).then_inc(stored, 16)
                with sp.Fori(0, NB) as b:
                    sp.dma_start(cx[:, :, :], ctxT[:, :, bass.ds(b * KB, KB)]).then_inc(c_in, 16)
                    sp.wait_ge(kv_kept, b * (G + CB) + G + CB)
                    sp.dma_start(kT_d.rearrange("(g p) n -> p g n", p=P)[:, :, bass.ds(b * KB, KB)], kb[:, :, :])\
                      .then_inc(stored, 16)
                    sp.dma_start(v_d.rearrange("(b c p) n -> b p c n", p=P, c=CB)[bass.ds(b, 1)].squeeze(0),
                                 vb[:, :, :]).then_inc(stored, 16)
                sp.wait_ge(stored, NB * 32 + 32)

            @block.tensor
            def _(pe):
                pe.wait_ge(stored, 32)
                with pe.Fori(0, NB) as b:
                    pe.wait_ge(c_in, b * 16 + 16)
                    for g in range(G):
                        for k in range(NK):
                            last = pe.matmul(bank(ps, g), wk[:, k, g * P:g * P + P], cx[:, k, :],
                                             start=(k == 0), stop=(k == NK - 1))
                        last.then_inc(k_made, 1)
                    for c in range(CB):
                        for k in range(NK):
                            last = pe.matmul(bank(ps, 4 + c), cx[:, k, c * P:c * P + P], wv[:, k, :],
                                             start=(k == 0), stop=(k == NK - 1))
                        last.then_inc(v_made, 1)

            @block.gpsimd
            def _(pool):
                pool.memset(even[:, :], 1.0 / N)

            @block.scalar
            def _(act):
                with act.Fori(0, NB) as b:
                    act.wait_ge(stored, b * 32 + 32)
                    for g in range(G):
                        act.wait_ge(k_made, b * G + g + 1)
                        act.activation(kb[:, g, :], bank(ps, g), ACT.Identity, bias=s.bk[:, g:g + 1])\
                           .then_inc(kv_kept, 1)

            @block.vector
            def _(dve):
                with dve.Fori(0, NB) as b:
                    dve.wait_ge(stored, b * 32 + 32)
                    for c in range(CB):
                        dve.wait_ge(v_made, b * CB + c + 1)
                        dve.tensor_copy(vb[:, c, :], bank(ps, 4 + c)).then_inc(kv_kept, 1)


def general_heads(s, d, kT_d, v_d, even, oacc):
    nc, ps = s.nc, s.ps
    o_d, m_d = [nc.dram_tensor(n, (C, T), F32).ap() for n in ("o_d", "mean_d")]
    CLAMP = 10000.0
    NS = N // 512
    with ExitStack() as ctx:
        def sb(name, shape, dt=F32):
            return ctx.enter_context(nc.sbuf_tensor(name, shape, dt))

        def sem(name):
            return ctx.enter_context(nc.semaphore(name))

        q, k, v = sb("g_qh", [D, P]), sb("g_kh", [D, N]), sb("g_vh", [P, N // P, D])
        sc, eq, pT = sb("g_sc", [P, N]), sb("g_eq", [P, N]), sb("g_pT", [P, N // P, P])
        ot, mt = sb("g_ot", [D, P]), sb("g_mt", [D, P])
        own, flag, mx, nmx = sb("g_own", [P, 1]), sb("g_flag", [P, 1]), sb("g_mx", [P, 1]), sb("g_nmx", [P, 1])
        den, rden = sb("g_den", [P, 1]), sb("g_rden", [P, 1])
        mean, om = sb("g_mean", [P, G, T]), sb("g_om", [P, G, T])
        mask = sb("g_mask", [P, G, T], I32)
        (loaded, s_made, s_kept, step, max_done, e_done, p_done, t_made, t_kept, o_made, o_kept, stored, back,
         flag_done, count_made) = \
            [sem("g_" + n) for n in ("loaded", "s_made", "s_kept", "step", "max_done", "e_done", "p_done", "t_made",
                                     "t_kept", "o_made", "o_kept", "out", "back", "flag_done", "count_made")]
        STEPS = 7
        with nc.Block() as block:

            @block.sync
            def _(sp):
                with sp.Fori(0, H) as h:
                    with sp.Fori(0, NT) as t:
                        r = h * NT + t
                        sp.wait_ge(stored, r * 32 + 32)
                        sp.dma_start(q[:, :], d["qT_d"][bass.ds(h * D, D), bass.ds(t * P, P)]).then_inc(loaded, 16)
                        sp.dma_start(k[:, :], kT_d[bass.ds(h * D, D), :]).then_inc(loaded, 16)
                        sp.dma_start(v[:, :, :], v_d.rearrange("(c p) n -> p c n", p=P)[:, :, bass.ds(h * D, D)])\
                          .then_inc(loaded, 16)
                        sp.wait_ge(o_kept, r * 2 + 2)
                        sp.dma_start(o_d[bass.ds(h * D, D), bass.ds(t * P, P)], ot[:, :]).then_inc(stored, 16)
                        sp.dma_start(m_d[bass.ds(h * D, D), bass.ds(t * P, P)], mt[:, :]).then_inc(stored, 16)
                sp.wait_ge(stored, H * NT * 32 + 32)
                sp.dma_start(om[:, :, :], o_d.rearrange("(g p) n -> p g n", p=P)).then_inc(back, 16)
                sp.dma_start(mean[:, :, :], m_d.rearrange("(g p) n -> p g n", p=P)).then_inc(back, 16)

            @block.tensor
            def _(pe):
                with pe.Fori(0, H) as h:
                    with pe.Fori(0, NT) as t:
                        r = h * NT + t
                        pe.wait_ge(loaded, r * 48 + 48)
                        for j in range(NS):
                            if j >= 8:
                                pe.wait_ge(s_kept, r * NS + j - 7)
                            pe.matmul(bank(ps, j % 8), q[:, :], k[:, j * 512:j * 512 + 512], start=True,
                                      stop=True).then_inc(s_made, 1)
                        pe.wait_ge(p_done, r + 1)
                        for j in range(NS):
                            if j >= 8:
                                pe.wait_ge(t_kept, r * NS + j - 7)
                            for i in range(4):
                                c = 4 * j + i
                                last = pe.transpose(ps[:, (j % 8) * 512 + i * P:(j % 8) * 512 + i * P + P],
                                                    sc[:, c * P:c * P + P], s.ident[:, :])
                            last.then_inc(t_made, 1)
                        pe.wait_ge(t_kept, r * NS + NS)
                        for c in range(N // P):
                            last = pe.matmul(ps[0:D, 0:P], v[:, c, :], pT[:, c, :], start=(c == 0),
                                             stop=(c == N // P - 1))
                        last.then_inc(o_made, 1)
                        for c in range(N // P):
                            last = pe.matmul(ps[0:D, 512:512 + P], v[:, c, :], even[:, :], start=(c == 0),
                                             stop=(c == N // P - 1))
                        last.then_inc(o_made, 1)
                pe.wait_ge(flag_done, 1)
                pe.matmul(ps[:, 0:1], s.ones[:, :], flag[:, :], start=True, stop=True).then_inc(count_made, 1)

            @block.gpsimd
            def _(pool):
                pool.memset(mt[:, :], 0.0).then_inc(stored, 32)

            @block.scalar
            def _(act):
                with act.Fori(0, H) as h:
                    with act.Fori(0, NT) as t:
                        r = h * NT + t
                        act.wait_ge(max_done, r + 1)
                        act.activation(sc[:, :], sc[:, :], ACT.Exp, bias=nmx[:, 0:1], accum_out=den[:, 0:1])\
                           .then_inc(e_done, 1)

            @block.vector
            def _(dve):
                dve.memset(flag[:, :], 1.0).then_inc(step, 1)
                with dve.Fori(0, H) as h:
                    with dve.Fori(0, NT) as t:
                        r = h * NT + t
                        for j in range(NS):
                            dve.wait_ge(s_made, r * NS + j + 1)
                            dve.tensor_copy(sc[:, j * 512:j * 512 + 512], bank(ps, j % 8)).then_inc(s_kept, 1)
                        dve.wait_ge(s_kept, r * NS + NS)

                        def then(n, ins):
                            ins.then_inc(step, 1)
                            dve.wait_ge(step, r * STEPS + n + 1)

                        then(1, dve.tensor_tensor(eq[:, :], sc[:, :], sc[:, :], ALU.is_equal))
                        then(2, dve.tensor_reduce(own[:, :], eq[:, :], AX.X, ALU.min))
                        then(3, dve.tensor_tensor(flag[:, :], flag[:, :], own[:, :], ALU.min))
                        then(4, dve.tensor_scalar(sc[:, :], sc[:, :], -CLAMP, CLAMP, ALU.max, ALU.min))
                        then(5, dve.tensor_reduce(mx[:, :], sc[:, :], AX.X, ALU.max))
                        dve.tensor_scalar(nmx[:, :], mx[:, :], -1.0, None, ALU.mult).then_inc(max_done, 1)
                        dve.wait_ge(e_done, r + 1)
                        then(6, dve.reciprocal(rden[:, :], den[:, :]))
                        then(7, dve.tensor_scalar(sc[:, :], sc[:, :], rden[:, 0:1], None, ALU.mult))
                        dve.memset(own[:, :], 0.0).then_inc(p_done, 1)
                        for j in range(NS):
                            dve.wait_ge(t_made, r * NS + j + 1)
                            dve.tensor_copy(pT[:, 4 * j:4 * j + 4, :],
                                            bank(ps, j % 8).rearrange("p (c n) -> p c n", n=P)).then_inc(t_kept, 1)
                        dve.wait_ge(o_made, r * 2 + 2)
                        dve.tensor_copy(ot[:, :], ps[0:D, 0:P]).then_inc(o_kept, 1)
                        dve.tensor_copy(mt[:, :], ps[0:D, 512:512 + P]).then_inc(o_kept, 1)
                dve.memset(own[:, :], 0.0).then_inc(flag_done, 1)
                dve.wait_ge(back, 32)
                dve.tensor_copy(oacc[:, :, :], om[:, :, :]).then_inc(step, 1)
                dve.wait_ge(count_made, 1)
                dve.tensor_scalar(mask[:, :, :], ps[:, 0:1].unsqueeze(2).broadcast_to([P, G, T]), float(P), None,
                                  ALU.is_lt).then_inc(step, 1)
                dve.wait_ge(step, H * NT * STEPS + 3)
                dve.copy_predicated(oacc[:, :, :], mask[:, :, :], mean[:, :, :])


def general_cross(s, d, oacc):
    nc = s.nc
    kT_d, v_d = nc.dram_tensor("kT_d", (C, N), F32).ap(), nc.dram_tensor("v_d", (N, C), F32).ap()
    with nc.sbuf_tensor("g_even", [P, P], F32) as even:
        general_keys_values(s, d, kT_d, v_d, even)
        general_heads(s, d, kT_d, v_d, even, oacc)


def test_and_divide(s, d, oacc, dacc, bad):
    nc, ps = s.nc, s.ps
    with ExitStack() as ctx:
        def sb(name, shape, dt=F32):
            return ctx.enter_context(nc.sbuf_tensor(name, shape, dt))

        def sem(name):
            return ctx.enter_context(nc.semaphore(name))

        rden = sb("rden", [P, G, T])
        low = sb("low", [P, G, T])
        mid = sb("mid", [P, G, T])
        okc = sb("ok_cols", [P, 2 * G])
        okm = sb("ok_min", [P, 1])
        den_made, rec_done, low_done, mid_done, ok_done, min_done, sum_made = \
            [sem(n) for n in ("den_made", "rec_done", "low_done", "mid_done", "ok_done", "min_done", "sum_made")]
        with nc.Block() as block:

            @block.tensor
            def _(pe):
                for g in range(G):
                    for j in range(HG):
                        last = pe.matmul(ps[D * j:D * j + D, g * 512:g * 512 + T], s.ones[:, 0:D],
                                         dacc[:, g, j, :], start=True, stop=True, tile_position=(0, D * j))
                    last.then_inc(den_made, 1)
                pe.wait_ge(min_done, 1)
                pe.matmul(ps[:, 4 * 512:4 * 512 + 1], s.ones[:, :], okm[:, :], start=True,
                          stop=True).then_inc(sum_made, 1)

            @block.gpsimd
            def _(pool):
                for g in range(G):
                    pool.tensor_scalar(mid[:, g, :], oacc[:, g, :], -SUM_MAX, None, ALU.is_ge).then_inc(mid_done, 1)

            @block.vector
            def _(dve):
                for g in range(G):
                    dve.wait_ge(den_made, g + 1)
                    dve.reciprocal(rden[:, g, :], bank(ps, g)).then_inc(rec_done, 1)
                    dve.tensor_scalar(low[:, g, :], bank(ps, g), DEN_MIN, None, ALU.is_ge).then_inc(low_done, 1)
                    dve.wait_ge(low_done, 3 * g + 1)
                    dve.scalar_tensor_tensor(low[:, g, :], bank(ps, g), DEN_MAX, low[:, g, :], ALU.is_le,
                                             ALU.mult).then_inc(low_done, 1)
                    dve.wait_ge(mid_done, g + 1)
                    dve.scalar_tensor_tensor(mid[:, g, :], oacc[:, g, :], SUM_MAX, mid[:, g, :], ALU.is_le,
                                             ALU.mult).then_inc(low_done, 1)
                    dve.wait_ge(low_done, 3 * g + 3)
                    dve.tensor_reduce(okc[:, 2 * g:2 * g + 1], low[:, g, :], AX.X, ALU.min).then_inc(ok_done, 1)
                    dve.tensor_reduce(okc[:, 2 * g + 1:2 * g + 2], mid[:, g, :], AX.X, ALU.min)\
                       .then_inc(ok_done, 1)
                    dve.wait_ge(rec_done, g + 1)
                    dve.tensor_tensor(oacc[:, g, :], oacc[:, g, :], rden[:, g, :], ALU.mult)
                dve.wait_ge(ok_done, 2 * G)
                dve.tensor_reduce(okm[:, :], okc[:, :], AX.X, ALU.min).then_inc(min_done, 1)
                dve.wait_ge(sum_made, 1)
                dve.tensor_scalar(bad[:, :], ps[:, 4 * 512:4 * 512 + 1], float(P), None, ALU.is_lt)


def cross_output(s, d, oacc, x_out):
    nc, ps = s.nc, s.ps
    with ExitStack() as ctx:
        def sb(name, shape, dt=F32):
            return ctx.enter_context(nc.sbuf_tensor(name, shape, dt))

        def sem(name):
            return ctx.enter_context(nc.semaphore(name))

        wo = sb("wo_x", [P, NC, C])
        bo = sb("bo_x", [P, C])
        x = sb("x_again", [P, NT, C])
        loaded, o_ready, y_made, out_sum = [sem(n) for n in ("f_loaded", "o_ready", "y_made", "out_sum")]
        with nc.Block() as block:

            @block.sync
            def _(sp):
                sp.dma_start(wo[:, :, :], d["Wo"].rearrange("(k p) n -> p k n", p=P)).then_inc(loaded, 16)
                sp.dma_start(bo[:, :], d["bo"].partition_broadcast(P)).then_inc(loaded, 16)
                sp.dma_start(x[:, :, :], d["x"].rearrange("(t p) c -> p t c", p=P)).then_inc(loaded, 16)

            @block.tensor
            def _(pe):
                pe.wait_ge(loaded, 48)
                pe.wait_ge(o_ready, G)
                for t in range(NT):
                    for g in range(G):
                        last = pe.matmul(bank(ps, t), oacc[:, g, t * P:t * P + P], wo[:, g, :],
                                         start=(g == 0), stop=(g == G - 1))
                    last.then_inc(y_made, 1)

            @block.vector
            def _(dve):
                for t in range(NT):
                    dve.wait_ge(y_made, t + 1)
                    dve.wait_ge(out_sum, t + 1)
                    dve.tensor_tensor(x_out[:, t, :], x[:, t, :], bank(ps, t), ALU.add)

            @block.scalar
            def _(act):
                for g in range(G):
                    act.activation(oacc[:, g, :], oacc[:, g, :], ACT.Identity, bias=s.bv[:, g:g + 1])\
                       .then_inc(o_ready, 1)

            @block.gpsimd
            def _(pool):
                pool.wait_ge(loaded, 48)
                for t in range(NT):
                    pool.tensor_tensor(x[:, t, :], x[:, t, :], bo[:, :], ALU.add).then_inc(out_sum, 1)


def self_attention(s, d, x, x_out):
    nc, ps = s.nc, s.ps
    with ExitStack() as ctx:
        def sb(name, shape, dt=F32):
            return ctx.enter_context(nc.sbuf_tensor(name, shape, dt))

        def sem(name):
            return ctx.enter_context(nc.semaphore(name))

        wo = sb("wo_s", [P, NC, C])
        strip = sb("strip", [P, T])
        qs = sb("q_stack_s", [P, H, T], F32R)
        ks = sb("k_stack_s", [P, H, T], F32R)
        v = sb("v_s", [P, NT, C])
        qh, ql = sb("qh_s", [P, G, T], F32R), sb("ql_s", [P, G, T], F32R)
        khl = sb("khl_s", [P, G, 2, T], F32R)
        early = ctx.enter_context(ExitStack())

        def eb(name, shape, dt=F32):
            return early.enter_context(nc.sbuf_tensor(name, shape, dt))

        w = [eb(f"w{n}_s", [P, NC, C]) for n in "qkv"] + [wo]
        xn = eb("xn2", [P, NT, C])
        xnT = eb("xnT2", [P, NC, T])
        qf = eb("qf_s", [P, G, T])
        loaded = sem("s_loaded")
        with nc.Block() as block:

            @block.sync
            def _(sp):
                for wt, n in zip(w, "qkvo"):
                    sp.dma_start(wt[:, :, :], d[f"W{n}T_s"].rearrange("(k p) n -> p k n", p=P)).then_inc(loaded, 16)
                sp.dma_start(strip[:, :], d["strip"]).then_inc(loaded, 16)

        layer_norm(s, "ln2", x, xn)
        transpose_tokens(s, "ln2", xn, xnT)

        first = [0, P, 512, 1024]
        width = [P * (t + 1) for t in range(NT)]
        kept = [sum(width[:t]) for t in range(NT)]
        tot = sum(width)
        tfirst = [0, 1024, 512, 512 + 256]
        twidth = [T - P * c for c in range(NT)]
        tkept = [sum(twidth[:c]) for c in range(NT)]

        proj = sem("s_proj")
        q_step, k_step, ql_done, kl_done = [sem(n) for n in ("q_step", "k_step_s", "ql_done", "kl_done_s")]
        v_kept = sem("v_kept_s")
        q_in = [sem(f"q_in{g}") for g in range(G)]
        k_in = [sem(f"k_in{g}") for g in range(G)]
        bias_done, s_made, m_done, nm_done, e_done, r_done, n_done = \
            [sem(n) for n in ("bias_done", "s_made", "m_done", "nm_done", "e_done", "r_done", "n_done")]
        t_made, t_kept_a, t_kept_d, o_made, o_kept, y_made = \
            [sem(n) for n in ("t_made", "t_kept_a", "t_kept_d", "o_made_s", "o_kept_s", "y_made_s")]

        with nc.Block() as block:

            @block.tensor
            def _(pe):
                pe.wait_ge(loaded, 80)
                for g in range(G):
                    for i in range(2):
                        for k in range(NC):
                            last = pe.matmul(bank(ps, 2 * g + i), w[i][:, k, g * P:g * P + P], xnT[:, k, :],
                                             start=(k == 0), stop=(k == NC - 1))
                        last.then_inc(proj, 1)
                for t in range(NT):
                    pe.wait_ge((ql_done, kl_done)[t % 2], t // 2 + 1)
                    for k in range(NC):
                        last = pe.matmul(bank(ps, t), xnT[:, k, t * P:t * P + P], w[2][:, k, :],
                                         start=(k == 0), stop=(k == NC - 1))
                    last.then_inc(proj, 1)

            @block.vector
            def _(dve):
                for g in range(G):
                    dve.wait_ge(proj, 2 * g + 1)
                    dve.tensor_scalar(qf[:, g, :], bank(ps, 2 * g), float(D) ** -0.5, None, ALU.mult)\
                       .then_inc(q_step, 1)
                    dve.wait_ge(q_step, 2 * g + 1)
                    dve.tensor_copy(qh[:, g, :], qf[:, g, :]).then_inc(q_step, 1)
                    dve.wait_ge(q_step, 2 * g + 2)
                    dve.tensor_tensor(ql[:, g, :], qf[:, g, :], qh[:, g, :].bitcast(F32), ALU.subtract)\
                       .then_inc(ql_done, 1)
                    dve.wait_ge(k_step, g + 1)
                    dve.tensor_tensor(khl[:, g, 1, :], bank(ps, 2 * g + 1), khl[:, g, 0, :].bitcast(F32),
                                      ALU.subtract).then_inc(kl_done, 1)

            @block.scalar
            def _(act):
                for g in range(G):
                    act.wait_ge(proj, 2 * g + 2)
                    act.copy(khl[:, g, 0, :], bank(ps, 2 * g + 1)).then_inc(k_step, 1)
                for t in range(NT):
                    act.wait_ge(proj, 2 * G + t + 1)
                    act.copy(v[:, t, :], bank(ps, t)).then_inc(v_kept, 1)

            @block.sync
            def _(sp):
                for g in range(G):
                    sp.wait_ge(ql_done, g + 1)
                    for j in range(HG):
                        for half, part in enumerate((qh, ql)):
                            src = part[D * j:D * j + D, g:g + 1, :].bitcast(F32).broadcast_to([D, 2, T])
                            sp.dma_start(qs[64 * half:64 * half + 64, g * HG + j, :].bitcast(F32), src)\
                              .then_inc(q_in[g], 16)

            @block.gpsimd
            def _(pool):
                for g in range(G):
                    pool.wait_ge(kl_done, g + 1)
                    for j in range(HG):
                        for half in range(2):
                            pool.dma_start(ks[64 * half:64 * half + 64, g * HG + j, :].bitcast(F32),
                                           khl[D * j:D * j + D, g, :, :].bitcast(F32)).then_inc(k_in[g], 16)

        early.close()
        sc = [sb(f"scores{i}", [P, tot]) for i in range(2)]
        pT = [sb(f"probsT{i}", [P, HG, tot]) for i in range(2)]
        bias = [sb(f"bias{i}", [P, T]) for i in range(2)]
        mx = sb("mx", [P, H, NT])
        nmx = sb("nmx", [P, H, NT])
        den = sb("den", [P, H, NT])
        rden = sb("rden_s", [P, H, NT])
        oT = sb("oT", [P, G, T])

        with nc.Block() as block:

            @block.tensor
            def _(pe):
                def scores(h):
                    if h % HG == 0:
                        pe.wait_ge(q_in[h // HG], 128)
                        pe.wait_ge(k_in[h // HG], 128)
                    if h:
                        pe.wait_ge(m_done, h * NT)
                    for t in range(NT):
                        pe.matmul(ps[:, first[t]:first[t] + width[t]], qs[:, h, t * P:t * P + P],
                                  ks[:, h, 0:width[t]], start=True, stop=True).then_inc(s_made, 1)

                def turn(h):
                    pe.wait_ge(n_done, h * NT + NT)
                    if h:
                        pe.wait_ge(t_kept_a, 2 * h)
                        pe.wait_ge(t_kept_d, h)
                    for c in range(NT):
                        for t in range(c, NT):
                            at = 1536 + tfirst[c] + (t - c) * P
                            last = pe.transpose(ps[:, at:at + P], sc[h % 2][:, kept[t] + c * P:kept[t] + c * P + P],
                                                s.ident[:, :])
                    last.then_inc(t_made, 1)

                def weighted(g):
                    pe.wait_ge(t_kept_a, 2 * (g * HG + HG))
                    pe.wait_ge(t_kept_d, g * HG + HG)
                    if g >= 2:
                        pe.wait_ge(o_kept, g - 1)
                    b = 6 + g % 2
                    for c in range(NT):
                        for j in range(HG):
                            hd = (g * HG + j) * D
                            last = pe.matmul(ps[D * j:D * j + D, b * 512 + c * P:b * 512 + T], v[:, c, hd:hd + D],
                                             pT[g % 2][:, j, tkept[c]:tkept[c] + twidth[c]],
                                             start=(c == 0), stop=(c == NT - 1), tile_position=(0, D * j),
                                             skip_group_check=True)
                    last.then_inc(o_made, 1)

                scores(0)
                for h in range(H):
                    if h + 1 < H:
                        scores(h + 1)
                    turn(h)
                    if h % HG == 0 and h:
                        weighted(h // HG - 1)
                weighted(G - 1)
                pe.wait_ge(o_kept, G)
                for t in range(NT):
                    for g in range(G):
                        last = pe.matmul(bank(ps, t), oT[:, g, t * P:t * P + P], w[3][:, g, :],
                                         start=(g == 0), stop=(g == G - 1))
                    last.then_inc(y_made, 1)

            @block.vector
            def _(dve):
                def finish(h):
                    dve.wait_ge(e_done, h * NT + NT)
                    dve.reciprocal(rden[:, h, :], den[:, h, :]).then_inc(r_done, 1)
                    dve.wait_ge(r_done, h + 1)
                    for t in range(NT):
                        p = sc[h % 2][:, kept[t]:kept[t] + width[t]]
                        dve.tensor_scalar(p, p, rden[:, h, t:t + 1], None, ALU.mult).then_inc(n_done, 1)

                def keep(h):
                    dve.wait_ge(t_made, h + 1)
                    if h >= 2 * HG and h % HG == 0:
                        dve.wait_ge(o_made, h // HG - 1)
                    g, j = h // HG, h % HG
                    dve.tensor_copy(pT[g % 2][:, j, 0:512], ps[:, 1536:2048]).then_inc(t_kept_d, 1)

                def keep_o(g):
                    dve.wait_ge(o_made, g + 1)
                    dve.tensor_copy(oT[:, g, :], bank(ps, 6 + g % 2)).then_inc(o_kept, 1)

                for h in range(H):
                    dve.wait_ge(bias_done, h + 1)
                    if h >= 2:
                        dve.wait_ge(t_made, h - 1)
                    for t in range(NT):
                        dve.wait_ge(s_made, h * NT + max(t, 1) + 1)
                        dve.tensor_tensor_reduce(out=sc[h % 2][:, kept[t]:kept[t] + width[t]],
                                                 in0=ps[:, first[t]:first[t] + width[t]],
                                                 in1=bias[h % 2][:, T - width[t]:T], scale=1.0, scalar=NEG,
                                                 op0=ALU.add, op1=ALU.max, accum_out=mx[:, h, t:t + 1])\
                           .then_inc(m_done, 1)
                    dve.wait_ge(m_done, h * NT + NT)
                    dve.tensor_scalar(nmx[:, h, :], mx[:, h, :], -1.0, None, ALU.mult).then_inc(nm_done, 1)
                    if h:
                        finish(h - 1)
                    if h >= 2:
                        keep(h - 2)
                    if h % HG == 2 and h > HG:
                        keep_o(h // HG - 1)
                finish(H - 1)
                keep(H - 2)
                keep(H - 1)
                keep_o(G - 1)
                for t in range(NT):
                    dve.wait_ge(y_made, t + 1)
                    dve.tensor_tensor(x_out[:, t, :], x[:, t, :], bank(ps, t), ALU.add)

            @block.scalar
            def _(act):
                def make_bias(h):
                    if h >= 2:
                        act.wait_ge(m_done, (h - 1) * NT)
                    act.mul(bias[h % 2][:, :], strip[:, :], 2.0 ** (-8.0 / H * (h + 1))).then_inc(bias_done, 1)

                def keep(h):
                    g, j = h // HG, h % HG
                    act.wait_ge(t_made, h + 1)
                    if h >= 2 * HG and h % HG == 0:
                        act.wait_ge(o_made, h // HG - 1)
                    act.copy(pT[g % 2][:, j, 512:512 + 384], ps[:, 1536 + 1024:1536 + 1024 + 384])\
                       .then_inc(t_kept_a, 1)
                    act.copy(pT[g % 2][:, j, 896:1280], ps[:, 1536 + 512:1536 + 512 + 384]).then_inc(t_kept_a, 1)

                make_bias(0)
                make_bias(1)
                for h in range(H):
                    act.wait_ge(nm_done, h + 1)
                    for t in range(NT):
                        p = sc[h % 2][:, kept[t]:kept[t] + width[t]]
                        act.activation(p, p, ACT.Exp, bias=nmx[:, h, t:t + 1],
                                       accum_out=den[:, h, t:t + 1]).then_inc(e_done, 1)
                    if h + 2 < H:
                        make_bias(h + 2)
                    if h:
                        keep(h - 1)
                keep(H - 1)


NEG = -3.0e38


def feed_forward(s, d, x, x_out):
    nc, ps = s.nc, s.ps
    E, HID = 8, 2048
    HC = HID // 512
    TILES = T // P + E
    with ExitStack() as ctx:
        def sb(name, shape, dt=F32):
            return ctx.enter_context(nc.sbuf_tensor(name, shape, dt))

        def sem(name):
            return ctx.enter_context(nc.semaphore(name))

        xn = sb("xn3", [P, NT, C])
        xh, xl = sb("xs_h", [P, NT, C], F32R), sb("xs_l", [P, NT, C], F32R)
        pos = sb("pos", [P, NT])
        table = sb("table", [1, TILES + 1], I32)
        iota = sb("iota", [P, P])
        w1 = [sb(f"w1_{i}", [P, NC, 512]) for i in range(HC)]
        w2 = [sb(f"w2_{i}", [P, 4, C]) for i in range(HC)]
        b1, b2 = sb("b1", [P, HID // P]), sb("b2", [P, C])
        loaded = sem("r_loaded")

        with ExitStack() as rc:
            def rb(name, shape, dt=F32):
                return rc.enter_context(nc.sbuf_tensor(name, shape, dt))

            xnT = rb("xnT3", [P, NC, T])
            gw, gb = rb("gate_w", [P, NC, E]), rb("gate_b", [P, E])
            tri, iota8, iotaT = rb("tri", [P, P]), rb("iota8", [P, E]), rb("iotaT", [P, TILES])
            with nc.Block() as block:

                @block.sync
                def _(sp):
                    sp.dma_start(gw[:, :, :], d["gate_w"].rearrange("(k p) e -> p k e", p=P)).then_inc(loaded, 16)
                    sp.dma_start(gb[:, :], d["gate_b"].partition_broadcast(P)).then_inc(loaded, 16)
                    sp.dma_start(tri[:, :], d["tri"]).then_inc(loaded, 16)
                    sp.dma_start(iota[:, :], d["iota"].partition_broadcast(P)).then_inc(loaded, 16)
                    sp.dma_start(iota8[:, :], d["iota"][0:E].partition_broadcast(P)).then_inc(loaded, 16)
                    sp.dma_start(iotaT[:, :], d["iota"][0:TILES].partition_broadcast(P)).then_inc(loaded, 16)

            layer_norm(s, "ln3", x, xn)
            transpose_tokens(s, "ln3", xn, xnT)

            A = [rb(f"route{i}", [P, NT, E]) for i in range(12)]
            (lg, ex, sco, e1, c1, o1, s2, c2, oh, pre, rk, tmp) = A
            S = [rb(f"tok{i}", [P, NT]) for i in range(11)]
            (m, sm, rs, m1, i1, m2, i2, v1, v2, es, wt) = S
            sums = rb("sums", [P, E])
            cum = [rb(f"cum{i}", [P, 2 * E]) for i in range(4)]
            nt4 = rb("nt4", [P, E, 4])
            cmp = rb("cmp", [P, TILES, E])
            tabf = rb("tabf", [P, TILES + 1])
            step, lg_made, shifted, exped, rank_made, oh_ready = \
                [rc.enter_context(nc.semaphore(n)) for n in ("r_step", "lg_made", "shifted", "exped", "rank_made",
                                                             "oh_ready")]

            def row(t):
                return t[:, :].unsqueeze(2).broadcast_to([P, NT, E])

            i8 = iota8[:, :].unsqueeze(1).broadcast_to([P, NT, E])
            with nc.Block() as block:

                @block.tensor
                def _(pe):
                    pe.wait_ge(loaded, 96)
                    for t in range(NT):
                        for k in range(NC):
                            last = pe.matmul(ps[:, t * E:t * E + E], xnT[:, k, t * P:t * P + P], gw[:, k, :],
                                             start=(k == 0), stop=(k == NC - 1))
                    last.then_inc(lg_made, 1)
                    pe.wait_ge(oh_ready, 1)
                    pe.matmul(ps[:, 512:512 + NT * E], s.ones[:, :], pre[:, :, :], start=True, stop=False)
                    pe.matmul(ps[:, 512:512 + NT * E], tri[:, :], oh[:, :, :], start=False, stop=True)
                    pe.matmul(ps[:, 1024:1024 + E], s.ones[:, :], sums[:, :], start=True,
                              stop=True).then_inc(rank_made, 1)

                @block.scalar
                def _(act):
                    act.wait_ge(shifted, 1)
                    act.activation(ex[:, :, :], tmp[:, :, :], ACT.Exp).then_inc(exped, 1)

                @block.vector
                def _(dve):
                    n = [0]

                    def then(ins):
                        n[0] += 1
                        ins.then_inc(step, 1)
                        dve.wait_ge(step, n[0])

                    dve.wait_ge(lg_made, 1)
                    psl = ps[:, 0:NT * E].rearrange("p (t e) -> p t e", e=E)
                    then(dve.tensor_tensor(lg[:, :, :], psl, gb[:, :].unsqueeze(1).broadcast_to([P, NT, E]), ALU.add))
                    then(dve.tensor_reduce(m[:, :], lg[:, :, :], AX.X, ALU.max))
                    dve.tensor_tensor(tmp[:, :, :], lg[:, :, :], row(m), ALU.subtract).then_inc(shifted, 1)
                    dve.wait_ge(exped, 1)
                    then(dve.tensor_reduce(sm[:, :], ex[:, :, :], AX.X, ALU.add))
                    then(dve.reciprocal(rs[:, :], sm[:, :]))
                    then(dve.tensor_tensor(sco[:, :, :], ex[:, :, :], row(rs), ALU.mult))

                    def top(src, val, idx, eq, cand):
                        then(dve.tensor_reduce(val[:, :], src[:, :, :], AX.X, ALU.max))
                        then(dve.tensor_tensor(eq[:, :, :], src[:, :, :], row(val), ALU.is_equal))
                        then(dve.scalar_tensor_tensor(cand[:, :, :], eq[:, :, :], -float(E), i8, ALU.mult, ALU.add))
                        then(dve.tensor_reduce(idx[:, :], cand[:, :, :], AX.X, ALU.min))
                        then(dve.tensor_scalar(idx[:, :], idx[:, :], float(E), None, ALU.add))

                    top(sco, m1, i1, e1, c1)
                    then(dve.tensor_tensor(o1[:, :, :], i8, row(i1), ALU.is_equal))
                    then(dve.scalar_tensor_tensor(s2[:, :, :], o1[:, :, :], -2.0, sco[:, :, :], ALU.mult, ALU.add))
                    top(s2, m2, i2, e1, c2)
                    for val, idx, v in ((m1, i1, v1), (m2, i2, v2)):
                        then(dve.tensor_scalar(v[:, :], val[:, :], 0.0, None, ALU.is_gt))
                        then(dve.scalar_tensor_tensor(v[:, :], idx[:, :], 1.0, v[:, :], ALU.add, ALU.mult))
                    then(dve.tensor_tensor(es[:, :], v1[:, :], v2[:, :], ALU.max))
                    then(dve.tensor_scalar(es[:, :], es[:, :], -1.0, None, ALU.add))
                    then(dve.tensor_tensor(oh[:, :, :], i8, row(es), ALU.is_equal))
                    then(dve.memset(pre[:, 0, :], 0.0))
                    for t in range(1, NT):
                        then(dve.tensor_tensor(pre[:, t, :], pre[:, t - 1, :], oh[:, t - 1, :], ALU.add))
                    dve.tensor_tensor(sums[:, :], pre[:, NT - 1, :], oh[:, NT - 1, :], ALU.add).then_inc(oh_ready, 1)
                    then(dve.tensor_tensor(tmp[:, :, :], sco[:, :, :], oh[:, :, :], ALU.mult))
                    then(dve.tensor_reduce(wt[:, :], tmp[:, :, :], AX.X, ALU.add))
                    for t in range(NT):
                        then(dve.tensor_scalar(xn[:, t, :], xn[:, t, :], wt[:, t:t + 1], None, ALU.mult))
                    then(dve.tensor_copy(xh[:, :, :], xn[:, :, :]))
                    then(dve.tensor_tensor(xl[:, :, :], xn[:, :, :], xh[:, :, :].bitcast(F32), ALU.subtract))
                    dve.wait_ge(rank_made, 1)
                    for j in range(4):
                        then(dve.tensor_scalar(nt4[:, :, j], ps[:, 1024:1024 + E], float(P * j), None, ALU.is_gt))
                    for c in cum:
                        then(dve.memset(c[:, :], 0.0))
                    then(dve.tensor_reduce(cum[0][:, E:2 * E], nt4[:, :, :], AX.X, ALU.add))
                    for i in range(3):
                        then(dve.tensor_tensor(cum[i + 1][:, E:2 * E], cum[i][:, E:2 * E],
                                               cum[i][:, E - 2 ** i:2 * E - 2 ** i], ALU.add))
                    base = cum[3][:, E - 1:2 * E - 1].unsqueeze(1).broadcast_to([P, NT, E])
                    then(dve.tensor_scalar(rk[:, :, :], ps[:, 512:512 + NT * E].rearrange("p (t e) -> p t e", e=E),
                                           1.0, None, ALU.add))
                    then(dve.scalar_tensor_tensor(tmp[:, :, :], base, float(P), rk[:, :, :], ALU.mult, ALU.add))
                    then(dve.tensor_tensor(tmp[:, :, :], tmp[:, :, :], oh[:, :, :], ALU.mult))
                    then(dve.tensor_reduce(pos[:, :], tmp[:, :, :], AX.X, ALU.add))
                    then(dve.tensor_scalar(pos[:, :], pos[:, :], -1.0, None, ALU.add))
                    incl = cum[3][:, E:2 * E].unsqueeze(1).broadcast_to([P, TILES, E])
                    then(dve.tensor_tensor(cmp[:, :, :], incl, iotaT[:, :].unsqueeze(2).broadcast_to([P, TILES, E]),
                                           ALU.is_le))
                    then(dve.tensor_reduce(tabf[:, 0:TILES], cmp[:, :, :], AX.X, ALU.add))
                    then(dve.tensor_scalar(tabf[:, 0:TILES], tabf[:, 0:TILES], float(E - 1), None, ALU.min))
                    then(dve.tensor_scalar(tabf[:, TILES:TILES + 1], cum[3][:, 2 * E - 1:2 * E], 2.0, None, ALU.max))
                    then(dve.tensor_copy(table[:, :], tabf[0:1, :]))

        with ExitStack() as ec:
            def eb(name, shape, dt=F32):
                return ec.enter_context(nc.sbuf_tensor(name, shape, dt))

            def esem(name):
                return ec.enter_context(nc.semaphore(name))

            perm = eb("perm", [P, NT, P], F32R)
            permT = [eb(f"permT{i}", [P, NT, P], F32R) for i in range(1)]
            xg = eb("xg", [P, NC, P])
            hs = [eb(f"hs{i}", [P, 512]) for i in range(2)]
            hT = eb("hT", [P, HID // P, P])
            y, yh, yl = eb("y", [P, C]), eb("yh", [P, C], F32R), eb("yl", [P, C], F32R)
            w1_in = [esem(f"w1_in{i}") for i in range(HC)]
            w2_in = [esem(f"w2_in{i}") for i in range(HC)]
            b1_in, b2_in = esem("b1_in"), esem("b2_in")
            (pos_down, perm_done, xg_made, xg_kept, pt_made, pt_kept, h_made, h_kept, ht_made, ht_kept, w2_used,
             y_done, yh_done, yl_done, sc_made, sc_added) = \
                [esem(n) for n in ("pos_down", "perm_done", "xg_made", "xg_kept", "pt_made", "pt_kept", "h_made",
                                   "h_kept", "ht_made", "ht_kept", "w2_used", "y_done", "yh_done", "yl_done",
                                   "sc_made", "sc_added")]
            w1_d = d["w1"].rearrange("e (k p) h -> e p k h", p=P)
            w2_d = d["w2"].rearrange("e (j p) n -> e p j n", p=P)

            with nc.Block() as block:

                def tiles(eng):
                    return eng.value_load(table[0:1, TILES:TILES + 1], min_val=2, max_val=TILES)

                @block.sync
                def _(sp):
                    def load(at, free):
                        e = sp.value_load(table[0:1, at], min_val=0, max_val=E - 1)
                        for i in range(HC):
                            if free is not None:
                                sp.wait_ge(h_made, free * HC + i + 1)
                            sp.dma_start(w1[i][:, :, :],
                                         w1_d[bass.ds(e, 1), :, :, i * 512:i * 512 + 512].squeeze(0)).then_inc(w1_in[i], 16)
                            if i == 0:
                                if free is not None:
                                    sp.wait_ge(ht_kept, free * HC + HC)
                                sp.dma_start(b1[:, :], d["b1c"][bass.ds(e, 1), :, :].squeeze(0)).then_inc(b1_in, 16)
                        if free is not None:
                            sp.wait_ge(y_done, free + 1)
                        sp.dma_start(b2[:, :], d["b2"][bass.ds(e, 1), :].broadcast_to([P, C])).then_inc(b2_in, 16)
                        for i in range(HC):
                            if free is not None:
                                sp.wait_ge(w2_used, free * HC + i + 1)
                            sp.dma_start(w2[i][:, :, :],
                                         w2_d[bass.ds(e, 1), :, 4 * i:4 * i + 4, :].squeeze(0)).then_inc(w2_in[i], 16)

                    load(slice(0, 1), None)
                    with sp.Fori(0, tiles(sp) - 1) as it:
                        load(bass.ds(it + 1, 1), it)

                @block.tensor
                def _(pe):
                    def gather(it):
                        pe.wait_ge(perm_done, it * NT + NT)
                        for k in range(NC):
                            for t in range(NT):
                                for i, part in enumerate((xh, xl)):
                                    last = pe.matmul(ps[:, 5 * 512 + k * P:5 * 512 + k * P + P],
                                                     part[:, t, k * P:k * P + P], perm[:, t, :],
                                                     start=(t == 0 and i == 0), stop=(t == NT - 1 and i == 1))
                        last.then_inc(xg_made, 1)

                    def turn(it):
                        for t in range(NT):
                            last = pe.transpose(ps[:, 6 * 512 + t * P:6 * 512 + t * P + P],
                                                perm[:, t, :].bitcast(F32), s.ident[:, :])
                        last.then_inc(pt_made, 1)

                    def scatter(it):
                        pe.wait_ge(yl_done, it + 1)
                        for t in range(NT):
                            for i, part in enumerate((yh, yl)):
                                last = pe.matmul(bank(ps, 4 + t), permT[0][:, t, :], part[:, :],
                                                 start=(i == 0), stop=(i == 1))
                            last.then_inc(sc_made, 1)

                    gather(0)
                    with pe.Fori(0, tiles(pe)) as it:
                        pe.wait_ge(xg_kept, it + 1)
                        turn(it)

                        def turn_h(i):
                            pe.wait_ge(h_kept, it * HC + i + 1)
                            for q in range(4):
                                last = pe.transpose(ps[:, (2 + i % 2) * 512 + q * P:(2 + i % 2) * 512 + q * P + P],
                                                    hs[i % 2][:, q * P:q * P + P], s.ident[:, :])
                            last.then_inc(ht_made, 1)

                        for i in range(HC):
                            pe.wait_ge(w1_in[i], it * 16 + 16)
                            if i >= 2:
                                pe.wait_ge(h_kept, it * HC + i - 1)
                            for k in range(NC):
                                last = pe.matmul(bank(ps, i % 2), xg[:, k, :], w1[i][:, k, :],
                                                 start=(k == 0), stop=(k == NC - 1))
                            last.then_inc(h_made, 1)
                            if i:
                                if i - 1 >= 2:
                                    pe.wait_ge(ht_kept, it * HC + i - 2)
                                turn_h(i - 1)
                        gather(it + 1)
                        pe.wait_ge(ht_kept, it * HC + HC - 2)
                        turn_h(HC - 1)
                        for i in range(HC):
                            pe.wait_ge(ht_kept, it * HC + i + 1)
                            pe.wait_ge(w2_in[i], it * 16 + 16)
                            for q in range(4):
                                j = 4 * i + q
                                last = pe.matmul(bank(ps, 4), hT[:, j, :], w2[i][:, q, :],
                                                 start=(j == 0), stop=(j == HID // P - 1))
                            last.then_inc(w2_used, 1)
                        pe.wait_ge(pt_kept, it + 1)
                        pe.wait_ge(xg_kept, it + 2)
                        scatter(it)
                        pe.wait_ge(sc_added, it * NT + NT)

                @block.vector
                def _(dve):
                    def place(it):
                        for t in range(NT):
                            dve.tensor_scalar(perm[:, t, :], iota[:, :], pos[:, t:t + 1], None, ALU.is_equal)\
                               .then_inc(perm_done, 1)

                    def keep(it):
                        dve.wait_ge(xg_made, it + 1)
                        dve.tensor_copy(xg[:, :, :], bank(ps, 5).rearrange("p (k n) -> p k n", n=P))\
                           .then_inc(xg_kept, 1)

                    place(0)
                    keep(0)
                    with dve.Fori(0, tiles(dve)) as it:
                        dve.wait_ge(pt_made, it + 1)
                        dve.tensor_copy(permT[0][:, :, :], bank(ps, 6).rearrange("p (t n) -> p t n", n=P))\
                           .then_inc(pt_kept, 1)
                        dve.tensor_scalar(pos[:, :], pos[:, :], -float(P), None, ALU.add).then_inc(pos_down, 1)
                        dve.wait_ge(pos_down, it + 1)
                        place(it + 1)
                        dve.wait_ge(h_made, it * HC + HC)
                        keep(it + 1)
                        dve.wait_ge(w2_used, it * HC + HC)
                        dve.wait_ge(b2_in, it * 16 + 16)
                        dve.tensor_tensor(y[:, :], bank(ps, 4), b2[:, :], ALU.add).then_inc(y_done, 1)
                        dve.wait_ge(y_done, it + 1)
                        dve.tensor_copy(yh[:, :], y[:, :]).then_inc(yh_done, 1)
                        dve.wait_ge(yh_done, it + 1)
                        dve.tensor_tensor(yl[:, :], y[:, :], yh[:, :].bitcast(F32), ALU.subtract).then_inc(yl_done, 1)
                        for t in range(NT):
                            dve.wait_ge(sc_made, it * NT + t + 1)
                            dve.tensor_tensor(x[:, t, :], x[:, t, :], bank(ps, 4 + t), ALU.add).then_inc(sc_added, 1)

                @block.scalar
                def _(act):
                    with act.Fori(0, tiles(act)) as it:
                        def relus(i):
                            act.wait_ge(ht_made, it * HC + i + 1)
                            for q in range(4):
                                j = 4 * i + q
                                last = act.activation(hT[:, j, :],
                                                      ps[:, (2 + i % 2) * 512 + q * P:(2 + i % 2) * 512 + q * P + P],
                                                      ACT.Relu, bias=b1[:, j:j + 1])
                            last.then_inc(ht_kept, 1)

                        act.wait_ge(b1_in, it * 16 + 16)
                        for i in range(HC):
                            act.wait_ge(h_made, it * HC + i + 1)
                            act.copy(hs[i % 2][:, :], bank(ps, i % 2)).then_inc(h_kept, 1)
                            if i:
                                relus(i - 1)
                        relus(HC - 1)


STOP = 3
DEN_MIN, DEN_MAX, SUM_MAX = 1e-6, 1e20, 1e37


def layer(nc, d, out):
    s = Stage()
    s.nc = nc
    with ExitStack() as ctx:
        def sb(name, shape, dt=F32):
            return ctx.enter_context(nc.sbuf_tensor(name, shape, dt))

        s.ps = ctx.enter_context(nc.psum_tensor("psum", [P, 4096], F32))
        s.ident = sb("ident", [P, P])
        s.cols = sb("cols", [P, 12])
        s.bq, s.bk, s.bv = s.cols[:, 0:4], s.cols[:, 4:8], s.cols[:, 8:12]
        s.eps = sb("eps", [P, 1])
        s.ones = sb("ones", [P, P])
        x1 = sb("x1", [P, NT, C])
        bad = sb("bad", [P, 1], I32)
        d["qT_d"] = nc.dram_tensor("qT_d", (C, T), F32).ap()
        with nc.sbuf_tensor("o_acc", [P, G, T], F32) as oacc:
            cross_attention(s, d, oacc, bad)
            is_bad = nc.values_load(bad[0:1, 0:1], min_val=0, max_val=1)
            with nc.If(is_bad > 0):
                general_cross(s, d, oacc)
            cross_output(s, d, oacc, x1)
        if STOP > 1:
            self_attention(s, d, x1, x1)
        if STOP > 2:
            feed_forward(s, d, x1, x1)
        done = ctx.enter_context(nc.semaphore("out_done"))
        with nc.Block() as block:

            @block.sync
            def _(sp):
                sp.dma_start(out.rearrange("(t p) c -> p t c", p=P), x1[:, :, :]).then_inc(done, 16)
                sp.wait_ge(done, 16)


def kernel(**inputs):
    import concourse.bacc as bacc
    from concourse.bass_utils import run_bass_kernel_spmd

    f = lambda n: np.asarray(inputs[n])
    col = lambda a: np.ascontiguousarray(a.reshape(-1, P).T)
    arrays = {
        "x": f("x").reshape(T, C),
        "ctxT": np.ascontiguousarray(f("ctx_768").reshape(N, CK).T),
        "Wq": f("L0_xattn_Wq"), "Wk": f("L0_xattn_Wk"), "Wv": f("L0_xattn_Wv"), "Wo": f("L0_xattn_Wo"),
        "cols": np.ascontiguousarray(np.concatenate([col(f("L0_xattn_b" + n)) for n in "qkv"], axis=1)),
        "bo": f("L0_xattn_bo"),
        "ident": np.eye(P, dtype=np.float32),
        "gate_w": f("L0_ffn_gate_w"), "gate_b": f("L0_ffn_gate_b"),
        "w1": f("L0_ffn_w1"), "w2": f("L0_ffn_w2"), "b2": f("L0_ffn_b2"),
        "b1c": np.ascontiguousarray(f("L0_ffn_b1").reshape(8, -1, P).transpose(0, 2, 1)),
        "tri": np.triu(np.ones((P, P), np.float32), 1),
        "iota": np.arange(P, dtype=np.float32),
    }
    for n in "qkvo":
        arrays[f"W{n}T_s"] = np.ascontiguousarray(f(f"L0_attn_W{n}").T)
    dist = np.arange(P)[:, None] + (T - P) - np.arange(T)[None, :]
    arrays["strip"] = np.where(dist >= 0, -dist, NEG).astype(np.float32)
    nc = bacc.Bacc("TRN2", target_bir_lowering=False, num_devices=1)
    d = {n: nc.dram_tensor("in_" + n, a.shape, mybir.dt.from_np(a.dtype), kind="ExternalInput").ap()
         for n, a in arrays.items()}
    out = nc.dram_tensor("out", (T, C), F32, kind="ExternalOutput").ap()
    layer(nc, d, out)
    r = run_bass_kernel_spmd(nc, [{"in_" + n: a for n, a in arrays.items()}], core_ids=[0])
    return r.results[0]["out"].reshape(1, T, C)
```

```python
import numpy as np
import concourse.bass as bass
from concourse import mybir
from contextlib import ExitStack

F32 = mybir.dt.float32
F32R = mybir.dt.float32r
I32 = mybir.dt.int32
ALU = mybir.AluOpType
ACT = mybir.ActivationFunctionType
AX = mybir.AxisListType

P = 128
T, C, CK = 512, 512, 384
N = 8192
H, D = 16, 32
NT = T // P
NC = C // P
NK = CK // P
G, HG = NC, P // D
EPS = 1e-5

KB = 512
NB = N // KB
CB = KB // P
U = G * CB


def bank(ps, i, n=512):
    return ps[:, i * 512:i * 512 + n]


class Stage:
    pass


def layer_norm(s, tag, src, dst):
    nc, ctx = s.nc, ExitStack()
    with ctx:
        stats = ctx.enter_context(nc.sbuf_tensor(f"{tag}_stats", [P, NT, 6], F32))
        mv = ctx.enter_context(nc.sbuf_tensor(f"{tag}_mv", [P, NT, 2], F32))
        std = ctx.enter_context(nc.sbuf_tensor(f"{tag}_std", [P, NT], F32))
        rstd = ctx.enter_context(nc.sbuf_tensor(f"{tag}_rstd", [P, NT], F32))
        stats_done = ctx.enter_context(nc.semaphore(f"{tag}_stats_done"))
        mv_done = ctx.enter_context(nc.semaphore(f"{tag}_mv_done"))
        std_done = ctx.enter_context(nc.semaphore(f"{tag}_std_done"))
        rstd_done = ctx.enter_context(nc.semaphore(f"{tag}_rstd_done"))
        with nc.Block() as block:

            @block.vector
            def _(dve):
                for t in range(NT):
                    dve.bn_stats(stats[:, t, :], src[:, t, :]).then_inc(stats_done, 1)
                for t in range(NT):
                    dve.wait_ge(stats_done, t + 1)
                    dve.bn_aggr(mv[:, t, :], stats[:, t, :]).then_inc(mv_done, 1)
                dve.wait_ge(std_done, 1)
                dve.reciprocal(rstd[:, :], std[:, :]).then_inc(rstd_done, 1)
                dve.wait_ge(rstd_done, 1)
                for t in range(NT):
                    dve.tensor_scalar(dst[:, t, :], src[:, t, :], mv[:, t, 0:1], rstd[:, t:t + 1],
                                      ALU.subtract, ALU.mult)

            @block.scalar
            def _(act):
                act.wait_ge(mv_done, NT)
                act.activation(std[:, :], mv[:, :, 1], ACT.Sqrt, bias=s.eps[:, 0:1]).then_inc(std_done, 1)


def transpose_tokens(s, tag, src, dst):
    nc, ps = s.nc, s.ps
    with ExitStack() as ctx:
        turned = ctx.enter_context(nc.semaphore(f"{tag}_turned"))
        with nc.Block() as block:

            @block.tensor
            def _(pe):
                for k in range(NC):
                    for t in range(NT):
                        last = pe.transpose(ps[:, k * 512 + t * P:k * 512 + t * P + P],
                                            src[:, t, k * P:k * P + P], s.ident[:, :])
                    last.then_inc(turned, 1)

            @block.vector
            def _(dve):
                for k in range(0, NC, 2):
                    dve.wait_ge(turned, k + 1)
                    dve.tensor_copy(dst[:, k, :], bank(ps, k))

            @block.scalar
            def _(act):
                for k in range(1, NC, 2):
                    act.wait_ge(turned, k + 1)
                    act.copy(dst[:, k, :], bank(ps, k))


def cross_attention(s, d, oacc, bad):
    nc, ps = s.nc, s.ps
    outer = ExitStack()
    with outer:
        def sb(ctx, name, shape, dt=F32):
            return ctx.enter_context(nc.sbuf_tensor(name, shape, dt))

        def sem(ctx, name):
            return ctx.enter_context(nc.semaphore(name))

        qs = sb(outer, "q_stack", [P, H, T], F32R)
        wk = [sb(outer, f"wk_{x}", [P, NK, C], F32R) for x in "hl"]
        wv = [sb(outer, f"wv_{x}", [P, NK, C], F32R) for x in "hl"]
        craw = sb(outer, "ctx_raw", [P, NK, KB])
        dacc = sb(outer, "den_acc", [P, G, HG, T])
        ctxT = d["ctxT"].rearrange("(k p) n -> p k n", p=P)

        with ExitStack() as ctx:
            x = sb(ctx, "x_in", [P, NT, C])
            xn = sb(ctx, "xn1", [P, NT, C])
            xnT = sb(ctx, "xnT1", [P, NC, T])
            wq = sb(ctx, "wq", [P, NC, C])
            wraw = sb(ctx, "w_raw", [P, 2, NK, C])
            qf = sb(ctx, "qf", [P, G, T])
            qh = sb(ctx, "qh", [P, G, T], F32R)
            ql = sb(ctx, "ql", [P, G, T], F32R)
            loaded = sem(ctx, "q_loaded")
            split_h = sem(ctx, "w_split_h")
            split_l = sem(ctx, "w_split_l")
            with nc.Block() as block:

                @block.sync
                def _(sp):
                    sp.dma_start(x[:, :, :], d["x"].rearrange("(t p) c -> p t c", p=P)).then_inc(loaded, 16)
                    sp.dma_start(s.ident[:, :], d["ident"]).then_inc(loaded, 16)
                    sp.dma_start(s.cols[:, :], d["cols"]).then_inc(loaded, 16)
                    sp.dma_start(wraw[:, 0], d["Wk"].rearrange("(k p) n -> p k n", p=P)).then_inc(loaded, 16)
                    sp.dma_start(wraw[:, 1], d["Wv"].rearrange("(k p) n -> p k n", p=P)).then_inc(loaded, 16)
                    sp.dma_start(wq[:, :, :], d["Wq"].rearrange("(k p) n -> p k n", p=P)).then_inc(loaded, 16)
                    sp.dma_start(craw[:, :, :], ctxT[:, :, 0:KB]).then_inc(loaded, 16)
                    sp.wait_ge(loaded, 112)

                @block.gpsimd
                def _(pool):
                    pool.memset(s.eps[:, :], EPS)
                    pool.memset(s.ones[:, :], 1.0)

            layer_norm(s, "ln1", x, xn)
            transpose_tokens(s, "ln1", xn, xnT)
            q_done = sem(ctx, "q_done")
            q_copied = sem(ctx, "q_copied")
            q_split = sem(ctx, "q_split")
            stacked = sem(ctx, "q_stacked")
            with nc.Block() as block:

                @block.tensor
                def _(pe):
                    for g in range(G):
                        for k in range(NC):
                            last = pe.matmul(bank(ps, g), wq[:, k, g * P:g * P + P], xnT[:, k, :],
                                             start=(k == 0), stop=(k == NC - 1))
                        last.then_inc(q_done, 1)

                @block.vector
                def _(dve):
                    for g in range(G):
                        dve.wait_ge(q_done, g + 1)
                        dve.tensor_scalar(qf[:, g, :], bank(ps, g), s.bq[:, g:g + 1], float(D) ** -0.5,
                                          ALU.add, ALU.mult).then_inc(q_copied, 1)
                        dve.wait_ge(q_copied, 2 * g + 1)
                        dve.tensor_copy(qh[:, g, :], qf[:, g, :]).then_inc(q_copied, 1)
                        dve.wait_ge(q_copied, 2 * g + 2)
                        dve.tensor_tensor(ql[:, g, :], qf[:, g, :], qh[:, g, :].bitcast(F32),
                                          ALU.subtract).then_inc(q_split, 1)

                @block.scalar
                def _(act):
                    for i, w in enumerate((wk, wv)):
                        act.copy(w[0][:, :, :], wraw[:, i]).then_inc(split_h, 1)

                @block.gpsimd
                def _(pool):
                    for i, w in enumerate((wk, wv)):
                        pool.wait_ge(split_h, i + 1)
                        pool.tensor_tensor(w[1][:, :, :], wraw[:, i], w[0][:, :, :].bitcast(F32), ALU.subtract)

                @block.sync
                def _(sp):
                    for g in range(G):
                        sp.wait_ge(q_split, g + 1)
                        for j in range(HG):
                            for half, part in enumerate((qh, ql)):
                                src = part[D * j:D * j + D, g:g + 1, :].bitcast(F32).broadcast_to([D, 2, T])
                                sp.dma_start(qs[64 * half:64 * half + 64, g * HG + j, :].bitcast(F32), src)\
                                  .then_inc(stacked, 16)
                    sp.dma_start(d["qT_d"].rearrange("(g p) n -> p g n", p=P), qf[:, :, :]).then_inc(stacked, 16)
                    sp.wait_ge(stacked, 16 * 2 * H + 16)

        with ExitStack() as ctx:
            ks = sb(ctx, "k_stack", [P, G, HG, KB], F32R)
            khl = [sb(ctx, f"k_split{i}", [P, 2, KB], F32R) for i in range(2)]
            vb = [sb(ctx, f"v{i}", [P, CB, C]) for i in range(2)]
            ch = [sb(ctx, f"ctx_h{i}", [P, NK, KB], F32R) for i in range(2)]
            cl = [sb(ctx, f"ctx_l{i}", [P, NK, KB], F32R) for i in range(2)]
            pr = [sb(ctx, f"probs{i}", [P, HG, T]) for i in range(2)]
            ND = 3

            names = ("ctx_loaded", "ch_done", "cl_done", "v_made", "k_made", "v_kept", "kh_kept", "kl_kept",
                     "sa_ready", "sb_ready", "ea_done", "eb_done", "pv_done", "o_kept", "den_dve", "den_pool", "o_cleared")
            (ctx_loaded, ch_done, cl_done, v_made, k_made, v_kept, kh_kept, kl_kept,
             sa_ready, sb_ready, ea_done, eb_done, pv_done, o_kept, den_dve, den_pool, o_cleared) = \
                [sem(ctx, n) for n in names]
            k_stacked = [sem(ctx, f"k_stacked{g}") for g in range(G)]
            SD = 16 * 2 * HG

            def sbank(j):
                return bank(ps, j)

            with nc.Block() as block:

                def ctx_low(pool, b, par, k):
                    pool.wait_ge(ch_done, b * NK + k + 1)
                    pool.tensor_tensor(cl[par][:, k, :], craw[:, k, :], ch[par][:, k, :].bitcast(F32),
                                       ALU.subtract).then_inc(cl_done, 1)

                @block.sync
                def _(sp):
                    def stack(b, g):
                        sp.wait_ge(kl_kept, b * G + g + 1)
                        for j in range(HG):
                            for half in range(2):
                                sp.dma_start(ks[64 * half:64 * half + 64, g, j, :].bitcast(F32),
                                             khl[g % 2][D * j:D * j + D, :, :].bitcast(F32)).then_inc(k_stacked[g], 16)

                    def load(b):
                        sp.wait_ge(cl_done, b * NK)
                        src = ctxT[:, :, bass.ds(b * KB, KB)]
                        sp.dma_start(craw[:, :, :], src).then_inc(ctx_loaded, 16)

                    load(1)
                    for g in range(G):
                        stack(0, g)

                    def blocks(it, last=False, first=False):
                        for par in range(2):
                            b = it * 2 + par
                            if not (first and par == 0):
                                stack(b, G - 1)
                            if not last:
                                load(b + 2)
                            if not (last and par == 1):
                                for g in range(G - 1):
                                    stack(b + 1, g)

                    blocks(0, first=True)
                    with sp.Fori(1, NB // 2 - 1) as it:
                        blocks(it)
                    blocks(NB // 2 - 1, last=True)

                @block.gpsimd
                def _(pool):
                    pool.memset(dacc[:, :, ND:, :], 0.0).then_inc(den_pool, 1)
                    for b in range(2):
                        for k in range(NK):
                            ctx_low(pool, b, b, k)

                    def blocks(it, last=False):
                        for par in range(2):
                            b = it * 2 + par
                            for i in range(U):
                                g = i // CB
                                n = b * U + i
                                pool.wait_ge(eb_done, n + 1)
                                pool.wait_ge(den_pool, n + 1)
                                pool.tensor_tensor(dacc[:, g, ND:, :], dacc[:, g, ND:, :], pr[i % 2][:, ND:, :],
                                                   ALU.add).then_inc(den_pool, 1)
                                if i in (6, 10, 14) and not last:
                                    ctx_low(pool, b + 2, par, i // 4 - 1)

                    blocks(0)
                    with pool.Fori(1, NB // 2 - 1) as it:
                        blocks(it)
                    blocks(NB // 2 - 1, last=True)

                @block.tensor
                def _(pe):
                    def product(b, par, kind, g, lo, hi):
                        if lo == 0:
                            if g == 0 and kind == "v":
                                pe.wait_ge(cl_done, b * NK + NK)
                            if kind == "v":
                                if isinstance(b, int) and b * CB + g == 0:
                                    pass
                                else:
                                    pe.wait_ge(v_kept, b * CB + g)
                            else:
                                if isinstance(b, int) and b * G + g == 0:
                                    pass
                                else:
                                    pe.wait_ge(kl_kept, b * G + g)
                        for m in range(lo, hi):
                            k, which = m // 3, m % 3
                            c = (ch, ch, cl)[which][par]
                            w = (wv if kind == "v" else wk)[(0, 1, 0)[which]]
                            cols = slice(g * P, g * P + P)
                            if kind == "v":
                                last = pe.matmul(bank(ps, 6), c[:, k, cols], w[:, k, :],
                                                 start=(m == 0), stop=(m == 8))
                            else:
                                last = pe.matmul(bank(ps, 7), w[:, k, cols], c[:, k, :],
                                                 start=(m == 0), stop=(m == 8))
                        if hi == 9:
                            last.then_inc(v_made if kind == "v" else k_made, 1)

                    def scores(b, i, pair, any_before=True):
                        g, c = i // CB, i % CB
                        if any_before:
                            pe.wait_ge((ea_done, eb_done)[pair], b * U + i)
                        if c == 0 and pair == 0:
                            pe.wait_ge(k_stacked[g], b * SD + SD)
                        for j in (2 * pair, 2 * pair + 1):
                            last = pe.matmul(sbank(j), ks[:, g, j, c * P:c * P + P], qs[:, g * HG + j, :],
                                             start=True, stop=True)
                        last.then_inc((sa_ready, sb_ready)[pair], 1)

                    for g in range(G):
                        product(0, 0, "v", g, 0, 9)
                        product(0, 0, "k", g, 0, 9)
                    scores(0, 0, 0, False)
                    scores(0, 0, 1, False)

                    def blocks(it, first=False, last=False):
                        for par in range(2):
                            b = it * 2 + par
                            end = last and par == 1
                            for i in range(U):
                                g, c = i // CB, i % CB
                                nxt = (b, i + 1) if i < U - 1 else (b + 1, 0)
                                if not (end and i == U - 1):
                                    scores(*nxt, 0)
                                if not end:
                                    kind = "v" if c < 2 else "k"
                                    lo, hi = ((0, 5), (5, 9))[c % 2]
                                    product(b + 1, 1 - par, kind, g, lo, hi)
                                if not (end and i == U - 1):
                                    scores(*nxt, 1)
                                else:
                                    pe.wait_ge(eb_done, b * U + i + 1)
                                if i == 0:
                                    pe.wait_ge(v_kept, b * CB + CB)
                                if c == 0 and not (first and par == 0 and g < 2):
                                    pe.wait_ge(o_kept, b * G + g - 1)
                                for j in range(HG):
                                    hd = (g * HG + j) * D
                                    last_mm = pe.matmul(ps[D * j:D * j + D, (4 + g % 2) * 512:(5 + g % 2) * 512],
                                                        vb[par][:, c, hd:hd + D], pr[i % 2][:, j, :],
                                                        start=(c == 0), stop=(c == CB - 1),
                                                        tile_position=(0, D * j))
                                last_mm.then_inc(pv_done, 1)

                    blocks(0, first=True)
                    with pe.Fori(1, NB // 2 - 1) as it:
                        blocks(it)
                    blocks(NB // 2 - 1, last=True)

                @block.scalar
                def _(act):
                    def keep_v(b, par, g, wait_free):
                        act.wait_ge(v_made, b * CB + g + 1)
                        if wait_free and g == 0:
                            act.wait_ge(pv_done, b * U - U)
                        act.copy(vb[par][:, g, :], bank(ps, 6)).then_inc(v_kept, 1)

                    def keep_kh(b, g, prev_stack):
                        act.wait_ge(k_made, b * G + g + 1)
                        if prev_stack is not None:
                            act.wait_ge(k_stacked[(g + 2) % G], prev_stack)
                        act.activation(khl[g % 2][:, 0, :], bank(ps, 7), ACT.Identity,
                                       bias=s.bk[:, g:g + 1]).then_inc(kh_kept, 1)

                    def exps(b, i, pair, wait_free=True):
                        n = b * U + i
                        act.wait_ge((sa_ready, sb_ready)[pair], n + 1)
                        if wait_free:
                            if pair == 0:
                                act.wait_ge(pv_done, n - 1)
                                act.wait_ge(den_dve, n)
                            else:
                                act.wait_ge(den_pool, n)
                        act.activation(pr[i % 2][:, 2 * pair:2 * pair + 2, :], ps[:, pair * 1024:pair * 1024 + 1024],
                                       ACT.Exp).then_inc((ea_done, eb_done)[pair], 1)

                    def ctx_high(b, par, k):
                        act.copy(ch[par][:, k, :], craw[:, k, :]).then_inc(ch_done, 1)

                    for b in range(2):
                        if b:
                            act.wait_ge(ctx_loaded, 16)
                        for k in range(NK):
                            ctx_high(b, b, k)
                    for g in range(G):
                        keep_v(0, 0, g, False)
                        keep_kh(0, g, SD if g >= 2 else None)

                    def blocks(it, first=False, last=False):
                        for par in range(2):
                            b = it * 2 + par
                            end = last and par == 1
                            for i in range(U):
                                g, c = i // CB, i % CB
                                free = not (first and par == 0 and i < 2)
                                exps(b, i, 0, free)
                                if i in (5, 9, 13) and not last:
                                    if i == 5:
                                        act.wait_ge(ctx_loaded, b * 16 + 32)
                                        act.wait_ge(k_made, b * G + G)
                                    ctx_high(b + 2, par, i // 4 - 1)
                                if c == 2 and not end:
                                    keep_v(b + 1, 1 - par, g, not (first and par == 0))
                                if c == 0:
                                    if i == 0:
                                        if not (first and par == 0):
                                            keep_kh(b, G - 1, b * SD + SD)
                                    elif not end:
                                        q = g - 1
                                        keep_kh(b + 1, q, b * SD + (2 * SD if q >= 2 else SD))
                                exps(b, i, 1, free)

                    blocks(0, first=True)
                    with act.Fori(1, NB // 2 - 1) as it:
                        blocks(it)
                    blocks(NB // 2 - 1, last=True)

                @block.vector
                def _(dve):
                    def keep_kl(b, g):
                        dve.wait_ge(kh_kept, b * G + g + 1)
                        dve.scalar_tensor_tensor(khl[g % 2][:, 1, :], bank(ps, 7), s.bk[:, g:g + 1],
                                                 khl[g % 2][:, 0, :].bitcast(F32), ALU.add,
                                                 ALU.subtract).then_inc(kl_kept, 1)

                    def keep_o(b, g, n):
                        dve.wait_ge(pv_done, n)
                        dve.tensor_tensor(oacc[:, g, :], oacc[:, g, :], bank(ps, 4 + g % 2),
                                          ALU.add).then_inc(o_kept, 1)

                    dve.memset(oacc[:, :, :], 0.0).then_inc(o_cleared, 1)
                    dve.memset(dacc[:, :, 0:ND, :], 0.0).then_inc(den_dve, 1)
                    for g in range(G):
                        keep_kl(0, g)
                    dve.wait_ge(o_cleared, 1)

                    def blocks(it, first=False, last=False):
                        for par in range(2):
                            b = it * 2 + par
                            end = last and par == 1
                            for i in range(U):
                                g, c = i // CB, i % CB
                                n = b * U + i
                                if c == 0:
                                    if i == 0:
                                        if not (first and par == 0):
                                            dve.wait_ge(o_kept, b * G - 1)
                                            keep_o(b - 1, G - 1, b * U)
                                            keep_kl(b, G - 1)
                                    else:
                                        if not (first and par == 0 and g == 1):
                                            dve.wait_ge(o_kept, b * G + g - 1)
                                        keep_o(b, g - 1, n)
                                        if not end:
                                            keep_kl(b + 1, g - 1)
                                dve.wait_ge(eb_done, n + 1)
                                dve.wait_ge(den_dve, n + 1)
                                dve.tensor_tensor(dacc[:, g, 0:ND, :], dacc[:, g, 0:ND, :], pr[i % 2][:, 0:ND, :],
                                                  ALU.add).then_inc(den_dve, 1)

                    blocks(0, first=True)
                    with dve.Fori(1, NB // 2 - 1) as it:
                        blocks(it)
                    blocks(NB // 2 - 1, last=True)
                    dve.wait_ge(o_kept, NB * G - 1)
                    keep_o(NB - 1, G - 1, NB * U)

        test_and_divide(s, d, oacc, dacc, bad)


def general_keys_values(s, d, kT_d, v_d, even):
    nc, ps = s.nc, s.ps
    with ExitStack() as ctx:
        def sb(name, shape, dt=F32):
            return ctx.enter_context(nc.sbuf_tensor(name, shape, dt))

        def sem(name):
            return ctx.enter_context(nc.semaphore(name))

        wk, wv = sb("g_wk", [P, NK, C]), sb("g_wv", [P, NK, C])
        cx = sb("g_ctx", [P, NK, KB])
        kb, vb = sb("g_k", [P, G, KB]), sb("g_v", [P, CB, C])
        c_in, k_made, v_made, kv_kept, stored = \
            [sem(n) for n in ("g_c_in", "g_k_made", "g_v_made", "g_kv_kept", "g_stored")]
        ctxT = d["ctxT"].rearrange("(k p) n -> p k n", p=P)
        with nc.Block() as block:

            @block.sync
            def _(sp):
                sp.dma_start(wk[:, :, :], d["Wk"].rearrange("(k p) n -> p k n", p=P)).then_inc(stored, 16)
                sp.dma_start(wv[:, :, :], d["Wv"].rearrange("(k p) n -> p k n", p=P)).then_inc(stored, 16)
                with sp.Fori(0, NB) as b:
                    sp.dma_start(cx[:, :, :], ctxT[:, :, bass.ds(b * KB, KB)]).then_inc(c_in, 16)
                    sp.wait_ge(kv_kept, b * (G + CB) + G + CB)
                    sp.dma_start(kT_d.rearrange("(g p) n -> p g n", p=P)[:, :, bass.ds(b * KB, KB)], kb[:, :, :])\
                      .then_inc(stored, 16)
                    sp.dma_start(v_d.rearrange("(b c p) n -> b p c n", p=P, c=CB)[bass.ds(b, 1)].squeeze(0),
                                 vb[:, :, :]).then_inc(stored, 16)
                sp.wait_ge(stored, NB * 32 + 32)

            @block.tensor
            def _(pe):
                pe.wait_ge(stored, 32)
                with pe.Fori(0, NB) as b:
                    pe.wait_ge(c_in, b * 16 + 16)
                    for g in range(G):
                        for k in range(NK):
                            last = pe.matmul(bank(ps, g), wk[:, k, g * P:g * P + P], cx[:, k, :],
                                             start=(k == 0), stop=(k == NK - 1))
                        last.then_inc(k_made, 1)
                    for c in range(CB):
                        for k in range(NK):
                            last = pe.matmul(bank(ps, 4 + c), cx[:, k, c * P:c * P + P], wv[:, k, :],
                                             start=(k == 0), stop=(k == NK - 1))
                        last.then_inc(v_made, 1)

            @block.gpsimd
            def _(pool):
                pool.memset(even[:, :], 1.0 / N)

            @block.scalar
            def _(act):
                with act.Fori(0, NB) as b:
                    act.wait_ge(stored, b * 32 + 32)
                    for g in range(G):
                        act.wait_ge(k_made, b * G + g + 1)
                        act.activation(kb[:, g, :], bank(ps, g), ACT.Identity, bias=s.bk[:, g:g + 1])\
                           .then_inc(kv_kept, 1)

            @block.vector
            def _(dve):
                with dve.Fori(0, NB) as b:
                    dve.wait_ge(stored, b * 32 + 32)
                    for c in range(CB):
                        dve.wait_ge(v_made, b * CB + c + 1)
                        dve.tensor_copy(vb[:, c, :], bank(ps, 4 + c)).then_inc(kv_kept, 1)


def general_heads(s, d, kT_d, v_d, even, oacc):
    nc, ps = s.nc, s.ps
    o_d, m_d = [nc.dram_tensor(n, (C, T), F32).ap() for n in ("o_d", "mean_d")]
    CLAMP = 10000.0
    NS = N // 512
    with ExitStack() as ctx:
        def sb(name, shape, dt=F32):
            return ctx.enter_context(nc.sbuf_tensor(name, shape, dt))

        def sem(name):
            return ctx.enter_context(nc.semaphore(name))

        q, k, v = sb("g_qh", [D, P]), sb("g_kh", [D, N]), sb("g_vh", [P, N // P, D])
        sc, eq, pT = sb("g_sc", [P, N]), sb("g_eq", [P, N]), sb("g_pT", [P, N // P, P])
        ot, mt = sb("g_ot", [D, P]), sb("g_mt", [D, P])
        own, flag, mx, nmx = sb("g_own", [P, 1]), sb("g_flag", [P, 1]), sb("g_mx", [P, 1]), sb("g_nmx", [P, 1])
        den, rden = sb("g_den", [P, 1]), sb("g_rden", [P, 1])
        mean, om = sb("g_mean", [P, G, T]), sb("g_om", [P, G, T])
        mask = sb("g_mask", [P, G, T], I32)
        (loaded, s_made, s_kept, step, max_done, e_done, p_done, t_made, t_kept, o_made, o_kept, stored, back,
         flag_done, count_made) = \
            [sem("g_" + n) for n in ("loaded", "s_made", "s_kept", "step", "max_done", "e_done", "p_done", "t_made",
                                     "t_kept", "o_made", "o_kept", "out", "back", "flag_done", "count_made")]
        STEPS = 7
        with nc.Block() as block:

            @block.sync
            def _(sp):
                with sp.Fori(0, H) as h:
                    with sp.Fori(0, NT) as t:
                        r = h * NT + t
                        sp.wait_ge(stored, r * 32 + 32)
                        sp.dma_start(q[:, :], d["qT_d"][bass.ds(h * D, D), bass.ds(t * P, P)]).then_inc(loaded, 16)
                        sp.dma_start(k[:, :], kT_d[bass.ds(h * D, D), :]).then_inc(loaded, 16)
                        sp.dma_start(v[:, :, :], v_d.rearrange("(c p) n -> p c n", p=P)[:, :, bass.ds(h * D, D)])\
                          .then_inc(loaded, 16)
                        sp.wait_ge(o_kept, r * 2 + 2)
                        sp.dma_start(o_d[bass.ds(h * D, D), bass.ds(t * P, P)], ot[:, :]).then_inc(stored, 16)
                        sp.dma_start(m_d[bass.ds(h * D, D), bass.ds(t * P, P)], mt[:, :]).then_inc(stored, 16)
                sp.wait_ge(stored, H * NT * 32 + 32)
                sp.dma_start(om[:, :, :], o_d.rearrange("(g p) n -> p g n", p=P)).then_inc(back, 16)
                sp.dma_start(mean[:, :, :], m_d.rearrange("(g p) n -> p g n", p=P)).then_inc(back, 16)

            @block.tensor
            def _(pe):
                with pe.Fori(0, H) as h:
                    with pe.Fori(0, NT) as t:
                        r = h * NT + t
                        pe.wait_ge(loaded, r * 48 + 48)
                        for j in range(NS):
                            if j >= 8:
                                pe.wait_ge(s_kept, r * NS + j - 7)
                            pe.matmul(bank(ps, j % 8), q[:, :], k[:, j * 512:j * 512 + 512], start=True,
                                      stop=True).then_inc(s_made, 1)
                        pe.wait_ge(p_done, r + 1)
                        for j in range(NS):
                            if j >= 8:
                                pe.wait_ge(t_kept, r * NS + j - 7)
                            for i in range(4):
                                c = 4 * j + i
                                last = pe.transpose(ps[:, (j % 8) * 512 + i * P:(j % 8) * 512 + i * P + P],
                                                    sc[:, c * P:c * P + P], s.ident[:, :])
                            last.then_inc(t_made, 1)
                        pe.wait_ge(t_kept, r * NS + NS)
                        for c in range(N // P):
                            last = pe.matmul(ps[0:D, 0:P], v[:, c, :], pT[:, c, :], start=(c == 0),
                                             stop=(c == N // P - 1))
                        last.then_inc(o_made, 1)
                        for c in range(N // P):
                            last = pe.matmul(ps[0:D, 512:512 + P], v[:, c, :], even[:, :], start=(c == 0),
                                             stop=(c == N // P - 1))
                        last.then_inc(o_made, 1)
                pe.wait_ge(flag_done, 1)
                pe.matmul(ps[:, 0:1], s.ones[:, :], flag[:, :], start=True, stop=True).then_inc(count_made, 1)

            @block.gpsimd
            def _(pool):
                pool.memset(mt[:, :], 0.0).then_inc(stored, 32)

            @block.scalar
            def _(act):
                with act.Fori(0, H) as h:
                    with act.Fori(0, NT) as t:
                        r = h * NT + t
                        act.wait_ge(max_done, r + 1)
                        act.activation(sc[:, :], sc[:, :], ACT.Exp, bias=nmx[:, 0:1], accum_out=den[:, 0:1])\
                           .then_inc(e_done, 1)

            @block.vector
            def _(dve):
                dve.memset(flag[:, :], 1.0).then_inc(step, 1)
                with dve.Fori(0, H) as h:
                    with dve.Fori(0, NT) as t:
                        r = h * NT + t
                        for j in range(NS):
                            dve.wait_ge(s_made, r * NS + j + 1)
                            dve.tensor_copy(sc[:, j * 512:j * 512 + 512], bank(ps, j % 8)).then_inc(s_kept, 1)
                        dve.wait_ge(s_kept, r * NS + NS)

                        def then(n, ins):
                            ins.then_inc(step, 1)
                            dve.wait_ge(step, r * STEPS + n + 1)

                        then(1, dve.tensor_tensor(eq[:, :], sc[:, :], sc[:, :], ALU.is_equal))
                        then(2, dve.tensor_reduce(own[:, :], eq[:, :], AX.X, ALU.min))
                        then(3, dve.tensor_tensor(flag[:, :], flag[:, :], own[:, :], ALU.min))
                        then(4, dve.tensor_scalar(sc[:, :], sc[:, :], -CLAMP, CLAMP, ALU.max, ALU.min))
                        then(5, dve.tensor_reduce(mx[:, :], sc[:, :], AX.X, ALU.max))
                        dve.tensor_scalar(nmx[:, :], mx[:, :], -1.0, None, ALU.mult).then_inc(max_done, 1)
                        dve.wait_ge(e_done, r + 1)
                        then(6, dve.reciprocal(rden[:, :], den[:, :]))
                        then(7, dve.tensor_scalar(sc[:, :], sc[:, :], rden[:, 0:1], None, ALU.mult))
                        dve.memset(own[:, :], 0.0).then_inc(p_done, 1)
                        for j in range(NS):
                            dve.wait_ge(t_made, r * NS + j + 1)
                            dve.tensor_copy(pT[:, 4 * j:4 * j + 4, :],
                                            bank(ps, j % 8).rearrange("p (c n) -> p c n", n=P)).then_inc(t_kept, 1)
                        dve.wait_ge(o_made, r * 2 + 2)
                        dve.tensor_copy(ot[:, :], ps[0:D, 0:P]).then_inc(o_kept, 1)
                        dve.tensor_copy(mt[:, :], ps[0:D, 512:512 + P]).then_inc(o_kept, 1)
                dve.memset(own[:, :], 0.0).then_inc(flag_done, 1)
                dve.wait_ge(back, 32)
                dve.tensor_copy(oacc[:, :, :], om[:, :, :]).then_inc(step, 1)
                dve.wait_ge(count_made, 1)
                dve.tensor_scalar(mask[:, :, :], ps[:, 0:1].unsqueeze(2).broadcast_to([P, G, T]), float(P), None,
                                  ALU.is_lt).then_inc(step, 1)
                dve.wait_ge(step, H * NT * STEPS + 3)
                dve.copy_predicated(oacc[:, :, :], mask[:, :, :], mean[:, :, :])


def general_cross(s, d, oacc):
    nc = s.nc
    kT_d, v_d = nc.dram_tensor("kT_d", (C, N), F32).ap(), nc.dram_tensor("v_d", (N, C), F32).ap()
    with nc.sbuf_tensor("g_even", [P, P], F32) as even:
        general_keys_values(s, d, kT_d, v_d, even)
        general_heads(s, d, kT_d, v_d, even, oacc)


def test_and_divide(s, d, oacc, dacc, bad):
    nc, ps = s.nc, s.ps
    with ExitStack() as ctx:
        def sb(name, shape, dt=F32):
            return ctx.enter_context(nc.sbuf_tensor(name, shape, dt))

        def sem(name):
            return ctx.enter_context(nc.semaphore(name))

        rden = sb("rden", [P, G, T])
        low = sb("low", [P, G, T])
        mid = sb("mid", [P, G, T])
        okc = sb("ok_cols", [P, 2 * G])
        okm = sb("ok_min", [P, 1])
        den_made, rec_done, low_done, mid_done, ok_done, min_done, sum_made = \
            [sem(n) for n in ("den_made", "rec_done", "low_done", "mid_done", "ok_done", "min_done", "sum_made")]
        with nc.Block() as block:

            @block.tensor
            def _(pe):
                for g in range(G):
                    for j in range(HG):
                        last = pe.matmul(ps[D * j:D * j + D, g * 512:g * 512 + T], s.ones[:, 0:D],
                                         dacc[:, g, j, :], start=True, stop=True, tile_position=(0, D * j))
                    last.then_inc(den_made, 1)
                pe.wait_ge(min_done, 1)
                pe.matmul(ps[:, 4 * 512:4 * 512 + 1], s.ones[:, :], okm[:, :], start=True,
                          stop=True).then_inc(sum_made, 1)

            @block.gpsimd
            def _(pool):
                for g in range(G):
                    pool.tensor_scalar(mid[:, g, :], oacc[:, g, :], -SUM_MAX, None, ALU.is_ge).then_inc(mid_done, 1)

            @block.vector
            def _(dve):
                for g in range(G):
                    dve.wait_ge(den_made, g + 1)
                    dve.reciprocal(rden[:, g, :], bank(ps, g)).then_inc(rec_done, 1)
                    dve.tensor_scalar(low[:, g, :], bank(ps, g), DEN_MIN, None, ALU.is_ge).then_inc(low_done, 1)
                    dve.wait_ge(low_done, 3 * g + 1)
                    dve.scalar_tensor_tensor(low[:, g, :], bank(ps, g), DEN_MAX, low[:, g, :], ALU.is_le,
                                             ALU.mult).then_inc(low_done, 1)
                    dve.wait_ge(mid_done, g + 1)
                    dve.scalar_tensor_tensor(mid[:, g, :], oacc[:, g, :], SUM_MAX, mid[:, g, :], ALU.is_le,
                                             ALU.mult).then_inc(low_done, 1)
                    dve.wait_ge(low_done, 3 * g + 3)
                    dve.tensor_reduce(okc[:, 2 * g:2 * g + 1], low[:, g, :], AX.X, ALU.min).then_inc(ok_done, 1)
                    dve.tensor_reduce(okc[:, 2 * g + 1:2 * g + 2], mid[:, g, :], AX.X, ALU.min)\
                       .then_inc(ok_done, 1)
                    dve.wait_ge(rec_done, g + 1)
                    dve.tensor_tensor(oacc[:, g, :], oacc[:, g, :], rden[:, g, :], ALU.mult)
                dve.wait_ge(ok_done, 2 * G)
                dve.tensor_reduce(okm[:, :], okc[:, :], AX.X, ALU.min).then_inc(min_done, 1)
                dve.wait_ge(sum_made, 1)
                dve.tensor_scalar(bad[:, :], ps[:, 4 * 512:4 * 512 + 1], float(P), None, ALU.is_lt)


def cross_output(s, d, oacc, x_out):
    nc, ps = s.nc, s.ps
    with ExitStack() as ctx:
        def sb(name, shape, dt=F32):
            return ctx.enter_context(nc.sbuf_tensor(name, shape, dt))

        def sem(name):
            return ctx.enter_context(nc.semaphore(name))

        wo = sb("wo_x", [P, NC, C])
        bo = sb("bo_x", [P, C])
        x = sb("x_again", [P, NT, C])
        loaded, o_ready, y_made, out_sum = [sem(n) for n in ("f_loaded", "o_ready", "y_made", "out_sum")]
        with nc.Block() as block:

            @block.sync
            def _(sp):
                sp.dma_start(wo[:, :, :], d["Wo"].rearrange("(k p) n -> p k n", p=P)).then_inc(loaded, 16)
                sp.dma_start(bo[:, :], d["bo"].partition_broadcast(P)).then_inc(loaded, 16)
                sp.dma_start(x[:, :, :], d["x"].rearrange("(t p) c -> p t c", p=P)).then_inc(loaded, 16)

            @block.tensor
            def _(pe):
                pe.wait_ge(loaded, 48)
                pe.wait_ge(o_ready, G)
                for t in range(NT):
                    for g in range(G):
                        last = pe.matmul(bank(ps, t), oacc[:, g, t * P:t * P + P], wo[:, g, :],
                                         start=(g == 0), stop=(g == G - 1))
                    last.then_inc(y_made, 1)

            @block.vector
            def _(dve):
                for t in range(NT):
                    dve.wait_ge(y_made, t + 1)
                    dve.wait_ge(out_sum, t + 1)
                    dve.tensor_tensor(x_out[:, t, :], x[:, t, :], bank(ps, t), ALU.add)

            @block.scalar
            def _(act):
                for g in range(G):
                    act.activation(oacc[:, g, :], oacc[:, g, :], ACT.Identity, bias=s.bv[:, g:g + 1])\
                       .then_inc(o_ready, 1)

            @block.gpsimd
            def _(pool):
                pool.wait_ge(loaded, 48)
                for t in range(NT):
                    pool.tensor_tensor(x[:, t, :], x[:, t, :], bo[:, :], ALU.add).then_inc(out_sum, 1)


def self_attention(s, d, x, x_out):
    nc, ps = s.nc, s.ps
    with ExitStack() as ctx:
        def sb(name, shape, dt=F32):
            return ctx.enter_context(nc.sbuf_tensor(name, shape, dt))

        def sem(name):
            return ctx.enter_context(nc.semaphore(name))

        wo = sb("wo_s", [P, NC, C])
        strip = sb("strip", [P, T])
        qs = sb("q_stack_s", [P, HG, G, T], F32R)
        ks = sb("k_stack_s", [P, HG, G, T], F32R)
        v = sb("v_s", [P, NT, C])
        qh, ql = sb("qh_s", [P, G, T], F32R), sb("ql_s", [P, G, T], F32R)
        khl = sb("khl_s", [P, 2, G, T], F32R)
        early = ctx.enter_context(ExitStack())

        def eb(name, shape, dt=F32):
            return early.enter_context(nc.sbuf_tensor(name, shape, dt))

        w = [eb(f"w{n}_s", [P, NC, C]) for n in "qkv"] + [wo]
        xn = eb("xn2", [P, NT, C])
        xnT = eb("xnT2", [P, NC, T])
        qf = eb("qf_s", [P, G, T])
        loaded = sem("s_loaded")
        with nc.Block() as block:

            @block.sync
            def _(sp):
                for wt, n in zip(w, "qkvo"):
                    sp.dma_start(wt[:, :, :], d[f"W{n}T_s"].rearrange("(k p) n -> p k n", p=P)).then_inc(loaded, 16)
                sp.dma_start(strip[:, :], d["strip"]).then_inc(loaded, 16)

        layer_norm(s, "ln2", x, xn)
        transpose_tokens(s, "ln2", xn, xnT)

        first = [0, P, 512, 1024]
        width = [P * (t + 1) for t in range(NT)]
        kept = [sum(width[:t]) for t in range(NT)]
        tot = sum(width)
        tfirst = [0, 1024, 512, 512 + 256]
        twidth = [T - P * c for c in range(NT)]
        tkept = [sum(twidth[:c]) for c in range(NT)]

        proj = sem("s_proj")
        q_step, k_step, ql_done, kl_done = [sem(n) for n in ("q_step", "k_step_s", "ql_done", "kl_done_s")]
        v_kept = sem("v_kept_s")
        q_in = [sem(f"q_in{g}") for g in range(G // 2)]
        k_in = [sem(f"k_in{g}") for g in range(G // 2)]
        bias_done, s_made, m_done, nm_done, e_done, r_done, n_done = \
            [sem(n) for n in ("bias_done", "s_made", "m_done", "nm_done", "e_done", "r_done", "n_done")]
        t_made, t_kept_a, t_kept_d, o_made, o_kept, y_made = \
            [sem(n) for n in ("t_made", "t_kept_a", "t_kept_d", "o_made_s", "o_kept_s", "y_made_s")]

        with nc.Block() as block:

            @block.tensor
            def _(pe):
                pe.wait_ge(loaded, 80)
                for g in range(G):
                    for i in range(2):
                        for k in range(NC):
                            last = pe.matmul(bank(ps, 2 * g + i), w[i][:, k, g * P:g * P + P], xnT[:, k, :],
                                             start=(k == 0), stop=(k == NC - 1))
                        last.then_inc(proj, 1)
                for t in range(NT):
                    pe.wait_ge((ql_done, kl_done)[t % 2], t // 2 + 1)
                    for k in range(NC):
                        last = pe.matmul(bank(ps, t), xnT[:, k, t * P:t * P + P], w[2][:, k, :],
                                         start=(k == 0), stop=(k == NC - 1))
                    last.then_inc(proj, 1)

            @block.vector
            def _(dve):
                for g in range(G):
                    dve.wait_ge(proj, 2 * g + 1)
                    dve.tensor_scalar(qf[:, g, :], bank(ps, 2 * g), float(D) ** -0.5, None, ALU.mult)\
                       .then_inc(q_step, 1)
                    dve.wait_ge(q_step, 2 * g + 1)
                    dve.tensor_copy(qh[:, g, :], qf[:, g, :]).then_inc(q_step, 1)
                    dve.wait_ge(q_step, 2 * g + 2)
                    dve.tensor_tensor(ql[:, g, :], qf[:, g, :], qh[:, g, :].bitcast(F32), ALU.subtract)\
                       .then_inc(ql_done, 1)
                    dve.wait_ge(k_step, g + 1)
                    dve.tensor_tensor(khl[:, 1, g, :], bank(ps, 2 * g + 1), khl[:, 0, g, :].bitcast(F32),
                                      ALU.subtract).then_inc(kl_done, 1)

            @block.scalar
            def _(act):
                for g in range(G):
                    act.wait_ge(proj, 2 * g + 2)
                    act.copy(khl[:, 0, g, :], bank(ps, 2 * g + 1)).then_inc(k_step, 1)
                for t in range(NT):
                    act.wait_ge(proj, 2 * G + t + 1)
                    act.copy(v[:, t, :], bank(ps, t)).then_inc(v_kept, 1)

            @block.sync
            def _(sp):
                for g in range(0, G, 2):
                    sp.wait_ge(ql_done, g + 2)
                    for j in range(HG):
                        for half, part in enumerate((qh, ql)):
                            src = part[D * j:D * j + D, g:g + 2, :].bitcast(F32).rearrange("p g t -> p (g t)")
                            sp.dma_start(qs[64 * half:64 * half + 64, j, g:g + 2, :].bitcast(F32)
                                         .rearrange("p g t -> p (g t)"),
                                         src.unsqueeze(1).broadcast_to([D, 2, 2 * T])).then_inc(q_in[g // 2], 16)

            @block.gpsimd
            def _(pool):
                for g in range(0, G, 2):
                    pool.wait_ge(kl_done, g + 2)
                    for j in range(HG):
                        for half in range(2):
                            pool.dma_start(ks[64 * half:64 * half + 64, j, g:g + 2, :].bitcast(F32)
                                           .rearrange("p g t -> p (g t)"),
                                           khl[D * j:D * j + D, :, g:g + 2, :].bitcast(F32)
                                           .rearrange("p s g t -> p s (g t)")).then_inc(k_in[g // 2], 16)

        early.close()
        SR = 4
        sc = [sb(f"scores{i}", [P, tot]) for i in range(SR)]
        pT = [sb(f"probsT{i}", [P, HG, tot]) for i in range(2)]
        bias = [sb(f"bias{i}", [P, T]) for i in range(SR)]
        mx = sb("mx", [P, H, NT])
        nmx = sb("nmx", [P, H, NT])
        den = sb("den", [P, H, NT])
        rden = sb("rden_s", [P, H, NT])
        oT = sb("oT", [P, G, T])

        with nc.Block() as block:

            @block.tensor
            def _(pe):
                def scores(h):
                    if h % (2 * HG) == 0:
                        pe.wait_ge(q_in[h // (2 * HG)], 128)
                        pe.wait_ge(k_in[h // (2 * HG)], 128)
                    if h:
                        pe.wait_ge(m_done, h * NT)
                    for t in range(NT):
                        pe.matmul(ps[:, first[t]:first[t] + width[t]], qs[:, h % HG, h // HG, t * P:t * P + P],
                                  ks[:, h % HG, h // HG, 0:width[t]], start=True, stop=True).then_inc(s_made, 1)

                def turn(h):
                    pe.wait_ge(n_done, h * NT + NT)
                    if h:
                        pe.wait_ge(t_kept_a, 2 * h)
                        pe.wait_ge(t_kept_d, h)
                    for c in range(NT):
                        for t in range(c, NT):
                            at = 1536 + tfirst[c] + (t - c) * P
                            last = pe.transpose(ps[:, at:at + P], sc[h % SR][:, kept[t] + c * P:kept[t] + c * P + P],
                                                s.ident[:, :])
                    last.then_inc(t_made, 1)

                def weighted(g):
                    pe.wait_ge(t_kept_a, 2 * (g * HG + HG))
                    pe.wait_ge(t_kept_d, g * HG + HG)
                    if g >= 2:
                        pe.wait_ge(o_kept, g - 1)
                    b = 6 + g % 2
                    for c in range(NT):
                        for j in range(HG):
                            hd = (g * HG + j) * D
                            last = pe.matmul(ps[D * j:D * j + D, b * 512 + c * P:b * 512 + T], v[:, c, hd:hd + D],
                                             pT[g % 2][:, j, tkept[c]:tkept[c] + twidth[c]],
                                             start=(c == 0), stop=(c == NT - 1), tile_position=(0, D * j),
                                             skip_group_check=True)
                    last.then_inc(o_made, 1)

                scores(0)
                scores(1)
                for h in range(H):
                    if h + 2 < H:
                        scores(h + 2)
                    turn(h)
                    if h % HG == 0 and h:
                        weighted(h // HG - 1)
                weighted(G - 1)
                pe.wait_ge(o_kept, G)
                for t in range(NT):
                    for g in range(G):
                        last = pe.matmul(bank(ps, t), oT[:, g, t * P:t * P + P], w[3][:, g, :],
                                         start=(g == 0), stop=(g == G - 1))
                    last.then_inc(y_made, 1)

            @block.vector
            def _(dve):
                def finish(h):
                    dve.wait_ge(e_done, h * NT + NT)
                    dve.reciprocal(rden[:, h, :], den[:, h, :]).then_inc(r_done, 1)
                    dve.wait_ge(r_done, h + 1)
                    for t in range(NT):
                        p = sc[h % SR][:, kept[t]:kept[t] + width[t]]
                        dve.tensor_scalar(p, p, rden[:, h, t:t + 1], None, ALU.mult).then_inc(n_done, 1)

                def keep(h):
                    dve.wait_ge(t_made, h + 1)
                    if h >= 2 * HG and h % HG == 0:
                        dve.wait_ge(o_made, h // HG - 1)
                    g, j = h // HG, h % HG
                    dve.tensor_copy(pT[g % 2][:, j, 0:512], ps[:, 1536:2048]).then_inc(t_kept_d, 1)

                def keep_o(g):
                    dve.wait_ge(o_made, g + 1)
                    dve.tensor_copy(oT[:, g, :], bank(ps, 6 + g % 2)).then_inc(o_kept, 1)

                for h in range(H):
                    dve.wait_ge(bias_done, h + 1)
                    if h >= SR:
                        dve.wait_ge(t_made, h - SR + 1)
                    for t in range(NT):
                        dve.wait_ge(s_made, h * NT + max(t, 1) + 1)
                        dve.tensor_tensor_reduce(out=sc[h % SR][:, kept[t]:kept[t] + width[t]],
                                                 in0=ps[:, first[t]:first[t] + width[t]],
                                                 in1=bias[h % SR][:, T - width[t]:T], scale=1.0, scalar=NEG,
                                                 op0=ALU.add, op1=ALU.max, accum_out=mx[:, h, t:t + 1])\
                           .then_inc(m_done, 1)
                    dve.wait_ge(m_done, h * NT + NT)
                    dve.tensor_scalar(nmx[:, h, :], mx[:, h, :], -1.0, None, ALU.mult).then_inc(nm_done, 1)
                    if h:
                        finish(h - 1)
                    if h >= 2:
                        keep(h - 2)
                    if h % HG == 2 and h > HG:
                        keep_o(h // HG - 1)
                finish(H - 1)
                keep(H - 2)
                keep(H - 1)
                keep_o(G - 1)
                for t in range(NT):
                    dve.wait_ge(y_made, t + 1)
                    dve.tensor_tensor(x_out[:, t, :], x[:, t, :], bank(ps, t), ALU.add)

            @block.scalar
            def _(act):
                def keep(h):
                    g, j = h // HG, h % HG
                    act.wait_ge(t_made, h + 1)
                    if h >= 2 * HG and h % HG == 0:
                        act.wait_ge(o_made, h // HG - 1)
                    act.copy(pT[g % 2][:, j, 512:512 + 384], ps[:, 1536 + 1024:1536 + 1024 + 384])\
                       .then_inc(t_kept_a, 1)
                    act.copy(pT[g % 2][:, j, 896:1280], ps[:, 1536 + 512:1536 + 512 + 384]).then_inc(t_kept_a, 1)

                for h in range(H):
                    act.wait_ge(nm_done, h + 1)
                    for t in range(NT):
                        p = sc[h % SR][:, kept[t]:kept[t] + width[t]]
                        act.activation(p, p, ACT.Exp, bias=nmx[:, h, t:t + 1],
                                       accum_out=den[:, h, t:t + 1]).then_inc(e_done, 1)
                    if h:
                        keep(h - 1)
                keep(H - 1)

            @block.gpsimd
            def _(pool):
                for h in range(H):
                    if h >= SR:
                        pool.wait_ge(m_done, (h - SR + 1) * NT)
                    pool.tensor_scalar(bias[h % SR][:, :], strip[:, :], 2.0 ** (-8.0 / H * (h + 1)), None, ALU.mult)\
                        .then_inc(bias_done, 1)


NEG = -3.0e38


def feed_forward(s, d, x, x_out):
    nc, ps = s.nc, s.ps
    E, HID = 8, 2048
    HC = HID // 512
    TILES = T // P + E
    with ExitStack() as ctx:
        def sb(name, shape, dt=F32):
            return ctx.enter_context(nc.sbuf_tensor(name, shape, dt))

        def sem(name):
            return ctx.enter_context(nc.semaphore(name))

        xn = sb("xn3", [P, NT, C])
        xh, xl = sb("xs_h", [P, NT, C], F32R), sb("xs_l", [P, NT, C], F32R)
        pos = sb("pos", [P, NT])
        table = sb("table", [1, TILES + 1], I32)
        iota = sb("iota", [P, P])
        w1 = [sb(f"w1_{i}", [P, NC, 512]) for i in range(HC)]
        w2 = [sb(f"w2_{i}", [P, 4, C]) for i in range(HC)]
        b1, b2 = sb("b1", [P, HID // P]), sb("b2", [P, C])
        loaded = sem("r_loaded")

        with ExitStack() as rc:
            def rb(name, shape, dt=F32):
                return rc.enter_context(nc.sbuf_tensor(name, shape, dt))

            xnT = rb("xnT3", [P, NC, T])
            gw, gb = rb("gate_w", [P, NC, E]), rb("gate_b", [P, E])
            tri, iota8, iotaT = rb("tri", [P, P]), rb("iota8", [P, E]), rb("iotaT", [P, TILES])
            with nc.Block() as block:

                @block.sync
                def _(sp):
                    sp.dma_start(gw[:, :, :], d["gate_w"].rearrange("(k p) e -> p k e", p=P)).then_inc(loaded, 16)
                    sp.dma_start(gb[:, :], d["gate_b"].partition_broadcast(P)).then_inc(loaded, 16)
                    sp.dma_start(tri[:, :], d["tri"]).then_inc(loaded, 16)
                    sp.dma_start(iota[:, :], d["iota"].partition_broadcast(P)).then_inc(loaded, 16)
                    sp.dma_start(iota8[:, :], d["iota"][0:E].partition_broadcast(P)).then_inc(loaded, 16)
                    sp.dma_start(iotaT[:, :], d["iota"][0:TILES].partition_broadcast(P)).then_inc(loaded, 16)

            layer_norm(s, "ln3", x, xn)
            transpose_tokens(s, "ln3", xn, xnT)

            A = [rb(f"route{i}", [P, NT, E]) for i in range(12)]
            (lg, ex, sco, e1, c1, o1, s2, c2, oh, pre, rk, tmp) = A
            S = [rb(f"tok{i}", [P, NT]) for i in range(11)]
            (m, sm, rs, m1, i1, m2, i2, v1, v2, es, wt) = S
            sums = rb("sums", [P, E])
            cum = [rb(f"cum{i}", [P, 2 * E]) for i in range(4)]
            nt4 = rb("nt4", [P, E, 4])
            cmp = rb("cmp", [P, TILES, E])
            tabf = rb("tabf", [P, TILES + 1])
            step, lg_made, shifted, exped, rank_made, oh_ready = \
                [rc.enter_context(nc.semaphore(n)) for n in ("r_step", "lg_made", "shifted", "exped", "rank_made",
                                                             "oh_ready")]

            def row(t):
                return t[:, :].unsqueeze(2).broadcast_to([P, NT, E])

            i8 = iota8[:, :].unsqueeze(1).broadcast_to([P, NT, E])
            with nc.Block() as block:

                @block.tensor
                def _(pe):
                    pe.wait_ge(loaded, 96)
                    for t in range(NT):
                        for k in range(NC):
                            last = pe.matmul(ps[:, t * E:t * E + E], xnT[:, k, t * P:t * P + P], gw[:, k, :],
                                             start=(k == 0), stop=(k == NC - 1))
                    last.then_inc(lg_made, 1)
                    pe.wait_ge(oh_ready, 1)
                    pe.matmul(ps[:, 512:512 + NT * E], s.ones[:, :], pre[:, :, :], start=True, stop=False)
                    pe.matmul(ps[:, 512:512 + NT * E], tri[:, :], oh[:, :, :], start=False, stop=True)
                    pe.matmul(ps[:, 1024:1024 + E], s.ones[:, :], sums[:, :], start=True,
                              stop=True).then_inc(rank_made, 1)

                @block.scalar
                def _(act):
                    act.wait_ge(shifted, 1)
                    act.activation(ex[:, :, :], tmp[:, :, :], ACT.Exp).then_inc(exped, 1)

                @block.vector
                def _(dve):
                    n = [0]

                    def then(ins):
                        n[0] += 1
                        ins.then_inc(step, 1)
                        dve.wait_ge(step, n[0])

                    dve.wait_ge(lg_made, 1)
                    psl = ps[:, 0:NT * E].rearrange("p (t e) -> p t e", e=E)
                    then(dve.tensor_tensor(lg[:, :, :], psl, gb[:, :].unsqueeze(1).broadcast_to([P, NT, E]), ALU.add))
                    then(dve.tensor_reduce(m[:, :], lg[:, :, :], AX.X, ALU.max))
                    dve.tensor_tensor(tmp[:, :, :], lg[:, :, :], row(m), ALU.subtract).then_inc(shifted, 1)
                    dve.wait_ge(exped, 1)
                    then(dve.tensor_reduce(sm[:, :], ex[:, :, :], AX.X, ALU.add))
                    then(dve.reciprocal(rs[:, :], sm[:, :]))
                    then(dve.tensor_tensor(sco[:, :, :], ex[:, :, :], row(rs), ALU.mult))

                    def top(src, val, idx, eq, cand):
                        then(dve.tensor_reduce(val[:, :], src[:, :, :], AX.X, ALU.max))
                        then(dve.tensor_tensor(eq[:, :, :], src[:, :, :], row(val), ALU.is_equal))
                        then(dve.scalar_tensor_tensor(cand[:, :, :], eq[:, :, :], -float(E), i8, ALU.mult, ALU.add))
                        then(dve.tensor_reduce(idx[:, :], cand[:, :, :], AX.X, ALU.min))
                        then(dve.tensor_scalar(idx[:, :], idx[:, :], float(E), None, ALU.add))

                    top(sco, m1, i1, e1, c1)
                    then(dve.tensor_tensor(o1[:, :, :], i8, row(i1), ALU.is_equal))
                    then(dve.scalar_tensor_tensor(s2[:, :, :], o1[:, :, :], -2.0, sco[:, :, :], ALU.mult, ALU.add))
                    top(s2, m2, i2, e1, c2)
                    for val, idx, v in ((m1, i1, v1), (m2, i2, v2)):
                        then(dve.tensor_scalar(v[:, :], val[:, :], 0.0, None, ALU.is_gt))
                        then(dve.scalar_tensor_tensor(v[:, :], idx[:, :], 1.0, v[:, :], ALU.add, ALU.mult))
                    then(dve.tensor_tensor(es[:, :], v1[:, :], v2[:, :], ALU.max))
                    then(dve.tensor_scalar(es[:, :], es[:, :], -1.0, None, ALU.add))
                    then(dve.tensor_tensor(oh[:, :, :], i8, row(es), ALU.is_equal))
                    then(dve.memset(pre[:, 0, :], 0.0))
                    for t in range(1, NT):
                        then(dve.tensor_tensor(pre[:, t, :], pre[:, t - 1, :], oh[:, t - 1, :], ALU.add))
                    dve.tensor_tensor(sums[:, :], pre[:, NT - 1, :], oh[:, NT - 1, :], ALU.add).then_inc(oh_ready, 1)
                    then(dve.tensor_tensor(tmp[:, :, :], sco[:, :, :], oh[:, :, :], ALU.mult))
                    then(dve.tensor_reduce(wt[:, :], tmp[:, :, :], AX.X, ALU.add))
                    for t in range(NT):
                        then(dve.tensor_scalar(xn[:, t, :], xn[:, t, :], wt[:, t:t + 1], None, ALU.mult))
                    then(dve.tensor_copy(xh[:, :, :], xn[:, :, :]))
                    then(dve.tensor_tensor(xl[:, :, :], xn[:, :, :], xh[:, :, :].bitcast(F32), ALU.subtract))
                    dve.wait_ge(rank_made, 1)
                    for j in range(4):
                        then(dve.tensor_scalar(nt4[:, :, j], ps[:, 1024:1024 + E], float(P * j), None, ALU.is_gt))
                    for c in cum:
                        then(dve.memset(c[:, :], 0.0))
                    then(dve.tensor_reduce(cum[0][:, E:2 * E], nt4[:, :, :], AX.X, ALU.add))
                    for i in range(3):
                        then(dve.tensor_tensor(cum[i + 1][:, E:2 * E], cum[i][:, E:2 * E],
                                               cum[i][:, E - 2 ** i:2 * E - 2 ** i], ALU.add))
                    base = cum[3][:, E - 1:2 * E - 1].unsqueeze(1).broadcast_to([P, NT, E])
                    then(dve.tensor_scalar(rk[:, :, :], ps[:, 512:512 + NT * E].rearrange("p (t e) -> p t e", e=E),
                                           1.0, None, ALU.add))
                    then(dve.scalar_tensor_tensor(tmp[:, :, :], base, float(P), rk[:, :, :], ALU.mult, ALU.add))
                    then(dve.tensor_tensor(tmp[:, :, :], tmp[:, :, :], oh[:, :, :], ALU.mult))
                    then(dve.tensor_reduce(pos[:, :], tmp[:, :, :], AX.X, ALU.add))
                    then(dve.tensor_scalar(pos[:, :], pos[:, :], -1.0, None, ALU.add))
                    incl = cum[3][:, E:2 * E].unsqueeze(1).broadcast_to([P, TILES, E])
                    then(dve.tensor_tensor(cmp[:, :, :], incl, iotaT[:, :].unsqueeze(2).broadcast_to([P, TILES, E]),
                                           ALU.is_le))
                    then(dve.tensor_reduce(tabf[:, 0:TILES], cmp[:, :, :], AX.X, ALU.add))
                    then(dve.tensor_scalar(tabf[:, 0:TILES], tabf[:, 0:TILES], float(E - 1), None, ALU.min))
                    then(dve.tensor_scalar(tabf[:, TILES:TILES + 1], cum[3][:, 2 * E - 1:2 * E], 2.0, None, ALU.max))
                    then(dve.tensor_copy(table[:, :], tabf[0:1, :]))

        with ExitStack() as ec:
            def eb(name, shape, dt=F32):
                return ec.enter_context(nc.sbuf_tensor(name, shape, dt))

            def esem(name):
                return ec.enter_context(nc.semaphore(name))

            WC = 2 * HC
            WS = HC
            POOL_LOW = (HC - 1, WC - 1)
            perm = eb("perm", [P, NT, P], F32R)
            permT = eb("permT", [P, NT, P], F32R)
            xg = [eb(f"xg_{i}", [P, NC, P], F32R) for i in "hl"]
            hs = [eb(f"hs{i}", [P, 512]) for i in range(2)]
            hf = [eb(f"hf{i}", [P, 4, P]) for i in range(2)]
            hT = [eb(f"hT_{i}", [P, HID // P, P], F32R) for i in "hl"]
            y, yh, yl = eb("y", [P, C]), eb("yh", [P, C], F32R), eb("yl", [P, C], F32R)
            wh = [eb(f"wsplit_h{i}", [P, 4, 512], F32R) for i in range(WS)]
            wl = [eb(f"wsplit_l{i}", [P, 4, 512], F32R) for i in range(WS)]
            w_in = [esem(f"w_in{i}") for i in range(WC)]
            b1_in, b2_in = esem("b1_in"), esem("b2_in")
            (wh_done, wl_dve, wl_pool, pos_down, perm_done, xg_made, xgh_kept, xgl_kept, pt_made, pt_kept, h_made,
             h_kept, ht_made, hf_kept, hh_kept, hl_kept, w2_used, y_done, yh_done, yl_done, sc_made, sc_added) = \
                [esem(n) for n in ("wh_done", "wl_dve", "wl_pool", "pos_down", "perm_done", "xg_made", "xgh_kept",
                                   "xgl_kept", "pt_made", "pt_kept", "h_made", "h_kept", "ht_made", "hf_kept",
                                   "hh_kept", "hl_kept", "w2_used", "y_done", "yh_done", "yl_done", "sc_made",
                                   "sc_added")]
            raw = w1 + w2
            w1_d = d["w1"].rearrange("e (k p) h -> e p k h", p=P)
            w2_d = d["w2"].rearrange("e (j p) n -> e p j n", p=P)
            ND = WC - len(POOL_LOW)
            sc_bank = (0, 1, 2, 7)

            def low_order(i):
                mine = [c for c in range(WC) if (c in POOL_LOW) == (i in POOL_LOW)]
                return mine.index(i) + 1

            with nc.Block() as block:

                def tiles(eng):
                    return eng.value_load(table[0:1, TILES:TILES + 1], min_val=2, max_val=TILES - 1)

                @block.sync
                def _(sp):
                    def load(e, i, n):
                        if n is not None:
                            lows = (wl_pool, len(POOL_LOW)) if i in POOL_LOW else (wl_dve, ND)
                            sp.wait_ge(lows[0], n * lows[1] + low_order(i))
                        if i < HC:
                            src = w1_d[bass.ds(e, 1), :, :, i * 512:i * 512 + 512]
                        else:
                            src = w2_d[bass.ds(e, 1), :, 4 * (i - HC):4 * (i - HC) + 4, :]
                        sp.dma_start(raw[i][:, :, :], src.squeeze(0)).then_inc(w_in[i], 16)

                    def expert(at):
                        return sp.value_load(table[0:1, at], min_val=0, max_val=E - 1)

                    e, following = expert(slice(0, 1)), expert(slice(1, 2))
                    for i in range(WC):
                        load(e, i, None)
                    for i in range(HC):
                        load(following, i, 0)
                    with sp.Fori(1, tiles(sp)) as it:
                        e, following = expert(bass.ds(it, 1)), expert(bass.ds(it + 1, 1))
                        for i in range(HC, WC):
                            load(e, i, it - 1)
                        for i in range(HC):
                            load(following, i, it)

                @block.gpsimd
                def _(pool):
                    def low(n, i):
                        pool.wait_ge(wh_done, n * WC + i + 1)
                        pool.tensor_tensor(wl[i % WS][:, :, :], raw[i][:, :, :], wh[i % WS][:, :, :].bitcast(F32),
                                           ALU.subtract).then_inc(wl_pool, 1)

                    def biases(at):
                        e = pool.value_load(table[0:1, at], min_val=0, max_val=E - 1)
                        return (d["b1c"][bass.ds(e, 1), :, :].squeeze(0),
                                d["b2"][bass.ds(e, 1), :].broadcast_to([P, C]))

                    b1_src, b2_src = biases(slice(0, 1))
                    pool.dma_start(b1[:, :], b1_src).then_inc(b1_in, 16)
                    pool.dma_start(b2[:, :], b2_src).then_inc(b2_in, 16)
                    low(0, HC - 1)
                    with pool.Fori(0, tiles(pool)) as it:
                        low(it, WC - 1)
                        b1_src, b2_src = biases(bass.ds(it + 1, 1))
                        pool.wait_ge(hf_kept, it * HC + HC)
                        pool.dma_start(b1[:, :], b1_src).then_inc(b1_in, 16)
                        low(it + 1, HC - 1)
                        pool.wait_ge(y_done, it + 1)
                        pool.dma_start(b2[:, :], b2_src).then_inc(b2_in, 16)

                @block.tensor
                def _(pe):
                    def gather(it):
                        pe.wait_ge(perm_done, it * NT + NT)
                        for k in range(NC):
                            for t in range(NT):
                                for i, part in enumerate((xh, xl)):
                                    last = pe.matmul(ps[:, 5 * 512 + k * P:5 * 512 + k * P + P],
                                                     part[:, t, k * P:k * P + P], perm[:, t, :],
                                                     start=(t == 0 and i == 0), stop=(t == NT - 1 and i == 1))
                        last.then_inc(xg_made, 1)

                    def three(out, x, xcols, i, q, first, last):
                        w = (wh[i % WS][:, q, :], wl[i % WS][:, q, :])
                        for m, (a, b) in enumerate(((0, 0), (0, 1), (1, 0))):
                            mm = pe.matmul(out, x[a][:, xcols, :], w[b], start=(first and m == 0),
                                           stop=(last and m == 2))
                        return mm

                    def split_ready(it, i):
                        lows = (wl_pool, len(POOL_LOW)) if i in POOL_LOW else (wl_dve, ND)
                        pe.wait_ge(lows[0], it * lows[1] + low_order(i))

                    gather(0)
                    with pe.Fori(0, tiles(pe)) as it:
                        for t in range(NT):
                            last = pe.transpose(ps[:, 6 * 512 + t * P:6 * 512 + t * P + P],
                                                perm[:, t, :].bitcast(F32), s.ident[:, :])
                        last.then_inc(pt_made, 1)
                        pe.wait_ge(xgl_kept, it + 1)

                        def turn_h(i):
                            pe.wait_ge(h_kept, it * HC + i + 1)
                            for q in range(4):
                                last = pe.transpose(ps[:, (2 + i % 2) * 512 + q * P:(2 + i % 2) * 512 + q * P + P],
                                                    hs[i % 2][:, q * P:q * P + P], s.ident[:, :])
                            last.then_inc(ht_made, 1)

                        for i in range(HC):
                            split_ready(it, i)
                            if i < 2:
                                pe.wait_ge(sc_added, it * NT + i + 1)
                            else:
                                pe.wait_ge(h_kept, it * HC + i - 1)
                            for k in range(NC):
                                last = three(bank(ps, i % 2), xg, k, i, k, k == 0, k == NC - 1)
                            last.then_inc(h_made, 1)
                            if i:
                                if i == 1:
                                    pe.wait_ge(sc_added, it * NT + 3)
                                if i - 1 >= 2:
                                    pe.wait_ge(hf_kept, it * HC + i - 2)
                                turn_h(i - 1)
                        pe.wait_ge(hf_kept, it * HC + HC - 2)
                        for i in range(HC):
                            if i == 1:
                                turn_h(HC - 1)
                            split_ready(it, HC + i)
                            pe.wait_ge(hl_kept, it * HC + i + 1)
                            for q in range(4):
                                j = 4 * i + q
                                last = three(bank(ps, 4), hT, j, HC + i, q, j == 0, j == HID // P - 1)
                            last.then_inc(w2_used, 1)
                        gather(it + 1)
                        pe.wait_ge(pt_kept, it + 1)
                        pe.wait_ge(yl_done, it + 1)
                        for t in range(NT):
                            if t == 3:
                                pe.wait_ge(sc_added, it * NT + NT)
                            for i, part in enumerate((yh, yl)):
                                last = pe.matmul(bank(ps, sc_bank[t]), permT[:, t, :], part[:, :],
                                                 start=(i == 0), stop=(i == 1))
                            last.then_inc(sc_made, 1)

                @block.vector
                def _(dve):
                    def low(n, i):
                        dve.wait_ge(wh_done, n * WC + i + 1)
                        dve.tensor_tensor(wl[i % WS][:, :, :], raw[i][:, :, :], wh[i % WS][:, :, :].bitcast(F32),
                                          ALU.subtract).then_inc(wl_dve, 1)

                    def place(it):
                        for t in range(NT):
                            dve.tensor_scalar(perm[:, t, :], iota[:, :], pos[:, t:t + 1], None, ALU.is_equal)\
                               .then_inc(perm_done, 1)

                    def keep(it):
                        b5 = bank(ps, 5).rearrange("p (k n) -> p k n", n=P)
                        dve.wait_ge(xg_made, it + 1)
                        dve.tensor_copy(xg[0][:, :, :], b5).then_inc(xgh_kept, 1)
                        dve.wait_ge(xgh_kept, it + 1)
                        dve.tensor_tensor(xg[1][:, :, :], b5, xg[0][:, :, :].bitcast(F32), ALU.subtract)\
                           .then_inc(xgl_kept, 1)

                    dve.memset(y[:, :], 0.0).then_inc(sc_added, NT)
                    place(0)
                    keep(0)
                    for i in range(HC - 1):
                        low(0, i)
                    with dve.Fori(0, tiles(dve)) as it:
                        def split_h(i):
                            part = slice(4 * i, 4 * i + 4)
                            dve.wait_ge(hf_kept, it * HC + i + 1)
                            dve.tensor_copy(hT[0][:, part, :], hf[i % 2][:, :, :]).then_inc(hh_kept, 1)
                            dve.wait_ge(hh_kept, it * HC + i + 1)
                            dve.tensor_tensor(hT[1][:, part, :], hf[i % 2][:, :, :], hT[0][:, part, :].bitcast(F32),
                                              ALU.subtract).then_inc(hl_kept, 1)

                        dve.wait_ge(pt_made, it + 1)
                        dve.tensor_copy(permT[:, :, :], bank(ps, 6).rearrange("p (t n) -> p t n", n=P))\
                           .then_inc(pt_kept, 1)
                        dve.tensor_scalar(pos[:, :], pos[:, :], -float(P), None, ALU.add).then_inc(pos_down, 1)
                        dve.wait_ge(pos_down, it + 1)
                        place(it + 1)
                        for i in range(HC):
                            if i < HC - 1:
                                low(it, HC + i)
                            split_h(i)
                        low(it + 1, 0)
                        dve.wait_ge(w2_used, it * HC + 2 * HC)
                        dve.wait_ge(b2_in, it * 16 + 16)
                        dve.tensor_tensor(y[:, :], bank(ps, 4), b2[:, :], ALU.add).then_inc(y_done, 1)
                        dve.wait_ge(y_done, it + 1)
                        dve.tensor_copy(yh[:, :], y[:, :]).then_inc(yh_done, 1)
                        dve.wait_ge(yh_done, it + 1)
                        dve.tensor_tensor(yl[:, :], y[:, :], yh[:, :].bitcast(F32), ALU.subtract).then_inc(yl_done, 1)
                        keep(it + 1)
                        for t in range(NT):
                            dve.wait_ge(sc_made, it * NT + t + 1)
                            dve.tensor_tensor(x[:, t, :], x[:, t, :], bank(ps, sc_bank[t]), ALU.add)\
                               .then_inc(sc_added, 1)
                        low(it + 1, 1)
                        low(it + 1, 2)

                @block.scalar
                def _(act):
                    def high(n, i):
                        act.wait_ge(w_in[i], n * 16 + 16)
                        if i < WS:
                            act.wait_ge(w2_used, n * HC + i + 1)
                        else:
                            act.wait_ge(h_made, n * HC + i - HC + 1)
                        act.copy(wh[i % WS][:, :, :], raw[i][:, :, :]).then_inc(wh_done, 1)

                    act.copy(hs[0][:, 0:1], x[:, 0, 0:1]).then_inc(w2_used, HC)
                    for i in range(HC):
                        high(0, i)
                    with act.Fori(0, tiles(act)) as it:
                        def relus(i):
                            act.wait_ge(ht_made, it * HC + i + 1)
                            for q in range(4):
                                j = 4 * i + q
                                last = act.activation(hf[i % 2][:, q, :],
                                                      ps[:, (2 + i % 2) * 512 + q * P:(2 + i % 2) * 512 + q * P + P],
                                                      ACT.Relu, bias=b1[:, j:j + 1])
                            last.then_inc(hf_kept, 1)

                        act.wait_ge(b1_in, it * 16 + 16)
                        for i in range(HC):
                            act.wait_ge(h_made, it * HC + i + 1)
                            act.copy(hs[i % 2][:, :], bank(ps, i % 2)).then_inc(h_kept, 1)
                            high(it, HC + i)
                            if i:
                                if i - 1 >= 2:
                                    act.wait_ge(hl_kept, it * HC + i - 2)
                                relus(i - 1)
                        act.wait_ge(hl_kept, it * HC + HC - 2)
                        relus(HC - 1)
                        for i in range(HC):
                            high(it + 1, i)


STOP = 3
DEN_MIN, DEN_MAX, SUM_MAX = 1e-6, 1e20, 1e37


def layer(nc, d, out):
    s = Stage()
    s.nc = nc
    with ExitStack() as ctx:
        def sb(name, shape, dt=F32):
            return ctx.enter_context(nc.sbuf_tensor(name, shape, dt))

        s.ps = ctx.enter_context(nc.psum_tensor("psum", [P, 4096], F32))
        s.ident = sb("ident", [P, P])
        s.cols = sb("cols", [P, 12])
        s.bq, s.bk, s.bv = s.cols[:, 0:4], s.cols[:, 4:8], s.cols[:, 8:12]
        s.eps = sb("eps", [P, 1])
        s.ones = sb("ones", [P, P])
        x1 = sb("x1", [P, NT, C])
        bad = sb("bad", [P, 1], I32)
        d["qT_d"] = nc.dram_tensor("qT_d", (C, T), F32).ap()
        with nc.sbuf_tensor("o_acc", [P, G, T], F32) as oacc:
            cross_attention(s, d, oacc, bad)
            is_bad = nc.values_load(bad[0:1, 0:1], min_val=0, max_val=1)
            with nc.If(is_bad > 0):
                general_cross(s, d, oacc)
            cross_output(s, d, oacc, x1)
        if STOP > 1:
            self_attention(s, d, x1, x1)
        if STOP > 2:
            feed_forward(s, d, x1, x1)
        done = ctx.enter_context(nc.semaphore("out_done"))
        with nc.Block() as block:

            @block.sync
            def _(sp):
                sp.dma_start(out.rearrange("(t p) c -> p t c", p=P), x1[:, :, :]).then_inc(done, 16)
                sp.wait_ge(done, 16)


def kernel(**inputs):
    import concourse.bacc as bacc
    from concourse.bass_utils import run_bass_kernel_spmd

    f = lambda n: np.asarray(inputs[n])
    col = lambda a: np.ascontiguousarray(a.reshape(-1, P).T)
    arrays = {
        "x": f("x").reshape(T, C),
        "ctxT": np.ascontiguousarray(f("ctx_768").reshape(N, CK).T),
        "Wq": f("L0_xattn_Wq"), "Wk": f("L0_xattn_Wk"), "Wv": f("L0_xattn_Wv"), "Wo": f("L0_xattn_Wo"),
        "cols": np.ascontiguousarray(np.concatenate([col(f("L0_xattn_b" + n)) for n in "qkv"], axis=1)),
        "bo": f("L0_xattn_bo"),
        "ident": np.eye(P, dtype=np.float32),
        "gate_w": f("L0_ffn_gate_w"), "gate_b": f("L0_ffn_gate_b"),
        "w1": f("L0_ffn_w1"), "w2": f("L0_ffn_w2"), "b2": f("L0_ffn_b2"),
        "b1c": np.ascontiguousarray(f("L0_ffn_b1").reshape(8, -1, P).transpose(0, 2, 1)),
        "tri": np.triu(np.ones((P, P), np.float32), 1),
        "iota": np.arange(P, dtype=np.float32),
    }
    for n in "qkvo":
        arrays[f"W{n}T_s"] = np.ascontiguousarray(f(f"L0_attn_W{n}").T)
    dist = np.arange(P)[:, None] + (T - P) - np.arange(T)[None, :]
    arrays["strip"] = np.where(dist >= 0, -dist, NEG).astype(np.float32)
    nc = bacc.Bacc("TRN2", target_bir_lowering=False, num_devices=1)
    d = {n: nc.dram_tensor("in_" + n, a.shape, mybir.dt.from_np(a.dtype), kind="ExternalInput").ap()
         for n, a in arrays.items()}
    out = nc.dram_tensor("out", (T, C), F32, kind="ExternalOutput").ap()
    layer(nc, d, out)
    r = run_bass_kernel_spmd(nc, [{"in_" + n: a for n, a in arrays.items()}], core_ids=[0])
    return r.results[0]["out"].reshape(1, T, C)
```

```python
import numpy as np
import concourse.bass as bass
from concourse import mybir
from contextlib import ExitStack

F32 = mybir.dt.float32
F32R = mybir.dt.float32r
I32 = mybir.dt.int32
ALU = mybir.AluOpType
ACT = mybir.ActivationFunctionType
AX = mybir.AxisListType

P = 128
T, C, CK = 512, 512, 384
N = 8192
H, D = 16, 32
NT = T // P
NC = C // P
NK = CK // P
G, HG = NC, P // D
EPS = 1e-5

KB = 512
NB = N // KB
CB = KB // P
U = G * CB


def bank(ps, i, n=512):
    return ps[:, i * 512:i * 512 + n]


def next_place(nc):
    return (nc.sbuf_base + 31) // 32 * 32


class Stage:
    pass


class LayerNorm:

    def __init__(self, s, ctx):
        nc = s.nc
        self.ps, self.eps, self.ident = s.ps, s.eps, s.ident
        self.stats, self.mv, self.std, self.rstd = \
            [ctx.enter_context(nc.sbuf_tensor("ln_" + n, shape, F32))
             for n, shape in (("stats", [P, NT, 6]), ("mv", [P, NT, 2]), ("std", [P, NT]), ("rstd", [P, NT]))]
        (self.stats_done, self.mv_done, self.std_done, self.rstd_done, self.xn_done, self.turned, self.dve_kept,
         self.act_kept) = \
            [ctx.enter_context(nc.semaphore("ln_" + n))
             for n in ("stats_done", "mv_done", "std_done", "rstd_done", "xn_done", "turned", "dve_kept", "act_kept")]

    def vector_moments(self, dve, before, src, tile=None):
        tiles = range(NT) if tile is None else (tile,)
        for t in tiles:
            dve.bn_stats(self.stats[:, t, :], src[:, t, :]).then_inc(self.stats_done, 1)
        for t in tiles:
            dve.wait_ge(self.stats_done, before * NT + t + 1)
            dve.bn_aggr(self.mv[:, t, :], self.stats[:, t, :]).then_inc(self.mv_done, 1)

    def scalar_roots(self, act, before):
        act.wait_ge(self.mv_done, before * NT + NT)
        act.activation(self.std[:, :], self.mv[:, :, 1], ACT.Sqrt, bias=self.eps[:, 0:1]).then_inc(self.std_done, 1)

    def vector_normalise(self, dve, before, src, dst):
        dve.wait_ge(self.std_done, before + 1)
        dve.reciprocal(self.rstd[:, :], self.std[:, :]).then_inc(self.rstd_done, 1)
        dve.wait_ge(self.rstd_done, before + 1)
        for t in range(NT):
            dve.tensor_scalar(dst[:, t, :], src[:, t, :], self.mv[:, t, 0:1], self.rstd[:, t:t + 1],
                              ALU.subtract, ALU.mult).then_inc(self.xn_done, 1)

    def tensor_turn(self, pe, before, src):
        for t in range(NT):
            pe.wait_ge(self.xn_done, before * NT + t + 1)
            for k in range(NC):
                last = pe.transpose(self.ps[:, k * 512 + t * P:k * 512 + t * P + P], src[:, t, k * P:k * P + P],
                                    self.ident[:, :])
                if t == NT - 1:
                    last.then_inc(self.turned, 1)

    def vector_keep(self, dve, before, dst):
        for k in range(0, NC, 2):
            dve.wait_ge(self.turned, before * NC + k + 1)
            dve.tensor_copy(dst[:, k, :], bank(self.ps, k)).then_inc(self.dve_kept, 1)

    def scalar_keep(self, act, before, dst):
        for k in range(1, NC, 2):
            act.wait_ge(self.turned, before * NC + k + 1)
            act.copy(dst[:, k, :], bank(self.ps, k)).then_inc(self.act_kept, 1)

    def wait_kept(self, eng, before):
        eng.wait_ge(self.dve_kept, (before + 1) * NC // 2)
        eng.wait_ge(self.act_kept, (before + 1) * NC // 2)


def cross_attention(s, d, wide, oacc, x1, bad):
    nc, ps = s.nc, s.ps
    outer = ExitStack()
    with outer:
        def sb(ctx, name, shape, dt=F32):
            return ctx.enter_context(nc.sbuf_tensor(name, shape, dt))

        def sem(ctx, name):
            return ctx.enter_context(nc.semaphore(name))

        qs = wide[:, :, :].rearrange("p (j g) t -> p j g t", j=HG)
        qf = x1
        wk = [sb(outer, f"wk_{x}", [P, NK, C], F32R) for x in "hl"]
        wv = [sb(outer, f"wv_{x}", [P, NK, C], F32R) for x in "hl"]
        craw = sb(outer, "ctx_raw", [P, NK, KB])
        dacc_at = next_place(nc)
        dacc = sb(outer, "den_acc", [P, G, HG, T])
        ctxT = d["ctxT"].rearrange("(k p) n -> p k n", p=P)

        with ExitStack() as ctx:
            ks_at = next_place(nc)
            ks = sb(ctx, "k_stack", [P, G, HG, KB], F32R)
            khl = [sb(ctx, f"k_split{i}", [P, 2, KB], F32R) for i in range(2)]
            vb = [sb(ctx, f"v{i}", [P, CB, C]) for i in range(2)]
            ch = [sb(ctx, f"ctx_h{i}", [P, NK, KB], F32R) for i in range(2)]
            cl = [sb(ctx, f"ctx_l{i}", [P, NK, KB], F32R) for i in range(2)]
            pr_at = next_place(nc)
            pr = [sb(ctx, f"probs{i}", [P, HG, T]) for i in range(2)]
            ND = 3

            names = ("ctx_loaded", "ch_done", "cl_done", "v_made", "k_made", "v_kept", "kh_kept", "kl_kept",
                     "sa_ready", "sb_ready", "ea_done", "eb_done", "pv_done", "o_kept", "den_dve", "den_pool")
            (ctx_loaded, ch_done, cl_done, v_made, k_made, v_kept, kh_kept, kl_kept,
             sa_ready, sb_ready, ea_done, eb_done, pv_done, o_kept, den_dve, den_pool) = \
                [sem(ctx, n) for n in names]
            k_stacked = [sem(ctx, f"k_stacked{g}") for g in range(G)]
            names = ("x_in", "ctx0_in", "wv_in", "wk_in", "wq_in_q_out", "small_in", "consts", "w_high", "w_low",
                     "q_done", "q_copied", "q_split", "den_cleared", "q_stacked", "q_stacked_pool")
            (x_in, ctx0_in, wv_in, wk_in, wq_in_q_out, small_in, consts, w_high, w_low,
             q_done, q_copied, q_split, den_cleared, q_stacked, q_stacked_pool) = \
                [sem(ctx, n) for n in names]
            size = 4 * G * T

            def at(name, shape, offset, dt=F32):
                return nc.alloc_sbuf_tensor_at(name, shape, dt, offset=offset)[:, :, :]

            x, xn = [at(n, [P, NT, C], s.wide_at + i * size) for i, n in enumerate(("x_in", "xn1"))]
            wq, xnT = [at(n, [P, NC, C], ks_at + (2 + i) * size) for i, n in enumerate(("wq", "xnT1"))]
            wv_raw, wk_raw = [at(n, [P, NK, C], dacc_at + i * size) for i, n in enumerate(("wv_raw", "wk_raw"))]
            qh, ql = [at(n, [P, G, T], pr_at + i * size, F32R) for i, n in enumerate(("qh", "ql"))]
            SD = 16 * 2 * HG

            def sbank(j):
                return bank(ps, j)

            with nc.Block() as block:

                def ctx_low(pool, b, par, k):
                    pool.wait_ge(ch_done, b * NK + k + 1)
                    pool.tensor_tensor(cl[par][:, k, :], craw[:, k, :], ch[par][:, k, :].bitcast(F32),
                                       ALU.subtract).then_inc(cl_done, 1)

                def stack_q(eng, g, halves, done):
                    eng.wait_ge(q_split, g + 2)
                    for j in range(HG):
                        for half in halves:
                            src = (qh, ql)[half][D * j:D * j + D, g:g + 2, :].bitcast(F32)
                            eng.dma_start(qs[64 * half:64 * half + 64, j, g:g + 2, :].bitcast(F32)
                                          .rearrange("p g t -> p (g t)"),
                                          src.rearrange("p g t -> p (g t)").unsqueeze(1).broadcast_to([D, 2, 2 * T]))\
                               .then_inc(done, 16)

                @block.sync
                def _(sp):
                    def stack(b, g):
                        sp.wait_ge(kl_kept, b * G + g + 1)
                        for j in range(HG):
                            for half in range(2):
                                sp.dma_start(ks[64 * half:64 * half + 64, g, j, :].bitcast(F32),
                                             khl[g % 2][D * j:D * j + D, :, :].bitcast(F32)).then_inc(k_stacked[g], 16)

                    def load(b):
                        sp.wait_ge(cl_done, b * NK)
                        src = ctxT[:, :, bass.ds(b * KB, KB)]
                        sp.dma_start(craw[:, :, :], src).then_inc(ctx_loaded, 16)

                    rows = "(k p) n -> p k n"
                    sp.dma_start(craw[:, :, :], ctxT[:, :, 0:KB]).then_inc(ctx0_in, 16)
                    sp.dma_start(wv_raw, d["Wv"].rearrange(rows, p=P)).then_inc(wv_in, 16)
                    sp.dma_start(wk_raw, d["Wk"].rearrange(rows, p=P)).then_inc(wk_in, 16)
                    sp.dma_start(x, d["x"].rearrange("(t p) c -> p t c", p=P)).then_inc(x_in, 16)
                    sp.dma_start(s.ident[:, :], d["ident"]).then_inc(small_in, 16)
                    sp.dma_start(s.cols[:, :], d["cols"]).then_inc(small_in, 16)
                    sp.dma_start(wq, d["Wq"].rearrange(rows, p=P)).then_inc(wq_in_q_out, 16)
                    load(1)
                    stack(0, 0)
                    stack(0, 1)
                    stack_q(sp, 0, (0, 1), q_stacked)
                    stack_q(sp, 2, (0,), q_stacked)
                    for g in range(2, G):
                        stack(0, g)
                    sp.dma_start(d["qT_d"].rearrange("(g p) n -> p g n", p=P), qf[:, :, :]).then_inc(wq_in_q_out, 16)

                    def blocks(it, last=False, first=False):
                        for par in range(2):
                            b = it * 2 + par
                            if not (first and par == 0):
                                stack(b, G - 1)
                            if not last:
                                load(b + 2)
                            if not (last and par == 1):
                                for g in range(G - 1):
                                    stack(b + 1, g)

                    blocks(0, first=True)
                    with sp.Fori(1, NB // 2 - 1) as it:
                        blocks(it)
                    blocks(NB // 2 - 1, last=True)
                    sp.wait_ge(wq_in_q_out, 32)

                @block.gpsimd
                def _(pool):
                    pool.memset(s.eps[:, :], EPS).then_inc(consts, 1)
                    pool.memset(s.ones[:, :], 1.0)
                    pool.memset(dacc[:, :, ND:, :], 0.0).then_inc(den_pool, 1)
                    for k in range(NK):
                        ctx_low(pool, 0, 0, k)
                    for k in range(NK):
                        ctx_low(pool, 1, 1, k)
                    stack_q(pool, 2, (1,), q_stacked_pool)

                    def blocks(it, last=False):
                        for par in range(2):
                            b = it * 2 + par
                            for i in range(U):
                                g = i // CB
                                n = b * U + i
                                pool.wait_ge(eb_done, n + 1)
                                pool.wait_ge(den_pool, n + 1)
                                pool.tensor_tensor(dacc[:, g, ND:, :], dacc[:, g, ND:, :], pr[i % 2][:, ND:, :],
                                                   ALU.add).then_inc(den_pool, 1)
                                if i in (6, 10, 14) and not last:
                                    ctx_low(pool, b + 2, par, i // 4 - 1)

                    blocks(0)
                    with pool.Fori(1, NB // 2 - 1) as it:
                        blocks(it)
                    blocks(NB // 2 - 1, last=True)

                @block.tensor
                def _(pe):
                    def product(b, par, kind, g, lo, hi):
                        if lo == 0:
                            if g == 0 and kind == "v":
                                pe.wait_ge(cl_done, b * NK + NK)
                            if kind == "v":
                                if isinstance(b, int) and b * CB + g == 0:
                                    pass
                                else:
                                    pe.wait_ge(v_kept, b * CB + g)
                            else:
                                if isinstance(b, int) and b * G + g == 0:
                                    pass
                                else:
                                    pe.wait_ge(kl_kept, b * G + g)
                        for m in range(lo, hi):
                            k, which = m // 3, m % 3
                            c = (ch, ch, cl)[which][par]
                            w = (wv if kind == "v" else wk)[(0, 1, 0)[which]]
                            cols = slice(g * P, g * P + P)
                            if kind == "v":
                                last = pe.matmul(bank(ps, 6), c[:, k, cols], w[:, k, :],
                                                 start=(m == 0), stop=(m == 8))
                            else:
                                last = pe.matmul(bank(ps, 7), w[:, k, cols], c[:, k, :],
                                                 start=(m == 0), stop=(m == 8))
                        if hi == 9:
                            last.then_inc(v_made if kind == "v" else k_made, 1)

                    def scores(b, i, pair, any_before=True):
                        g, c = i // CB, i % CB
                        if any_before:
                            pe.wait_ge((ea_done, eb_done)[pair], b * U + i)
                        if c == 0 and pair == 0:
                            pe.wait_ge(k_stacked[g], b * SD + SD)
                        for j in (2 * pair, 2 * pair + 1):
                            last = pe.matmul(sbank(j), ks[:, g, j, c * P:c * P + P], qs[:, j, g, :],
                                             start=True, stop=True)
                        last.then_inc((sa_ready, sb_ready)[pair], 1)

                    pe.wait_ge(w_low, 1)
                    product(0, 0, "v", 0, 0, 9)
                    pe.wait_ge(w_low, 2)
                    product(0, 0, "k", 0, 0, 9)
                    product(0, 0, "v", 1, 0, 9)
                    product(0, 0, "k", 1, 0, 9)
                    pe.wait_ge(small_in, 32)
                    s.ln.tensor_turn(pe, 0, xn)
                    pe.wait_ge(wq_in_q_out, 16)
                    s.ln.wait_kept(pe, 0)
                    for g in range(G):
                        for k in range(NC):
                            last = pe.matmul(bank(ps, g), wq[:, k, g * P:g * P + P], xnT[:, k, :],
                                             start=(k == 0), stop=(k == NC - 1))
                        last.then_inc(q_done, 1)
                    for g in range(2, G):
                        product(0, 0, "k", g, 0, 9)
                        product(0, 0, "v", g, 0, 9)
                    pe.wait_ge(q_stacked, 16 * 3 * HG)
                    pe.wait_ge(q_stacked_pool, 16 * HG)
                    scores(0, 0, 0, False)
                    scores(0, 0, 1, False)

                    def blocks(it, first=False, last=False):
                        for par in range(2):
                            b = it * 2 + par
                            end = last and par == 1
                            for i in range(U):
                                g, c = i // CB, i % CB
                                nxt = (b, i + 1) if i < U - 1 else (b + 1, 0)
                                if not (end and i == U - 1):
                                    scores(*nxt, 0)
                                if not end:
                                    kind = "v" if c < 2 else "k"
                                    lo, hi = ((0, 5), (5, 9))[c % 2]
                                    product(b + 1, 1 - par, kind, g, lo, hi)
                                if not (end and i == U - 1):
                                    scores(*nxt, 1)
                                else:
                                    pe.wait_ge(eb_done, b * U + i + 1)
                                if i == 0:
                                    pe.wait_ge(v_kept, b * CB + CB)
                                if c == 0 and not (first and par == 0 and g < 2):
                                    pe.wait_ge(o_kept, b * G + g - 1)
                                for j in range(HG):
                                    hd = (g * HG + j) * D
                                    last_mm = pe.matmul(ps[D * j:D * j + D, (4 + g % 2) * 512:(5 + g % 2) * 512],
                                                        vb[par][:, c, hd:hd + D], pr[i % 2][:, j, :],
                                                        start=(c == 0), stop=(c == CB - 1),
                                                        tile_position=(0, D * j))
                                last_mm.then_inc(pv_done, 1)

                    blocks(0, first=True)
                    with pe.Fori(1, NB // 2 - 1) as it:
                        blocks(it)
                    blocks(NB // 2 - 1, last=True)

                @block.scalar
                def _(act):
                    def keep_v(b, par, g, wait_free):
                        act.wait_ge(v_made, b * CB + g + 1)
                        if wait_free and g == 0:
                            act.wait_ge(pv_done, b * U - U)
                        act.copy(vb[par][:, g, :], bank(ps, 6)).then_inc(v_kept, 1)

                    def keep_kh(b, g, prev_stack):
                        act.wait_ge(k_made, b * G + g + 1)
                        if prev_stack is not None:
                            act.wait_ge(k_stacked[(g + 2) % G], prev_stack)
                        act.activation(khl[g % 2][:, 0, :], bank(ps, 7), ACT.Identity,
                                       bias=s.bk[:, g:g + 1]).then_inc(kh_kept, 1)

                    def exps(b, i, pair, wait_free=True):
                        n = b * U + i
                        act.wait_ge((sa_ready, sb_ready)[pair], n + 1)
                        if wait_free:
                            if pair == 0:
                                act.wait_ge(pv_done, n - 1)
                                act.wait_ge(den_dve, n)
                            else:
                                act.wait_ge(den_pool, n)
                        act.activation(pr[i % 2][:, 2 * pair:2 * pair + 2, :], ps[:, pair * 1024:pair * 1024 + 1024],
                                       ACT.Exp).then_inc((ea_done, eb_done)[pair], 1)

                    def ctx_high(b, par, k):
                        act.copy(ch[par][:, k, :], craw[:, k, :]).then_inc(ch_done, 1)

                    act.wait_ge(ctx0_in, 16)
                    for k in range(NK):
                        ctx_high(0, 0, k)
                    act.wait_ge(wv_in, 16)
                    act.copy(wv[0][:, :, :], wv_raw).then_inc(w_high, 1)
                    act.wait_ge(wk_in, 16)
                    act.copy(wk[0][:, :, :], wk_raw).then_inc(w_high, 1)
                    act.wait_ge(consts, 1)
                    s.ln.scalar_roots(act, 0)
                    act.wait_ge(small_in, 32)
                    keep_v(0, 0, 0, False)
                    keep_kh(0, 0, None)
                    keep_v(0, 0, 1, False)
                    keep_kh(0, 1, None)
                    s.ln.scalar_keep(act, 0, xnT)
                    act.wait_ge(ctx_loaded, 16)
                    for k in range(NK):
                        ctx_high(1, 1, k)
                    for g in range(2, G):
                        keep_kh(0, g, SD)
                        keep_v(0, 0, g, False)

                    def blocks(it, first=False, last=False):
                        for par in range(2):
                            b = it * 2 + par
                            end = last and par == 1
                            for i in range(U):
                                g, c = i // CB, i % CB
                                free = not (first and par == 0 and i < 2)
                                exps(b, i, 0, free)
                                if i in (5, 9, 13) and not last:
                                    if i == 5:
                                        act.wait_ge(ctx_loaded, b * 16 + 32)
                                        act.wait_ge(k_made, b * G + G)
                                    ctx_high(b + 2, par, i // 4 - 1)
                                if c == 2 and not end:
                                    keep_v(b + 1, 1 - par, g, not (first and par == 0))
                                if c == 0:
                                    if i == 0:
                                        if not (first and par == 0):
                                            keep_kh(b, G - 1, b * SD + SD)
                                    elif not end:
                                        q = g - 1
                                        keep_kh(b + 1, q, b * SD + (2 * SD if q >= 2 else SD))
                                exps(b, i, 1, free)

                    blocks(0, first=True)
                    with act.Fori(1, NB // 2 - 1) as it:
                        blocks(it)
                    blocks(NB // 2 - 1, last=True)

                @block.vector
                def _(dve):
                    def keep_kl(b, g):
                        dve.wait_ge(kh_kept, b * G + g + 1)
                        dve.scalar_tensor_tensor(khl[g % 2][:, 1, :], bank(ps, 7), s.bk[:, g:g + 1],
                                                 khl[g % 2][:, 0, :].bitcast(F32), ALU.add,
                                                 ALU.subtract).then_inc(kl_kept, 1)

                    def keep_o(b, g, n):
                        dve.wait_ge(pv_done, n)
                        dve.tensor_tensor(oacc[:, g, :], oacc[:, g, :], bank(ps, 4 + g % 2),
                                          ALU.add).then_inc(o_kept, 1)

                    dve.wait_ge(w_high, 1)
                    dve.tensor_tensor(wv[1][:, :, :], wv_raw, wv[0][:, :, :].bitcast(F32), ALU.subtract)\
                       .then_inc(w_low, 1)
                    dve.wait_ge(w_high, 2)
                    dve.tensor_tensor(wk[1][:, :, :], wk_raw, wk[0][:, :, :].bitcast(F32), ALU.subtract)\
                       .then_inc(w_low, 1)
                    dve.wait_ge(x_in, 16)
                    s.ln.vector_moments(dve, 0, x)
                    s.ln.vector_normalise(dve, 0, x, xn)
                    keep_kl(0, 0)
                    keep_kl(0, 1)
                    s.ln.vector_keep(dve, 0, xnT)
                    dve.wait_ge(w_low, 2)
                    for g in range(G):
                        dve.memset(dacc[:, g, 0:ND, :], 0.0).then_inc(den_cleared, 1)
                        dve.wait_ge(q_done, g + 1)
                        dve.tensor_scalar(qf[:, g, :], bank(ps, g), s.bq[:, g:g + 1], float(D) ** -0.5,
                                          ALU.add, ALU.mult).then_inc(q_copied, 1)
                        dve.wait_ge(q_copied, 2 * g + 1)
                        dve.tensor_copy(qh[:, g, :], qf[:, g, :]).then_inc(q_copied, 1)
                        dve.wait_ge(q_copied, 2 * g + 2)
                        dve.tensor_tensor(ql[:, g, :], qf[:, g, :], qh[:, g, :].bitcast(F32),
                                          ALU.subtract).then_inc(q_split, 1)
                    keep_kl(0, 2)
                    keep_kl(0, 3)
                    dve.memset(oacc[:, :, :], 0.0).then_inc(den_dve, 1)
                    dve.wait_ge(den_cleared, G)

                    def blocks(it, first=False, last=False):
                        for par in range(2):
                            b = it * 2 + par
                            end = last and par == 1
                            for i in range(U):
                                g, c = i // CB, i % CB
                                n = b * U + i
                                if c == 0:
                                    if i == 0:
                                        if not (first and par == 0):
                                            dve.wait_ge(o_kept, b * G - 1)
                                            keep_o(b - 1, G - 1, b * U)
                                            keep_kl(b, G - 1)
                                    else:
                                        if not (first and par == 0 and g == 1):
                                            dve.wait_ge(o_kept, b * G + g - 1)
                                        keep_o(b, g - 1, n)
                                        if not end:
                                            keep_kl(b + 1, g - 1)
                                dve.wait_ge(eb_done, n + 1)
                                dve.wait_ge(den_dve, n + 1)
                                dve.tensor_tensor(dacc[:, g, 0:ND, :], dacc[:, g, 0:ND, :], pr[i % 2][:, 0:ND, :],
                                                  ALU.add).then_inc(den_dve, 1)

                    blocks(0, first=True)
                    with dve.Fori(1, NB // 2 - 1) as it:
                        blocks(it)
                    blocks(NB // 2 - 1, last=True)
                    dve.wait_ge(o_kept, NB * G - 1)
                    keep_o(NB - 1, G - 1, NB * U)

        test_and_output(s, d, oacc, dacc, x1, bad)


def general_keys_values(s, d, kT_d, v_d, even):
    nc, ps = s.nc, s.ps
    with ExitStack() as ctx:
        def sb(name, shape, dt=F32):
            return ctx.enter_context(nc.sbuf_tensor(name, shape, dt))

        def sem(name):
            return ctx.enter_context(nc.semaphore(name))

        wk, wv = sb("g_wk", [P, NK, C]), sb("g_wv", [P, NK, C])
        cx = sb("g_ctx", [P, NK, KB])
        kb, vb = sb("g_k", [P, G, KB]), sb("g_v", [P, CB, C])
        c_in, k_made, v_made, kv_kept, stored = \
            [sem(n) for n in ("g_c_in", "g_k_made", "g_v_made", "g_kv_kept", "g_stored")]
        ctxT = d["ctxT"].rearrange("(k p) n -> p k n", p=P)
        with nc.Block() as block:

            @block.sync
            def _(sp):
                sp.dma_start(wk[:, :, :], d["Wk"].rearrange("(k p) n -> p k n", p=P)).then_inc(stored, 16)
                sp.dma_start(wv[:, :, :], d["Wv"].rearrange("(k p) n -> p k n", p=P)).then_inc(stored, 16)
                with sp.Fori(0, NB) as b:
                    sp.dma_start(cx[:, :, :], ctxT[:, :, bass.ds(b * KB, KB)]).then_inc(c_in, 16)
                    sp.wait_ge(kv_kept, b * (G + CB) + G + CB)
                    sp.dma_start(kT_d.rearrange("(g p) n -> p g n", p=P)[:, :, bass.ds(b * KB, KB)], kb[:, :, :])\
                      .then_inc(stored, 16)
                    sp.dma_start(v_d.rearrange("(b c p) n -> b p c n", p=P, c=CB)[bass.ds(b, 1)].squeeze(0),
                                 vb[:, :, :]).then_inc(stored, 16)
                sp.wait_ge(stored, NB * 32 + 32)

            @block.tensor
            def _(pe):
                pe.wait_ge(stored, 32)
                with pe.Fori(0, NB) as b:
                    pe.wait_ge(c_in, b * 16 + 16)
                    for g in range(G):
                        for k in range(NK):
                            last = pe.matmul(bank(ps, g), wk[:, k, g * P:g * P + P], cx[:, k, :],
                                             start=(k == 0), stop=(k == NK - 1))
                        last.then_inc(k_made, 1)
                    for c in range(CB):
                        for k in range(NK):
                            last = pe.matmul(bank(ps, 4 + c), cx[:, k, c * P:c * P + P], wv[:, k, :],
                                             start=(k == 0), stop=(k == NK - 1))
                        last.then_inc(v_made, 1)

            @block.gpsimd
            def _(pool):
                pool.memset(even[:, :], 1.0 / N)

            @block.scalar
            def _(act):
                with act.Fori(0, NB) as b:
                    act.wait_ge(stored, b * 32 + 32)
                    for g in range(G):
                        act.wait_ge(k_made, b * G + g + 1)
                        act.activation(kb[:, g, :], bank(ps, g), ACT.Identity, bias=s.bk[:, g:g + 1])\
                           .then_inc(kv_kept, 1)

            @block.vector
            def _(dve):
                with dve.Fori(0, NB) as b:
                    dve.wait_ge(stored, b * 32 + 32)
                    for c in range(CB):
                        dve.wait_ge(v_made, b * CB + c + 1)
                        dve.tensor_copy(vb[:, c, :], bank(ps, 4 + c)).then_inc(kv_kept, 1)


def general_heads(s, d, kT_d, v_d, even, oacc):
    nc, ps = s.nc, s.ps
    o_d, m_d = [nc.dram_tensor(n, (C, T), F32).ap() for n in ("o_d", "mean_d")]
    CLAMP = 10000.0
    NS = N // 512
    with ExitStack() as ctx:
        def sb(name, shape, dt=F32):
            return ctx.enter_context(nc.sbuf_tensor(name, shape, dt))

        def sem(name):
            return ctx.enter_context(nc.semaphore(name))

        q, k, v = sb("g_qh", [D, P]), sb("g_kh", [D, N]), sb("g_vh", [P, N // P, D])
        sc, eq, pT = sb("g_sc", [P, N]), sb("g_eq", [P, N]), sb("g_pT", [P, N // P, P])
        ot, mt = sb("g_ot", [D, P]), sb("g_mt", [D, P])
        own, flag, mx, nmx = sb("g_own", [P, 1]), sb("g_flag", [P, 1]), sb("g_mx", [P, 1]), sb("g_nmx", [P, 1])
        den, rden = sb("g_den", [P, 1]), sb("g_rden", [P, 1])
        mean, om = [eq[:, i * G * T:(i + 1) * G * T].rearrange("p (g t) -> p g t", g=G) for i in range(2)]
        mask = sb("g_mask", [P, G, T], I32)
        (loaded, s_made, s_kept, step, max_done, e_done, p_done, t_made, t_kept, o_made, o_kept, stored, back,
         flag_done, count_made) = \
            [sem("g_" + n) for n in ("loaded", "s_made", "s_kept", "step", "max_done", "e_done", "p_done", "t_made",
                                     "t_kept", "o_made", "o_kept", "out", "back", "flag_done", "count_made")]
        STEPS = 7
        with nc.Block() as block:

            @block.sync
            def _(sp):
                with sp.Fori(0, H) as h:
                    with sp.Fori(0, NT) as t:
                        r = h * NT + t
                        sp.wait_ge(stored, r * 32 + 32)
                        sp.dma_start(q[:, :], d["qT_d"][bass.ds(h * D, D), bass.ds(t * P, P)]).then_inc(loaded, 16)
                        sp.dma_start(k[:, :], kT_d[bass.ds(h * D, D), :]).then_inc(loaded, 16)
                        sp.dma_start(v[:, :, :], v_d.rearrange("(c p) n -> p c n", p=P)[:, :, bass.ds(h * D, D)])\
                          .then_inc(loaded, 16)
                        sp.wait_ge(o_kept, r * 2 + 2)
                        sp.dma_start(o_d[bass.ds(h * D, D), bass.ds(t * P, P)], ot[:, :]).then_inc(stored, 16)
                        sp.dma_start(m_d[bass.ds(h * D, D), bass.ds(t * P, P)], mt[:, :]).then_inc(stored, 16)
                sp.wait_ge(stored, H * NT * 32 + 32)
                sp.dma_start(om[:, :, :], o_d.rearrange("(g p) n -> p g n", p=P)).then_inc(back, 16)
                sp.dma_start(mean[:, :, :], m_d.rearrange("(g p) n -> p g n", p=P)).then_inc(back, 16)

            @block.tensor
            def _(pe):
                with pe.Fori(0, H) as h:
                    with pe.Fori(0, NT) as t:
                        r = h * NT + t
                        pe.wait_ge(loaded, r * 48 + 48)
                        for j in range(NS):
                            if j >= 8:
                                pe.wait_ge(s_kept, r * NS + j - 7)
                            pe.matmul(bank(ps, j % 8), q[:, :], k[:, j * 512:j * 512 + 512], start=True,
                                      stop=True).then_inc(s_made, 1)
                        pe.wait_ge(p_done, r + 1)
                        for j in range(NS):
                            if j >= 8:
                                pe.wait_ge(t_kept, r * NS + j - 7)
                            for i in range(4):
                                c = 4 * j + i
                                last = pe.transpose(ps[:, (j % 8) * 512 + i * P:(j % 8) * 512 + i * P + P],
                                                    sc[:, c * P:c * P + P], s.ident[:, :])
                            last.then_inc(t_made, 1)
                        pe.wait_ge(t_kept, r * NS + NS)
                        for c in range(N // P):
                            last = pe.matmul(ps[0:D, 0:P], v[:, c, :], pT[:, c, :], start=(c == 0),
                                             stop=(c == N // P - 1))
                        last.then_inc(o_made, 1)
                        for c in range(N // P):
                            last = pe.matmul(ps[0:D, 512:512 + P], v[:, c, :], even[:, :], start=(c == 0),
                                             stop=(c == N // P - 1))
                        last.then_inc(o_made, 1)
                pe.wait_ge(flag_done, 1)
                pe.matmul(ps[:, 0:1], s.ones[:, :], flag[:, :], start=True, stop=True).then_inc(count_made, 1)

            @block.gpsimd
            def _(pool):
                pool.memset(mt[:, :], 0.0).then_inc(stored, 32)

            @block.scalar
            def _(act):
                with act.Fori(0, H) as h:
                    with act.Fori(0, NT) as t:
                        r = h * NT + t
                        act.wait_ge(max_done, r + 1)
                        act.activation(sc[:, :], sc[:, :], ACT.Exp, bias=nmx[:, 0:1], accum_out=den[:, 0:1])\
                           .then_inc(e_done, 1)

            @block.vector
            def _(dve):
                dve.memset(flag[:, :], 1.0).then_inc(step, 1)
                with dve.Fori(0, H) as h:
                    with dve.Fori(0, NT) as t:
                        r = h * NT + t
                        for j in range(NS):
                            dve.wait_ge(s_made, r * NS + j + 1)
                            dve.tensor_copy(sc[:, j * 512:j * 512 + 512], bank(ps, j % 8)).then_inc(s_kept, 1)
                        dve.wait_ge(s_kept, r * NS + NS)

                        def then(n, ins):
                            ins.then_inc(step, 1)
                            dve.wait_ge(step, r * STEPS + n + 1)

                        then(1, dve.tensor_tensor(eq[:, :], sc[:, :], sc[:, :], ALU.is_equal))
                        then(2, dve.tensor_reduce(own[:, :], eq[:, :], AX.X, ALU.min))
                        then(3, dve.tensor_tensor(flag[:, :], flag[:, :], own[:, :], ALU.min))
                        then(4, dve.tensor_scalar(sc[:, :], sc[:, :], -CLAMP, CLAMP, ALU.max, ALU.min))
                        then(5, dve.tensor_reduce(mx[:, :], sc[:, :], AX.X, ALU.max))
                        dve.tensor_scalar(nmx[:, :], mx[:, :], -1.0, None, ALU.mult).then_inc(max_done, 1)
                        dve.wait_ge(e_done, r + 1)
                        then(6, dve.reciprocal(rden[:, :], den[:, :]))
                        then(7, dve.tensor_scalar(sc[:, :], sc[:, :], rden[:, 0:1], None, ALU.mult))
                        dve.memset(own[:, :], 0.0).then_inc(p_done, 1)
                        for j in range(NS):
                            dve.wait_ge(t_made, r * NS + j + 1)
                            dve.tensor_copy(pT[:, 4 * j:4 * j + 4, :],
                                            bank(ps, j % 8).rearrange("p (c n) -> p c n", n=P)).then_inc(t_kept, 1)
                        dve.wait_ge(o_made, r * 2 + 2)
                        dve.tensor_copy(ot[:, :], ps[0:D, 0:P]).then_inc(o_kept, 1)
                        dve.tensor_copy(mt[:, :], ps[0:D, 512:512 + P]).then_inc(o_kept, 1)
                dve.memset(own[:, :], 0.0).then_inc(flag_done, 1)
                dve.wait_ge(back, 32)
                dve.tensor_copy(oacc[:, :, :], om[:, :, :]).then_inc(step, 1)
                dve.wait_ge(count_made, 1)
                dve.tensor_scalar(mask[:, :, :], ps[:, 0:1].unsqueeze(2).broadcast_to([P, G, T]), float(P), None,
                                  ALU.is_lt).then_inc(step, 1)
                dve.wait_ge(step, H * NT * STEPS + 3)
                dve.copy_predicated(oacc[:, :, :], mask[:, :, :], mean[:, :, :])


def general_cross(s, d, oacc):
    nc = s.nc
    kT_d, v_d = nc.dram_tensor("kT_d", (C, N), F32).ap(), nc.dram_tensor("v_d", (N, C), F32).ap()
    with nc.sbuf_tensor("g_even", [P, P], F32) as even:
        general_keys_values(s, d, kT_d, v_d, even)
        general_heads(s, d, kT_d, v_d, even, oacc)


def test_and_output(s, d, oacc, dacc, x_out, bad):
    nc, ps = s.nc, s.ps
    with ExitStack() as ctx:
        def sb(name, shape, dt=F32):
            return ctx.enter_context(nc.sbuf_tensor(name, shape, dt))

        def sem(name):
            return ctx.enter_context(nc.semaphore(name))

        rden = sb("rden", [P, G, T])
        on = sb("o_divided", [P, G, T])
        low = sb("low", [P, G, T])
        mid = sb("mid", [P, G, T])
        okm = sb("ok_min", [P, 1])
        wo = sb("wo_t", [P, NC, C])
        bo = sb("bo_t", [P, C])
        x = sb("x_t", [P, NT, C])
        wo_in, xb_in = sem("wo_in"), sem("xb_in")
        den_made, rec_done, div_done, o_ready, low_done, mid_done, min_done, sum_made, y_made, out_sum = \
            [sem(n) for n in ("den_made", "rec_done", "div_done", "o_ready_t", "low_done", "mid_done",
                              "min_done", "sum_made", "y_made_t", "out_sum_t")]
        with nc.Block() as block:

            @block.sync
            def _(sp):
                sp.dma_start(wo[:, :, :], d["Wo"].rearrange("(k p) n -> p k n", p=P)).then_inc(wo_in, 16)
                sp.dma_start(bo[:, :], d["bo"].partition_broadcast(P)).then_inc(xb_in, 16)
                sp.dma_start(x[:, :, :], d["x"].rearrange("(t p) c -> p t c", p=P)).then_inc(xb_in, 16)
                for i, n in enumerate("qkvo"):
                    sp.dma_start(s.w[i][:, :, :],
                                 d[f"W{n}T_s"].rearrange("(k p) n -> p k n", p=P)).then_inc(s.w_loaded, 16)

            @block.tensor
            def _(pe):
                for g in range(G):
                    for j in range(HG):
                        last = pe.matmul(ps[D * j:D * j + D, g * 512:g * 512 + T], s.ones[:, 0:D],
                                         dacc[:, g, j, :], start=True, stop=True, tile_position=(0, D * j))
                    last.then_inc(den_made, 1)
                pe.wait_ge(wo_in, 16)
                for g in range(G):
                    pe.wait_ge(o_ready, g + 1)
                    for t in range(NT):
                        last = pe.matmul(bank(ps, 4 + t), on[:, g, t * P:t * P + P], wo[:, g, :],
                                         start=(g == 0), stop=(g == G - 1))
                        if g == G - 1:
                            last.then_inc(y_made, 1)
                pe.wait_ge(min_done, 1)
                pe.matmul(ps[:, 0:1], s.ones[:, :], okm[:, :], start=True, stop=True).then_inc(sum_made, 1)

            @block.gpsimd
            def _(pool):
                pool.tensor_scalar(mid[:, :, :], oacc[:, :, :], 0.0, 0.0, ALU.mult, ALU.is_equal).then_inc(mid_done, 1)
                pool.wait_ge(xb_in, 32)
                for t in range(NT):
                    pool.tensor_tensor(x[:, t, :], x[:, t, :], bo[:, :], ALU.add).then_inc(out_sum, 1)

            @block.vector
            def _(dve):
                for g in range(G):
                    dve.wait_ge(den_made, g + 1)
                    dve.reciprocal(rden[:, g, :], bank(ps, g)).then_inc(rec_done, 1)
                    dve.wait_ge(rec_done, g + 1)
                    dve.tensor_tensor(on[:, g, :], oacc[:, g, :], rden[:, g, :], ALU.mult).then_inc(div_done, 1)
                for g in range(G):
                    dve.tensor_scalar(low[:, g, :], bank(ps, g), DEN_MIN, None, ALU.is_ge).then_inc(low_done, 1)
                for g in range(G):
                    dve.wait_ge(low_done, g + 1)
                    dve.scalar_tensor_tensor(low[:, g, :], bank(ps, g), DEN_MAX, low[:, g, :], ALU.is_le,
                                             ALU.mult).then_inc(low_done, 1)
                dve.wait_ge(low_done, 2 * G)
                dve.wait_ge(mid_done, 1)
                dve.tensor_tensor_reduce(out=low[:, :, :], in0=low[:, :, :], in1=mid[:, :, :], scale=1.0, scalar=2.0,
                                         op0=ALU.add, op1=ALU.min, accum_out=okm[:, :]).then_inc(min_done, 1)
                for t in range(NT):
                    dve.wait_ge(y_made, t + 1)
                    dve.wait_ge(out_sum, t + 1)
                    dve.tensor_tensor(x_out[:, t, :], x[:, t, :], bank(ps, 4 + t), ALU.add)
                dve.wait_ge(sum_made, 1)
                dve.tensor_scalar(bad[:, :], ps[:, 0:1], 2.0 * P, None, ALU.is_lt)

            @block.scalar
            def _(act):
                for g in range(G):
                    act.wait_ge(div_done, g + 1)
                    act.activation(on[:, g, :], on[:, g, :], ACT.Identity, bias=s.bv[:, g:g + 1])\
                       .then_inc(o_ready, 1)


def cross_output(s, d, oacc, x_out):
    nc, ps = s.nc, s.ps
    with ExitStack() as ctx:
        def sb(name, shape, dt=F32):
            return ctx.enter_context(nc.sbuf_tensor(name, shape, dt))

        def sem(name):
            return ctx.enter_context(nc.semaphore(name))

        wo = sb("wo_x", [P, NC, C])
        bo = sb("bo_x", [P, C])
        x = sb("x_again", [P, NT, C])
        loaded, o_ready, y_made, out_sum = [sem(n) for n in ("f_loaded", "o_ready", "y_made", "out_sum")]
        with nc.Block() as block:

            @block.sync
            def _(sp):
                sp.dma_start(wo[:, :, :], d["Wo"].rearrange("(k p) n -> p k n", p=P)).then_inc(loaded, 16)
                sp.dma_start(bo[:, :], d["bo"].partition_broadcast(P)).then_inc(loaded, 16)
                sp.dma_start(x[:, :, :], d["x"].rearrange("(t p) c -> p t c", p=P)).then_inc(loaded, 16)

            @block.tensor
            def _(pe):
                pe.wait_ge(loaded, 48)
                pe.wait_ge(o_ready, G)
                for t in range(NT):
                    for g in range(G):
                        last = pe.matmul(bank(ps, t), oacc[:, g, t * P:t * P + P], wo[:, g, :],
                                         start=(g == 0), stop=(g == G - 1))
                    last.then_inc(y_made, 1)

            @block.vector
            def _(dve):
                for t in range(NT):
                    dve.wait_ge(y_made, t + 1)
                    dve.wait_ge(out_sum, t + 1)
                    dve.tensor_tensor(x_out[:, t, :], x[:, t, :], bank(ps, t), ALU.add)

            @block.scalar
            def _(act):
                for g in range(G):
                    act.activation(oacc[:, g, :], oacc[:, g, :], ACT.Identity, bias=s.bv[:, g:g + 1])\
                       .then_inc(o_ready, 1)

            @block.gpsimd
            def _(pool):
                pool.wait_ge(loaded, 48)
                for t in range(NT):
                    pool.tensor_tensor(x[:, t, :], x[:, t, :], bo[:, :], ALU.add).then_inc(out_sum, 1)


def self_attention(s, d, x, x_out):
    nc, ps = s.nc, s.ps
    with ExitStack() as ctx:
        def sb(name, shape, dt=F32):
            return ctx.enter_context(nc.sbuf_tensor(name, shape, dt))

        def sem(name):
            return ctx.enter_context(nc.semaphore(name))

        w = s.w
        strip = sb("strip", [P, T])
        qs = sb("q_stack_s", [P, HG, G, T], F32R)
        ks = sb("k_stack_s", [P, HG, G, T], F32R)
        v = sb("v_s", [P, NT, C])
        qh, ql = sb("qh_s", [P, G, T], F32R), sb("ql_s", [P, G, T], F32R)
        khl = sb("khl_s", [P, 2, G, T], F32R)
        early = ctx.enter_context(ExitStack())

        def eb(name, shape, dt=F32):
            return early.enter_context(nc.sbuf_tensor(name, shape, dt))

        xn_at = next_place(nc)
        xn = eb("xn2", [P, NT, C])
        qf = nc.alloc_sbuf_tensor_at("qf_s", [P, G, T], F32, offset=xn_at)
        xnT = [eb(f"xnT2_{i}", [P, NC, T], F32R) for i in "hl"]
        wh = [eb(f"w{n}_high", [P, NC, C], F32R) for n in "qkv"]
        wl = [nc.alloc_sbuf_tensor_at(f"w{n}_low", [P, NC, C], F32R, offset=s.wide_at + 4 * i * NC * C)
              for i, n in enumerate("qkv")]
        wh_done, wl_done, xh_kept, xl_kept = [sem(n) for n in ("wh_done_s", "wl_done_s", "xh_kept", "xl_kept")]
        strip_in = sem("strip_in")

        first = [0, P, 512, 1024]
        width = [P * (t + 1) for t in range(NT)]
        kept = [sum(width[:t]) for t in range(NT)]
        tot = sum(width)
        tfirst = [0, 1024, 512, 512 + 256]
        twidth = [T - P * c for c in range(NT)]
        tkept = [sum(twidth[:c]) for c in range(NT)]

        proj = sem("s_proj")
        q_step, k_step, ql_done, kl_done = [sem(n) for n in ("q_step", "k_step_s", "ql_done", "kl_done_s")]
        v_kept = sem("v_kept_s")
        q_in = [sem(f"q_in{g}") for g in range(G // 2)]
        k_in = [sem(f"k_in{g}") for g in range(G // 2)]
        bias_done, s_made, m_done, nm_done, e_done, r_done, n_done, np_done = \
            [sem(n) for n in ("bias_done", "s_made", "m_done", "nm_done", "e_done", "r_done", "n_done", "np_done")]
        t_made, t_kept_a, t_kept_d, o_made, o_kept, y_made, x_done = \
            [sem(n) for n in ("t_made", "t_kept_a", "t_kept_d", "o_made_s", "o_kept_s", "y_made_s", "x_done_s")]

        def stack_q(eng, g):
            eng.wait_ge(ql_done, g + 2)
            for j in range(HG):
                for half, part in enumerate((qh, ql)):
                    src = part[D * j:D * j + D, g:g + 2, :].bitcast(F32).rearrange("p g t -> p (g t)")
                    eng.dma_start(qs[64 * half:64 * half + 64, j, g:g + 2, :].bitcast(F32)
                                  .rearrange("p g t -> p (g t)"),
                                  src.unsqueeze(1).broadcast_to([D, 2, 2 * T])).then_inc(q_in[g // 2], 16)

        def stack_k(eng, g):
            eng.wait_ge(kl_done, g + 2)
            for j in range(HG):
                for half in range(2):
                    eng.dma_start(ks[64 * half:64 * half + 64, j, g:g + 2, :].bitcast(F32)
                                  .rearrange("p g t -> p (g t)"),
                                  khl[D * j:D * j + D, :, g:g + 2, :].bitcast(F32)
                                  .rearrange("p s g t -> p s (g t)")).then_inc(k_in[g // 2], 16)

        with nc.Block() as block:

            @block.tensor
            def _(pe):
                s.ln.tensor_turn(pe, 1, xn)
                pe.wait_ge(xl_kept, NC)
                parts = ((0, 0), (0, 1), (1, 0))
                for g in range(G):
                    for i in range(2):
                        if g == 0:
                            pe.wait_ge(wl_done, i + 1)
                        for k in range(NC):
                            for m, (a, b) in enumerate(parts):
                                last = pe.matmul(bank(ps, 2 * g + i), (wh, wl)[a][i][:, k, g * P:g * P + P],
                                                 xnT[b][:, k, :], start=(k == 0 and m == 0),
                                                 stop=(k == NC - 1 and m == 2))
                        last.then_inc(proj, 1)
                pe.wait_ge(wl_done, 3)
                for t in range(NT):
                    pe.wait_ge((ql_done, kl_done)[t % 2], t // 2 + 1)
                    for k in range(NC):
                        for m, (a, b) in enumerate(parts):
                            last = pe.matmul(bank(ps, t), xnT[b][:, k, t * P:t * P + P], (wh, wl)[a][2][:, k, :],
                                             start=(k == 0 and m == 0), stop=(k == NC - 1 and m == 2))
                    last.then_inc(proj, 1)

            @block.vector
            def _(dve):
                s.ln.vector_moments(dve, 1, x)
                s.ln.vector_normalise(dve, 1, x, xn)
                for k in range(NC):
                    dve.wait_ge(xh_kept, k + 1)
                    dve.tensor_tensor(xnT[1][:, k, :], bank(ps, k), xnT[0][:, k, :].bitcast(F32), ALU.subtract)\
                       .then_inc(xl_kept, 1)
                for g in range(G):
                    dve.wait_ge(proj, 2 * g + 1)
                    dve.tensor_scalar(qf[:, g, :], bank(ps, 2 * g), float(D) ** -0.5, None, ALU.mult)\
                       .then_inc(q_step, 1)
                    dve.wait_ge(q_step, 2 * g + 1)
                    dve.tensor_copy(qh[:, g, :], qf[:, g, :]).then_inc(q_step, 1)
                    dve.wait_ge(q_step, 2 * g + 2)
                    dve.tensor_tensor(ql[:, g, :], qf[:, g, :], qh[:, g, :].bitcast(F32), ALU.subtract)\
                       .then_inc(ql_done, 1)
                    dve.wait_ge(k_step, g + 1)
                    dve.tensor_tensor(khl[:, 1, g, :], bank(ps, 2 * g + 1), khl[:, 0, g, :].bitcast(F32),
                                      ALU.subtract).then_inc(kl_done, 1)

            @block.scalar
            def _(act):
                act.wait_ge(s.w_loaded, 64)
                act.copy(wh[0][:, :, :], w[0][:, :, :]).then_inc(wh_done, 1)
                s.ln.scalar_roots(act, 1)
                act.copy(wh[1][:, :, :], w[1][:, :, :]).then_inc(wh_done, 1)
                for k in range(NC):
                    act.wait_ge(s.ln.turned, NC + k + 1)
                    act.copy(xnT[0][:, k, :], bank(ps, k)).then_inc(xh_kept, 1)
                act.copy(wh[2][:, :, :], w[2][:, :, :]).then_inc(wh_done, 1)
                for g in range(G):
                    act.wait_ge(proj, 2 * g + 2)
                    act.copy(khl[:, 0, g, :], bank(ps, 2 * g + 1)).then_inc(k_step, 1)
                for t in range(NT):
                    act.wait_ge(proj, 2 * G + t + 1)
                    act.copy(v[:, t, :], bank(ps, t)).then_inc(v_kept, 1)

            @block.sync
            def _(sp):
                sp.dma_start(strip[:, :], d["strip"]).then_inc(strip_in, 16)
                stack_q(sp, 0)

            @block.gpsimd
            def _(pool):
                for i in range(3):
                    pool.wait_ge(wh_done, i + 1)
                    pool.tensor_tensor(wl[i][:, :, :], w[i][:, :, :], wh[i][:, :, :].bitcast(F32), ALU.subtract)\
                        .then_inc(wl_done, 1)
                stack_k(pool, 0)

        early.close()
        SR = 4
        sc = [sb(f"scores{i}", [P, tot]) for i in range(SR)]
        pT = [nc.alloc_sbuf_tensor_at("probsT0", [P, HG, tot], F32, offset=s.wide_at), sb("probsT1", [P, HG, tot])]
        bias = [sb(f"bias{i}", [P, T]) for i in range(SR)]
        mx = sb("mx", [P, H, NT])
        nmx = sb("nmx", [P, H, NT])
        den = sb("den", [P, H, NT])
        rden = sb("rden_s", [P, H, NT])
        oT = sb("oT", [P, G, T])

        with nc.Block() as block:

            @block.sync
            def _(sp):
                stack_q(sp, 2)
                stack_k(sp, 2)

            @block.tensor
            def _(pe):
                def scores(h):
                    if h % (2 * HG) == 0:
                        pe.wait_ge(q_in[h // (2 * HG)], 128)
                        pe.wait_ge(k_in[h // (2 * HG)], 128)
                    if h:
                        pe.wait_ge(m_done, h * NT)
                    for t in range(NT):
                        pe.matmul(ps[:, first[t]:first[t] + width[t]], qs[:, h % HG, h // HG, t * P:t * P + P],
                                  ks[:, h % HG, h // HG, 0:width[t]], start=True, stop=True).then_inc(s_made, 1)

                def turn(h):
                    pe.wait_ge(n_done, h * (NT - 1) + NT - 1)
                    pe.wait_ge(np_done, h + 1)
                    if h:
                        pe.wait_ge(t_kept_a, 2 * h)
                        pe.wait_ge(t_kept_d, h)
                    for c in range(NT):
                        for t in range(c, NT):
                            at = 1536 + tfirst[c] + (t - c) * P
                            last = pe.transpose(ps[:, at:at + P], sc[h % SR][:, kept[t] + c * P:kept[t] + c * P + P],
                                                s.ident[:, :])
                    last.then_inc(t_made, 1)

                def weighted(g):
                    pe.wait_ge(t_kept_a, 2 * (g * HG + HG))
                    pe.wait_ge(t_kept_d, g * HG + HG)
                    if g >= 2:
                        pe.wait_ge(o_kept, g - 1)
                    b = 6 + g % 2
                    for c in range(NT):
                        for j in range(HG):
                            hd = (g * HG + j) * D
                            last = pe.matmul(ps[D * j:D * j + D, b * 512 + c * P:b * 512 + T], v[:, c, hd:hd + D],
                                             pT[g % 2][:, j, tkept[c]:tkept[c] + twidth[c]],
                                             start=(c == 0), stop=(c == NT - 1), tile_position=(0, D * j),
                                             skip_group_check=True)
                    last.then_inc(o_made, 1)

                scores(0)
                scores(1)
                for h in range(H):
                    if h + 2 < H:
                        scores(h + 2)
                    turn(h)
                    if h % HG == 0 and h:
                        weighted(h // HG - 1)
                weighted(G - 1)
                pe.wait_ge(o_kept, G)
                for t in range(NT):
                    for g in range(G):
                        last = pe.matmul(bank(ps, t), oT[:, g, t * P:t * P + P], w[3][:, g, :],
                                         start=(g == 0), stop=(g == G - 1))
                    last.then_inc(y_made, 1)

            @block.vector
            def _(dve):
                def finish(h):
                    dve.wait_ge(e_done, h * NT + NT)
                    dve.reciprocal(rden[:, h, :], den[:, h, :]).then_inc(r_done, 1)
                    dve.wait_ge(r_done, h + 1)
                    for t in (0, 1, 3):
                        p = sc[h % SR][:, kept[t]:kept[t] + width[t]]
                        dve.tensor_scalar(p, p, rden[:, h, t:t + 1], None, ALU.mult).then_inc(n_done, 1)

                def keep(h):
                    dve.wait_ge(t_made, h + 1)
                    if h >= 2 * HG and h % HG == 0:
                        dve.wait_ge(o_made, h // HG - 1)
                    g, j = h // HG, h % HG
                    dve.tensor_copy(pT[g % 2][:, j, 0:512], ps[:, 1536:2048]).then_inc(t_kept_d, 1)

                def keep_o(g):
                    dve.wait_ge(o_made, g + 1)
                    dve.tensor_copy(oT[:, g, :], bank(ps, 6 + g % 2)).then_inc(o_kept, 1)

                for h in range(H):
                    dve.wait_ge(bias_done, h + 1)
                    if h >= SR:
                        dve.wait_ge(t_made, h - SR + 1)
                    for t in range(NT):
                        dve.wait_ge(s_made, h * NT + max(t, 1) + 1)
                        dve.tensor_tensor_reduce(out=sc[h % SR][:, kept[t]:kept[t] + width[t]],
                                                 in0=ps[:, first[t]:first[t] + width[t]],
                                                 in1=bias[h % SR][:, T - width[t]:T], scale=1.0, scalar=NEG,
                                                 op0=ALU.add, op1=ALU.max, accum_out=mx[:, h, t:t + 1])\
                           .then_inc(m_done, 1)
                    dve.wait_ge(m_done, h * NT + NT)
                    dve.tensor_scalar(nmx[:, h, :], mx[:, h, :], -1.0, None, ALU.mult).then_inc(nm_done, 1)
                    if h:
                        finish(h - 1)
                    if h >= 2:
                        keep(h - 2)
                    if h % HG == 2 and h > HG:
                        keep_o(h // HG - 1)
                finish(H - 1)
                keep(H - 2)
                keep(H - 1)
                keep_o(G - 1)
                for t in range(NT):
                    dve.wait_ge(y_made, t + 1)
                    dve.tensor_tensor(x_out[:, t, :], x[:, t, :], bank(ps, t), ALU.add).then_inc(x_done, 1)
                    dve.wait_ge(x_done, t + 1)
                    s.ln.vector_moments(dve, 2, x_out, t)

            @block.scalar
            def _(act):
                def keep(h):
                    g, j = h // HG, h % HG
                    act.wait_ge(t_made, h + 1)
                    if h >= 2 * HG and h % HG == 0:
                        act.wait_ge(o_made, h // HG - 1)
                    act.copy(pT[g % 2][:, j, 512:512 + 384], ps[:, 1536 + 1024:1536 + 1024 + 384])\
                       .then_inc(t_kept_a, 1)
                    act.copy(pT[g % 2][:, j, 896:1280], ps[:, 1536 + 512:1536 + 512 + 384]).then_inc(t_kept_a, 1)

                for h in range(H):
                    act.wait_ge(nm_done, h + 1)
                    for t in range(NT):
                        p = sc[h % SR][:, kept[t]:kept[t] + width[t]]
                        act.activation(p, p, ACT.Exp, bias=nmx[:, h, t:t + 1],
                                       accum_out=den[:, h, t:t + 1]).then_inc(e_done, 1)
                    if h:
                        keep(h - 1)
                keep(H - 1)

            @block.gpsimd
            def _(pool):
                def scale(h):
                    pool.wait_ge(r_done, h + 1)
                    p = sc[h % SR][:, kept[2]:kept[2] + width[2]]
                    pool.tensor_scalar(p, p, rden[:, h, 2:3], None, ALU.mult).then_inc(np_done, 1)

                pool.wait_ge(strip_in, 16)
                for h in range(H):
                    if h >= SR:
                        pool.wait_ge(m_done, (h - SR + 1) * NT)
                    pool.tensor_scalar(bias[h % SR][:, :], strip[:, :], 2.0 ** (-8.0 / H * (h + 1)), None, ALU.mult)\
                        .then_inc(bias_done, 1)
                    if h >= 2:
                        scale(h - 2)
                scale(H - 2)
                scale(H - 1)


NEG = -3.0e38


def feed_forward(s, d, x, x_out):
    nc, ps = s.nc, s.ps
    E, HID = 8, 2048
    HC = HID // 512
    TILES = T // P + E
    with ExitStack() as ctx:
        def sb(name, shape, dt=F32):
            return ctx.enter_context(nc.sbuf_tensor(name, shape, dt))

        def sem(name):
            return ctx.enter_context(nc.semaphore(name))

        xn = sb("xn3", [P, NT, C])
        xh, xl = sb("xs_h", [P, NT, C], F32R), sb("xs_l", [P, NT, C], F32R)
        pos = sb("pos", [P, NT])
        slot = sb("slot", [P, 1])
        table = sb("table", [1, TILES + 1], I32)
        iota = sb("iota", [P, P])
        w1 = [sb(f"w1_{i}", [P, NC, 512]) for i in range(HC)]
        w2 = [sb(f"w2_{i}", [P, 4, C]) for i in range(HC)]
        b1, b2 = sb("b1", [P, HID // P]), sb("b2", [P, C])
        loaded, table_done = sem("r_loaded"), sem("table_done")
        WC = 2 * HC
        w_in = [sem(f"w_in{i}") for i in range(WC)]
        raw = w1 + w2
        w1_d = d["w1"].rearrange("e (k p) h -> e p k h", p=P)
        w2_d = d["w2"].rearrange("e (j p) n -> e p j n", p=P)

        def chunk(e, i):
            if i < HC:
                return w1_d[bass.ds(e, 1), :, :, i * 512:i * 512 + 512].squeeze(0)
            return w2_d[bass.ds(e, 1), :, 4 * (i - HC):4 * (i - HC) + 4, :].squeeze(0)

        with ExitStack() as rc:
            def rb(name, shape, dt=F32):
                return rc.enter_context(nc.sbuf_tensor(name, shape, dt))

            xnT = rb("xnT3", [P, NC, T])
            gw, gb = rb("gate_w", [P, NC, E]), rb("gate_b", [P, E])
            tri, iota8, iotaT = rb("tri", [P, P]), rb("iota8", [P, E]), rb("iotaT", [P, TILES])
            A = [rb(f"route{i}", [P, NT, E]) for i in range(12)]
            (lg, ex, sco, e1, c1, o1, s2, c2, oh, pre, rk, tmp) = A
            S = [rb(f"tok{i}", [P, NT]) for i in range(11)]
            (m, sm, rs, m1, i1, m2, i2, v1, v2, es, wt) = S
            sums = rb("sums", [P, E])
            cum = [rb(f"cum{i}", [P, 2 * E]) for i in range(4)]
            nt4 = rb("nt4", [P, E, 4])
            cmp = rb("cmp", [P, TILES, E])
            tabf = rb("tabf", [P, TILES + 1])
            step, lg_made, shifted, exped, rank_made, oh_ready, scaled, xh_done = \
                [rc.enter_context(nc.semaphore(n)) for n in ("r_step", "lg_made", "shifted", "exped", "rank_made",
                                                             "oh_ready", "xw_scaled", "xh_done")]

            def row(t):
                return t[:, :].unsqueeze(2).broadcast_to([P, NT, E])

            i8 = iota8[:, :].unsqueeze(1).broadcast_to([P, NT, E])
            with nc.Block() as block:

                @block.sync
                def _(sp):
                    sp.dma_start(gw[:, :, :], d["gate_w"].rearrange("(k p) e -> p k e", p=P)).then_inc(loaded, 16)
                    sp.dma_start(gb[:, :], d["gate_b"].partition_broadcast(P)).then_inc(loaded, 16)
                    sp.dma_start(tri[:, :], d["tri"]).then_inc(loaded, 16)
                    sp.dma_start(iota[:, :], d["iota"].partition_broadcast(P)).then_inc(loaded, 16)
                    sp.dma_start(slot[:, :], d["slots"]).then_inc(loaded, 16)
                    sp.dma_start(iota8[:, :], d["iota"][0:E].partition_broadcast(P)).then_inc(loaded, 16)
                    sp.dma_start(iotaT[:, :], d["iota"][0:TILES].partition_broadcast(P)).then_inc(loaded, 16)
                    sp.wait_ge(table_done, 1)
                    e = sp.value_load(table[0:1, 0:1], min_val=0, max_val=E - 1)
                    for i in range(WC):
                        sp.dma_start(raw[i][:, :, :], chunk(e, i)).then_inc(w_in[i], 16)

                @block.tensor
                def _(pe):
                    s.ln.tensor_turn(pe, 2, xn)
                    pe.wait_ge(loaded, 112)
                    s.ln.wait_kept(pe, 1)
                    for t in range(NT):
                        for k in range(NC):
                            last = pe.matmul(ps[:, t * E:t * E + E], xnT[:, k, t * P:t * P + P], gw[:, k, :],
                                             start=(k == 0), stop=(k == NC - 1))
                    last.then_inc(lg_made, 1)
                    pe.wait_ge(oh_ready, 1)
                    pe.matmul(ps[:, 512:512 + NT * E], s.ones[:, :], pre[:, :, :], start=True, stop=False)
                    pe.matmul(ps[:, 512:512 + NT * E], tri[:, :], oh[:, :, :], start=False, stop=True)
                    pe.matmul(ps[:, 1024:1024 + E], s.ones[:, :], sums[:, :], start=True,
                              stop=True).then_inc(rank_made, 1)

                @block.scalar
                def _(act):
                    s.ln.scalar_roots(act, 2)
                    s.ln.scalar_keep(act, 2, xnT)
                    act.wait_ge(shifted, 1)
                    act.activation(ex[:, :, :], tmp[:, :, :], ACT.Exp).then_inc(exped, 1)
                    for t in range(NT):
                        act.wait_ge(scaled, t + 1)
                        act.copy(xh[:, t, :], xn[:, t, :]).then_inc(xh_done, 1)

                @block.gpsimd
                def _(pool):
                    for t in range(2):
                        pool.wait_ge(xh_done, t + 1)
                        pool.tensor_tensor(xl[:, t, :], xn[:, t, :], xh[:, t, :].bitcast(F32), ALU.subtract)

                @block.vector
                def _(dve):
                    n = [0]

                    def then(ins):
                        n[0] += 1
                        ins.then_inc(step, 1)
                        dve.wait_ge(step, n[0])

                    s.ln.vector_normalise(dve, 2, x, xn)
                    s.ln.vector_keep(dve, 2, xnT)
                    dve.wait_ge(lg_made, 1)
                    psl = ps[:, 0:NT * E].rearrange("p (t e) -> p t e", e=E)
                    then(dve.tensor_tensor(lg[:, :, :], psl, gb[:, :].unsqueeze(1).broadcast_to([P, NT, E]), ALU.add))
                    then(dve.tensor_reduce(m[:, :], lg[:, :, :], AX.X, ALU.max))
                    dve.tensor_tensor(tmp[:, :, :], lg[:, :, :], row(m), ALU.subtract).then_inc(shifted, 1)
                    dve.wait_ge(exped, 1)
                    then(dve.tensor_reduce(sm[:, :], ex[:, :, :], AX.X, ALU.add))
                    then(dve.reciprocal(rs[:, :], sm[:, :]))
                    then(dve.tensor_tensor(sco[:, :, :], ex[:, :, :], row(rs), ALU.mult))

                    def top(src, val, idx, eq, cand):
                        then(dve.tensor_reduce(val[:, :], src[:, :, :], AX.X, ALU.max))
                        then(dve.tensor_tensor(eq[:, :, :], src[:, :, :], row(val), ALU.is_equal))
                        then(dve.scalar_tensor_tensor(cand[:, :, :], eq[:, :, :], -float(E), i8, ALU.mult, ALU.add))
                        then(dve.tensor_reduce(idx[:, :], cand[:, :, :], AX.X, ALU.min))
                        then(dve.tensor_scalar(idx[:, :], idx[:, :], float(E), None, ALU.add))

                    top(sco, m1, i1, e1, c1)
                    then(dve.tensor_tensor(o1[:, :, :], i8, row(i1), ALU.is_equal))
                    then(dve.scalar_tensor_tensor(s2[:, :, :], o1[:, :, :], -2.0, sco[:, :, :], ALU.mult, ALU.add))
                    top(s2, m2, i2, e1, c2)
                    for val, idx, v in ((m1, i1, v1), (m2, i2, v2)):
                        then(dve.tensor_scalar(v[:, :], val[:, :], 0.0, None, ALU.is_gt))
                        then(dve.scalar_tensor_tensor(v[:, :], idx[:, :], 1.0, v[:, :], ALU.add, ALU.mult))
                    then(dve.tensor_tensor(es[:, :], v1[:, :], v2[:, :], ALU.max))
                    then(dve.tensor_scalar(es[:, :], es[:, :], -1.0, None, ALU.add))
                    then(dve.tensor_tensor(oh[:, :, :], i8, row(es), ALU.is_equal))
                    then(dve.memset(pre[:, 0, :], 0.0))
                    for t in range(1, NT):
                        then(dve.tensor_tensor(pre[:, t, :], pre[:, t - 1, :], oh[:, t - 1, :], ALU.add))
                    dve.tensor_tensor(sums[:, :], pre[:, NT - 1, :], oh[:, NT - 1, :], ALU.add).then_inc(oh_ready, 1)
                    then(dve.tensor_tensor(tmp[:, :, :], sco[:, :, :], oh[:, :, :], ALU.mult))
                    then(dve.tensor_reduce(wt[:, :], tmp[:, :, :], AX.X, ALU.add))
                    dve.wait_ge(rank_made, 1)
                    for j in range(4):
                        then(dve.tensor_scalar(nt4[:, :, j], ps[:, 1024:1024 + E], float(P * j), None, ALU.is_gt))
                    for c in cum:
                        then(dve.memset(c[:, :], 0.0))
                    then(dve.tensor_reduce(cum[0][:, E:2 * E], nt4[:, :, :], AX.X, ALU.add))
                    for i in range(3):
                        then(dve.tensor_tensor(cum[i + 1][:, E:2 * E], cum[i][:, E:2 * E],
                                               cum[i][:, E - 2 ** i:2 * E - 2 ** i], ALU.add))
                    incl = cum[3][:, E:2 * E].unsqueeze(1).broadcast_to([P, TILES, E])
                    then(dve.tensor_tensor(cmp[:, :, :], incl, iotaT[:, :].unsqueeze(2).broadcast_to([P, TILES, E]),
                                           ALU.is_le))
                    then(dve.tensor_reduce(tabf[:, 0:TILES], cmp[:, :, :], AX.X, ALU.add))
                    then(dve.tensor_scalar(tabf[:, 0:TILES], tabf[:, 0:TILES], float(E - 1), None, ALU.min))
                    then(dve.tensor_scalar(tabf[:, TILES:TILES + 1], cum[3][:, 2 * E - 1:2 * E], 2.0, None, ALU.max))
                    dve.tensor_copy(table[:, :], tabf[0:1, :]).then_inc(table_done, 1)
                    for t in range(NT):
                        dve.tensor_scalar(xn[:, t, :], xn[:, t, :], wt[:, t:t + 1], None, ALU.mult)\
                           .then_inc(scaled, 1)
                    base = cum[3][:, E - 1:2 * E - 1].unsqueeze(1).broadcast_to([P, NT, E])
                    then(dve.tensor_scalar(rk[:, :, :], ps[:, 512:512 + NT * E].rearrange("p (t e) -> p t e", e=E),
                                           1.0, None, ALU.add))
                    then(dve.scalar_tensor_tensor(tmp[:, :, :], base, float(P), rk[:, :, :], ALU.mult, ALU.add))
                    then(dve.tensor_tensor(tmp[:, :, :], tmp[:, :, :], oh[:, :, :], ALU.mult))
                    then(dve.tensor_reduce(pos[:, :], tmp[:, :, :], AX.X, ALU.add))
                    then(dve.tensor_scalar(pos[:, :], pos[:, :], -1.0, None, ALU.add))
                    for t in range(2, NT):
                        dve.wait_ge(xh_done, t + 1)
                        dve.tensor_tensor(xl[:, t, :], xn[:, t, :], xh[:, t, :].bitcast(F32), ALU.subtract)

        with ExitStack() as ec:
            def eb(name, shape, dt=F32):
                return ec.enter_context(nc.sbuf_tensor(name, shape, dt))

            def esem(name):
                return ec.enter_context(nc.semaphore(name))

            WS = HC
            POOL_LOW = (1, HC - 1, WC - 1)
            perm = eb("perm", [P, NT, P], F32R)
            permT = eb("permT", [P, NT, P], F32R)
            posB = eb("pos_row", [P, T])
            xr = eb("xg_rows", [P, C])
            xg = [eb(f"xg_{i}", [P, NC, P], F32R) for i in "hl"]
            hs = [eb(f"hs{i}", [P, 512]) for i in range(2)]
            hf = [eb(f"hf{i}", [P, 4, P]) for i in range(2)]
            hT = [eb(f"hT_{i}", [P, HID // P, P], F32R) for i in "hl"]
            y, yh, yl = eb("y", [P, C]), eb("yh", [P, C], F32R), eb("yl", [P, C], F32R)
            wh = [eb(f"wsplit_h{i}", [P, 4, 512], F32R) for i in range(WS)]
            wl = [eb(f"wsplit_l{i}", [P, 4, 512], F32R) for i in range(WS)]
            b1_in, b2_in = esem("b1_in"), esem("b2_in")
            (wh_done, wl_dve, wl_pool, pos_down, perm_done, xg_made, xgh_kept, xgl_kept, xr_made, xr_kept, pt_kept, h_made,
             h_kept, ht_made, hf_kept, hh_kept, hl_kept, w2_used, y_done, yh_done, yl_done, sc_made, sc_added,
             diag_done, posB_made) = \
                [esem(n) for n in ("wh_done", "wl_dve", "wl_pool", "pos_down", "perm_done", "xg_made", "xgh_kept",
                                   "xgl_kept", "xr_made", "xr_kept", "pt_kept", "h_made", "h_kept", "ht_made", "hf_kept",
                                   "hh_kept", "hl_kept", "w2_used", "y_done", "yh_done", "yl_done", "sc_made",
                                   "sc_added", "diag_done", "posB_made")]
            ND = WC - len(POOL_LOW)
            sc_bank = (7, 1, 2, 3)

            def low_order(i):
                mine = [c for c in range(WC) if (c in POOL_LOW) == (i in POOL_LOW)]
                return mine.index(i) + 1

            with nc.Block() as block:

                def tiles(eng):
                    return eng.value_load(table[0:1, TILES:TILES + 1], min_val=2, max_val=TILES - 1)

                @block.sync
                def _(sp):
                    def load(e, i, n):
                        lows = (wl_pool, len(POOL_LOW)) if i in POOL_LOW else (wl_dve, ND)
                        sp.wait_ge(lows[0], n * lows[1] + low_order(i))
                        sp.dma_start(raw[i][:, :, :], chunk(e, i)).then_inc(w_in[i], 16)

                    def expert(at):
                        return sp.value_load(table[0:1, at], min_val=0, max_val=E - 1)

                    following = expert(slice(1, 2))
                    for i in range(HC):
                        load(following, i, 0)
                    with sp.Fori(1, tiles(sp)) as it:
                        e, following = expert(bass.ds(it, 1)), expert(bass.ds(it + 1, 1))
                        for i in range(HC, WC):
                            load(e, i, it - 1)
                        for i in range(HC):
                            load(following, i, it)

                @block.gpsimd
                def _(pool):
                    def low(n, i):
                        pool.wait_ge(wh_done, n * WC + i + 1)
                        pool.tensor_tensor(wl[i % WS][:, :, :], raw[i][:, :, :], wh[i % WS][:, :, :].bitcast(F32),
                                           ALU.subtract).then_inc(wl_pool, 1)

                    def biases(at):
                        e = pool.value_load(table[0:1, at], min_val=0, max_val=E - 1)
                        return (d["b1c"][bass.ds(e, 1), :, :].squeeze(0),
                                d["b2"][bass.ds(e, 1), :].broadcast_to([P, C]))

                    b1_src, b2_src = biases(slice(0, 1))
                    pool.dma_start(b1[:, :], b1_src).then_inc(b1_in, 16)
                    pool.dma_start(b2[:, :], b2_src).then_inc(b2_in, 16)
                    low(0, 1)
                    low(0, HC - 1)
                    with pool.Fori(0, tiles(pool)) as it:
                        low(it, WC - 1)
                        b1_src, b2_src = biases(bass.ds(it + 1, 1))
                        pool.wait_ge(hf_kept, it * HC + HC)
                        pool.dma_start(b1[:, :], b1_src).then_inc(b1_in, 16)
                        low(it + 1, 1)
                        low(it + 1, HC - 1)
                        pool.wait_ge(y_done, it + 1)
                        pool.dma_start(b2[:, :], b2_src).then_inc(b2_in, 16)

                @block.tensor
                def _(pe):
                    def gather(it):
                        pe.wait_ge(perm_done, it * NT + NT)
                        for t in range(NT):
                            for i, part in enumerate((xh, xl)):
                                last = pe.matmul(bank(ps, 5), perm[:, t, :], part[:, t, :],
                                                 start=(t == 0 and i == 0), stop=(t == NT - 1 and i == 1))
                        last.then_inc(xr_made, 1)

                    def turn_x(it):
                        pe.wait_ge(xr_kept, it + 1)
                        for k in range(NC):
                            last = pe.transpose(ps[:, 6 * 512 + k * P:6 * 512 + k * P + P], xr[:, k * P:k * P + P],
                                                s.ident[:, :])
                        last.then_inc(xg_made, 1)

                    def three(out, x, xcols, i, q, first, last):
                        w = (wh[i % WS][:, q, :], wl[i % WS][:, q, :])
                        for m, (a, b) in enumerate(((0, 0), (0, 1), (1, 0))):
                            mm = pe.matmul(out, x[a][:, xcols, :], w[b], start=(first and m == 0),
                                           stop=(last and m == 2))
                        return mm

                    def split_ready(it, i):
                        lows = (wl_pool, len(POOL_LOW)) if i in POOL_LOW else (wl_dve, ND)
                        pe.wait_ge(lows[0], it * lows[1] + low_order(i))

                    gather(0)
                    pe.wait_ge(diag_done, NT)
                    pe.matmul(bank(ps, 4), s.ones[:, :], y[:, :], start=True, stop=True).then_inc(posB_made, 1)
                    turn_x(0)

                    def first_product(it, i):
                        split_ready(it, i)
                        for k in range(NC):
                            last = three(bank(ps, i % 2), xg, k, i, k, k == 0, k == NC - 1)
                        last.then_inc(h_made, 1)

                    pe.wait_ge(xgl_kept, 1)
                    first_product(0, 0)
                    with pe.Fori(0, tiles(pe)) as it:
                        def turn_h(i):
                            pe.wait_ge(h_kept, it * HC + i + 1)
                            for q in range(4):
                                last = pe.transpose(ps[:, (2 + i % 2) * 512 + q * P:(2 + i % 2) * 512 + q * P + P],
                                                    hs[i % 2][:, q * P:q * P + P], s.ident[:, :])
                            last.then_inc(ht_made, 1)

                        for i in range(1, HC):
                            if i == 1:
                                pe.wait_ge(sc_added, it * NT + 2)
                            else:
                                pe.wait_ge(h_kept, it * HC + i - 1)
                            first_product(it, i)
                            if i < 3:
                                pe.wait_ge(sc_added, it * NT + i + 2)
                            else:
                                pe.wait_ge(hf_kept, it * HC + i - 2)
                            turn_h(i - 1)
                        pe.wait_ge(hf_kept, it * HC + HC - 2)
                        for i in range(HC):
                            if i == 1:
                                turn_h(HC - 1)
                            if i == HC - 2:
                                gather(it + 1)
                            if i == HC - 1:
                                turn_x(it + 1)
                            split_ready(it, HC + i)
                            pe.wait_ge(hl_kept, it * HC + i + 1)
                            for q in range(4):
                                j = 4 * i + q
                                last = three(bank(ps, 4), hT, j, HC + i, q, j == 0, j == HID // P - 1)
                            last.then_inc(w2_used, 1)
                        pe.wait_ge(xgl_kept, it + 2)
                        first_product(it + 1, 0)
                        pe.wait_ge(pt_kept, it + 2)
                        pe.wait_ge(yl_done, it + 1)
                        for t in range(NT):
                            for i, part in enumerate((yh, yl)):
                                last = pe.matmul(bank(ps, sc_bank[t]), permT[:, t, :], part[:, :],
                                                 start=(i == 0), stop=(i == 1))
                            last.then_inc(sc_made, 1)

                @block.vector
                def _(dve):
                    def low(n, i):
                        dve.wait_ge(wh_done, n * WC + i + 1)
                        dve.tensor_tensor(wl[i % WS][:, :, :], raw[i][:, :, :], wh[i % WS][:, :, :].bitcast(F32),
                                          ALU.subtract).then_inc(wl_dve, 1)

                    def place(it):
                        for t in range(NT):
                            dve.tensor_scalar(perm[:, t, :], iota[:, :], pos[:, t:t + 1], None, ALU.is_equal)\
                               .then_inc(perm_done, 1)

                    def keep(it):
                        turned = bank(ps, 6).rearrange("p (k n) -> p k n", n=P)
                        dve.wait_ge(xg_made, it + 1)
                        dve.tensor_copy(xg[0][:, :, :], turned).then_inc(xgh_kept, 1)
                        dve.wait_ge(xgh_kept, it + 1)
                        dve.tensor_tensor(xg[1][:, :, :], turned, xg[0][:, :, :].bitcast(F32), ALU.subtract)\
                           .then_inc(xgl_kept, 1)

                    dve.memset(posB[:, :], 0.0).then_inc(sc_added, NT)
                    place(0)
                    for t in range(NT):
                        dve.tensor_scalar(y[:, t * P:t * P + P], s.ident[:, :], pos[:, t:t + 1], None, ALU.mult)\
                           .then_inc(diag_done, 1)
                    low(0, 0)
                    dve.wait_ge(sc_added, NT)
                    dve.wait_ge(posB_made, 1)
                    dve.tensor_copy(posB[:, :], bank(ps, 4)).then_inc(pt_kept, 1)
                    keep(0)
                    low(0, 2)
                    dve.wait_ge(pt_kept, 1)
                    with dve.Fori(0, tiles(dve)) as it:
                        def split_h(i):
                            part = slice(4 * i, 4 * i + 4)
                            dve.wait_ge(hf_kept, it * HC + i + 1)
                            dve.tensor_copy(hT[0][:, part, :], hf[i % 2][:, :, :]).then_inc(hh_kept, 1)
                            dve.wait_ge(hh_kept, it * HC + i + 1)
                            dve.tensor_tensor(hT[1][:, part, :], hf[i % 2][:, :, :], hT[0][:, part, :].bitcast(F32),
                                              ALU.subtract).then_inc(hl_kept, 1)

                        dve.tensor_scalar(permT[:, :, :].rearrange("p t n -> p (t n)"), posB[:, :], slot[:, 0:1], None,
                                          ALU.is_equal).then_inc(pt_kept, 1)
                        dve.tensor_scalar(slot[:, :], slot[:, :], float(P), None, ALU.add).then_inc(pos_down, 1)
                        dve.tensor_scalar(pos[:, :], pos[:, :], -float(P), None, ALU.add).then_inc(pos_down, 1)
                        dve.wait_ge(pos_down, it * 2 + 2)
                        place(it + 1)
                        for i in range(HC):
                            if i < HC - 1:
                                low(it, HC + i)
                            split_h(i)
                        low(it + 1, 0)
                        keep(it + 1)
                        dve.wait_ge(w2_used, it * HC + 2 * HC)
                        dve.wait_ge(b2_in, it * 16 + 16)
                        dve.tensor_tensor(y[:, :], bank(ps, 4), b2[:, :], ALU.add).then_inc(y_done, 1)
                        dve.wait_ge(y_done, it + 1)
                        dve.tensor_copy(yh[:, :], y[:, :]).then_inc(yh_done, 1)
                        dve.wait_ge(yh_done, it + 1)
                        dve.tensor_tensor(yl[:, :], y[:, :], yh[:, :].bitcast(F32), ALU.subtract).then_inc(yl_done, 1)
                        for t in range(NT):
                            dve.wait_ge(sc_made, it * NT + t + 1)
                            dve.tensor_tensor(x[:, t, :], x[:, t, :], bank(ps, sc_bank[t]), ALU.add)\
                               .then_inc(sc_added, 1)
                        low(it + 1, 2)

                @block.scalar
                def _(act):
                    def high(n, i):
                        act.wait_ge(w_in[i], n * 16 + 16)
                        if i < WS:
                            act.wait_ge(w2_used, n * HC + i + 1)
                        else:
                            act.wait_ge(h_made, n * HC + i - HC + 1)
                        act.copy(wh[i % WS][:, :, :], raw[i][:, :, :]).then_inc(wh_done, 1)

                    act.copy(hs[0][:, 0:1], x[:, 0, 0:1]).then_inc(w2_used, HC)
                    def keep_rows(it):
                        act.wait_ge(xr_made, it + 1)
                        act.copy(xr[:, :], bank(ps, 5)).then_inc(xr_kept, 1)

                    high(0, 0)
                    keep_rows(0)
                    for i in range(1, HC):
                        high(0, i)
                    with act.Fori(0, tiles(act)) as it:
                        def relus(i):
                            act.wait_ge(ht_made, it * HC + i + 1)
                            for q in range(4):
                                j = 4 * i + q
                                last = act.activation(hf[i % 2][:, q, :],
                                                      ps[:, (2 + i % 2) * 512 + q * P:(2 + i % 2) * 512 + q * P + P],
                                                      ACT.Relu, bias=b1[:, j:j + 1])
                            last.then_inc(hf_kept, 1)

                        act.wait_ge(b1_in, it * 16 + 16)
                        for i in range(HC):
                            act.wait_ge(h_made, it * HC + i + 1)
                            act.copy(hs[i % 2][:, :], bank(ps, i % 2)).then_inc(h_kept, 1)
                            high(it, HC + i)
                            if i:
                                if i - 1 >= 2:
                                    act.wait_ge(hl_kept, it * HC + i - 2)
                                relus(i - 1)
                        act.wait_ge(hl_kept, it * HC + HC - 2)
                        relus(HC - 1)
                        for i in range(HC):
                            high(it + 1, i)
                            if i == 1:
                                keep_rows(it + 1)


DEN_MIN, DEN_MAX = 1e-6, 1e20


def layer(nc, d, out):
    s = Stage()
    s.nc = nc
    with ExitStack() as ctx:
        def sb(name, shape, dt=F32):
            return ctx.enter_context(nc.sbuf_tensor(name, shape, dt))

        s.ps = ctx.enter_context(nc.psum_tensor("psum", [P, 4096], F32))
        s.ident = sb("ident", [P, P])
        s.cols = sb("cols", [P, 12])
        s.bq, s.bk, s.bv = s.cols[:, 0:4], s.cols[:, 4:8], s.cols[:, 8:12]
        s.eps = sb("eps", [P, 1])
        s.ones = sb("ones", [P, P])
        s.ln = LayerNorm(s, ctx)
        x1 = sb("x1", [P, NT, C])
        bad = sb("bad", [P, 1], I32)
        d["qT_d"] = nc.dram_tensor("qT_d", (C, T), F32).ap()
        attention = ctx.enter_context(ExitStack())
        s.wide_at = next_place(nc)
        wide = attention.enter_context(nc.sbuf_tensor("wide", [P, 16, 512], F32R))
        s.w = [nc.alloc_sbuf_tensor_at(f"w{n}_s", [P, NC, C], F32, offset=s.wide_at + 4 * i * NC * C)
               for i, n in enumerate("qkvo")]
        s.w_loaded = ctx.enter_context(nc.semaphore("s_loaded"))
        with nc.sbuf_tensor("o_acc", [P, G, T], F32) as oacc:
            cross_attention(s, d, wide, oacc, x1, bad)
            is_bad = nc.values_load(bad[0:1, 0:1], min_val=0, max_val=1)
            with nc.If(is_bad > 0):
                general_cross(s, d, oacc)
                cross_output(s, d, oacc, x1)
        self_attention(s, d, x1, x1)
        attention.close()
        feed_forward(s, d, x1, x1)
        done = ctx.enter_context(nc.semaphore("out_done"))
        with nc.Block() as block:

            @block.sync
            def _(sp):
                sp.dma_start(out.rearrange("(t p) c -> p t c", p=P), x1[:, :, :]).then_inc(done, 16)
                sp.wait_ge(done, 16)


def kernel(**inputs):
    import concourse.bacc as bacc
    from concourse.bass_utils import run_bass_kernel_spmd

    f = lambda n: np.asarray(inputs[n])
    col = lambda a: np.ascontiguousarray(a.reshape(-1, P).T)
    arrays = {
        "x": f("x").reshape(T, C),
        "ctxT": np.ascontiguousarray(f("ctx_768").reshape(N, CK).T),
        "Wq": f("L0_xattn_Wq"), "Wk": f("L0_xattn_Wk"), "Wv": f("L0_xattn_Wv"), "Wo": f("L0_xattn_Wo"),
        "cols": np.ascontiguousarray(np.concatenate([col(f("L0_xattn_b" + n)) for n in "qkv"], axis=1)),
        "bo": f("L0_xattn_bo"),
        "ident": np.eye(P, dtype=np.float32),
        "gate_w": f("L0_ffn_gate_w"), "gate_b": f("L0_ffn_gate_b"),
        "w1": f("L0_ffn_w1"), "w2": f("L0_ffn_w2"), "b2": f("L0_ffn_b2"),
        "b1c": np.ascontiguousarray(f("L0_ffn_b1").reshape(8, -1, P).transpose(0, 2, 1)),
        "tri": np.triu(np.ones((P, P), np.float32), 1),
        "iota": np.arange(P, dtype=np.float32),
        "slots": np.arange(P, dtype=np.float32).reshape(P, 1),
    }
    for n in "qkvo":
        arrays[f"W{n}T_s"] = np.ascontiguousarray(f(f"L0_attn_W{n}").T)
    dist = np.arange(P)[:, None] + (T - P) - np.arange(T)[None, :]
    arrays["strip"] = np.where(dist >= 0, -dist, NEG).astype(np.float32)
    nc = bacc.Bacc("TRN2", target_bir_lowering=False, num_devices=1)
    d = {n: nc.dram_tensor("in_" + n, a.shape, mybir.dt.from_np(a.dtype), kind="ExternalInput").ap()
         for n, a in arrays.items()}
    out = nc.dram_tensor("out", (T, C), F32, kind="ExternalOutput").ap()
    layer(nc, d, out)
    r = run_bass_kernel_spmd(nc, [{"in_" + n: a for n, a in arrays.items()}], core_ids=[0])
    return r.results[0]["out"].reshape(1, T, C)
```
